# Optimizing a Trainium2 kernel written in Bass

```python
import numpy as np
import jax
import jax.numpy as jnp

def _softmax(x, axis=-1):
    return jax.nn.softmax(x, axis=axis)

def _gelu(x):
    return jax.nn.gelu(x, approximate=True)

def _silu(x):
    return jax.nn.silu(x)

def _sigmoid(x):
    return jax.nn.sigmoid(x)

def _layernorm(x, axis=-1, eps=1e-05):
    m = jnp.mean(x, axis=axis, keepdims=True)
    v = jnp.var(x, axis=axis, keepdims=True)
    return (x - m) / jnp.sqrt(v + eps)

def _scatter_add(tgt, idx, src, axis=0):
    return tgt.at[idx].add(src)

def _segment_sum(src, seg, n):
    return jax.ops.segment_sum(src, seg, n)
kernel_name = 'mk_metaformer_d2_conv_nchw512_r4_37a0b8'

def setup_inputs(seed: int=0):
    np.random.seed(seed)
    _w = jnp.asarray

    def _rec_inputs():
        import jax
        import jax.numpy as jnp
        _gk = jax.random.key(seed)
        x = -0.000125 + 0.9999 * jax.random.normal(jax.random.fold_in(_gk, 1), (16, 128, 32, 32), jnp.float32)
        return x
    x = _rec_inputs()

    def _L0_conv_setup():
        import jax, jax.numpy as jnp
        import numpy as np
        from jax import lax
        EPS = 1e-05
        GROUPS = 16

        def _batchnorm(x, gamma, beta):
            m = jnp.mean(x, axis=(0, 2, 3), keepdims=True)
            v = jnp.mean((x - m) ** 2, axis=(0, 2, 3), keepdims=True)
            xhat = (x - m) * lax.rsqrt(v + EPS)
            return xhat * gamma[None, :, None, None] + beta[None, :, None, None]

        @jax.custom_vjp
        def binary_act(x):
            return jnp.sign(x)

        def _ba_fwd(x):
            return (jnp.sign(x), x)

        def _ba_bwd(x, g):
            return (jnp.clip(2.0 - 2.0 * jnp.abs(x), a_min=0.0) * g,)
        binary_act.defvjp(_ba_fwd, _ba_bwd)

        @jax.custom_vjp
        def binary_weight(w):
            return jnp.sign(w)

        def _bw_fwd(w):
            return (jnp.sign(w), w)

        def _bw_bwd(w, g):
            mask = jnp.logical_or(w >= 1.0, w <= -1.0)
            return (jnp.where(mask, 0.0, g),)
        binary_weight.defvjp(_bw_fwd, _bw_bwd)

        def _weight_scale(w):
            co = w.shape[0]
            wf = w.reshape(co, -1)
            bw = wf - jnp.mean(wf, axis=-1, keepdims=True)
            std = jnp.std(wf - jnp.mean(wf, axis=-1, keepdims=True), axis=-1, ddof=1, keepdims=True)
            bw = bw / std
            sw = jnp.mean(jnp.abs(bw), axis=-1).reshape(co, 1, 1, 1)
            return lax.stop_gradient(sw)
        key = jax.random.key(seed)
        ks = jax.random.split(key, 7)
        N, C, H, W = (16, 128, 32, 32)
        k = 3
        x = jax.random.normal(ks[0], (N, C, H, W), dtype=jnp.float32)
        conv_w = jax.random.normal(ks[1], (C, C // GROUPS, k, k), dtype=jnp.float32) * 0.1
        bn1_gamma = jnp.ones((C,), jnp.float32)
        bn1_beta = jnp.zeros((C,), jnp.float32)
        bn2_gamma = jnp.ones((C,), jnp.float32)
        bn2_beta = jnp.zeros((C,), jnp.float32)
        prelu_a = jnp.full((C,), 0.25, jnp.float32)
        return {'x': x, 'conv_w': conv_w, 'bn1_gamma': bn1_gamma, 'bn1_beta': bn1_beta, 'bn2_gamma': bn2_gamma, 'bn2_beta': bn2_beta, 'prelu_a': prelu_a}
    _L0_conv_all = _L0_conv_setup()
    _L0_conv_in = {k: v for k, v in _L0_conv_all.items() if k in ('conv_w', 'bn1_gamma', 'bn1_beta', 'bn2_gamma', 'bn2_beta', 'prelu_a')}
    del _L0_conv_all

    def _L0_ffn_setup():
        import jax, jax.numpy as jnp
        import numpy as np
        TOP_K = 2
        key = jax.random.key(seed)
        ks = jax.random.split(key, 6)
        B, T, C, E, H = (4, 1024, 128, 8, 512)
        x = jax.random.normal(ks[0], (B, T, C), dtype=jnp.float32)
        W_router = jax.random.normal(ks[1], (C, E), dtype=jnp.float32) * 0.02
        W1 = jax.random.normal(ks[2], (E, C, H), dtype=jnp.float32) * 0.02
        b1 = jnp.zeros((E, H), dtype=jnp.float32)
        W2 = jax.random.normal(ks[3], (E, H, C), dtype=jnp.float32) * 0.02
        b2 = jnp.zeros((E, C), dtype=jnp.float32)
        return {'x': x, 'W_router': W_router, 'W1': W1, 'b1': b1, 'W2': W2, 'b2': b2}
    _L0_ffn_all = _L0_ffn_setup()
    _L0_ffn_in = {k: v for k, v in _L0_ffn_all.items() if k in ('W_router', 'W1', 'b1', 'W2', 'b2')}
    del _L0_ffn_all

    def _L1_conv_setup():
        import jax, jax.numpy as jnp
        import numpy as np
        import math
        PERMS = ((0, 1, 2, 3, 4, 5, 6, 7), (3, 0, 1, 2, 5, 6, 7, 4), (2, 3, 0, 1, 6, 7, 4, 5), (1, 2, 3, 0, 7, 4, 5, 6), (4, 5, 6, 7, 0, 1, 2, 3), (5, 6, 7, 4, 3, 0, 1, 2), (6, 7, 4, 5, 2, 3, 0, 1), (7, 4, 5, 6, 1, 2, 3, 0))

        def d4_1x1(x, w):
            b, C, h, ww = x.shape
            cout, cin, _ = w.shape
            W = jnp.stack([w[..., jnp.array(p)] for p in PERMS], axis=1)
            xr = x.reshape(b, cin, 8, h, ww)
            y = jnp.einsum('ogif,bifhw->boghw', W, xr)
            return y.reshape(b, cout * 8, h, ww)

        def group_norm(x, gamma, beta, num_groups, eps=1e-05):
            b, C, h, w = x.shape
            xg = x.reshape(b, num_groups, C // num_groups, h, w)
            mean = xg.mean(axis=(2, 3, 4), keepdims=True)
            var = xg.var(axis=(2, 3, 4), keepdims=True)
            xn = ((xg - mean) / jnp.sqrt(var + eps)).reshape(b, C, h, w)
            return xn * gamma[None, :, None, None] + beta[None, :, None, None]

        def unfold_patches(x, k):
            b, C, h, w = x.shape
            p = (k - 1) // 2
            xp = jnp.pad(x, ((0, 0), (0, 0), (p, p), (p, p)))
            pats = jnp.stack([xp[:, :, i:i + h, j:j + w] for i in range(k) for j in range(k)], axis=2)
            return pats
        key = jax.random.key(seed)
        ks = jax.random.split(key, 4)
        b, H, W = (8, 56, 56)
        cin, cout, rr, k, gc = (16, 16, 2, 3, 16)
        cmid = cin // rr
        G = cout // gc
        x = jax.random.normal(ks[0], (b, cin * 8, H, W), jnp.float32)
        w_v = jax.random.normal(ks[1], (cout, cin, 8), jnp.float32) / math.sqrt(8 * cin / 2)
        w1 = jax.random.normal(ks[2], (cmid, cin, 8), jnp.float32) / math.sqrt(8 * cin / 2)
        gn_gamma = jnp.ones((cmid * 8,), jnp.float32)
        gn_beta = jnp.zeros((cmid * 8,), jnp.float32)
        w2 = jax.random.normal(ks[3], (k * k * G, cmid), jnp.float32) / math.sqrt(cmid)
        b2 = jnp.zeros((k * k * G,), jnp.float32)
        return {'x': x, 'w_v': w_v, 'w1': w1, 'gn_gamma': gn_gamma, 'gn_beta': gn_beta, 'w2': w2, 'b2': b2}
    _L1_conv_all = _L1_conv_setup()
    _L1_conv_in = {k: v for k, v in _L1_conv_all.items() if k in ('w_v', 'w1', 'gn_gamma', 'gn_beta', 'w2', 'b2')}
    del _L1_conv_all

    def _L1_ffn_setup():
        import jax, jax.numpy as jnp
        import numpy as np
        DIM = 128
        MOE_DIM = 64
        E = 16
        G = 8
        TOPK_G = 4
        K = 8
        SCALE = 2.5
        CAP = 256

        def _gate(x2, gate_w, gate_b):
            T = x2.shape[0]
            scores = jax.nn.sigmoid(x2 @ gate_w.T)
            s = (scores + gate_b).reshape(T, G, E // G)
            group_scores = jax.lax.top_k(s, 2)[0].sum(-1)
            top_groups = jax.lax.top_k(group_scores, TOPK_G)[1]
            gmask = jnp.zeros((T, G), bool).at[jnp.arange(T)[:, None], top_groups].set(True)
            s = jnp.where(gmask[..., None], s, -jnp.inf).reshape(T, E)
            idx = jax.lax.top_k(s, K)[1]
            w = jnp.take_along_axis(scores, idx, axis=1)
            w = w / w.sum(-1, keepdims=True) * SCALE
            return (w, idx)

        def _moe_forward(x, gate_w, gate_b, w1, w3, w2):
            shape = x.shape
            x2 = x.reshape(-1, DIM)
            T = x2.shape[0]
            w, idx = _gate(x2, gate_w, gate_b)
            flat_e = idx.reshape(-1)
            oh = (flat_e[:, None] == jnp.arange(E)[None, :]).astype(jnp.int32)
            pos = (jnp.cumsum(oh, axis=0) * oh).sum(-1) - 1
            x_rep = jnp.repeat(x2, K, axis=0)
            xb = jnp.zeros((E, CAP, DIM), x2.dtype).at[flat_e, pos].set(x_rep, mode='drop')
            h = jax.nn.silu(jnp.einsum('ecd,edm->ecm', xb, w1)) * jnp.einsum('ecd,edm->ecm', xb, w3)
            yb = jnp.einsum('ecm,emd->ecd', h, w2)
            y = yb.at[flat_e, pos].get(mode='fill', fill_value=0.0) * w.reshape(-1)[:, None]
            return y.reshape(T, K, DIM).sum(1).reshape(shape)
        key = jax.random.key(seed)
        ks = jax.random.split(key, 6)
        x = jax.random.normal(ks[0], (4, 128, DIM), jnp.float32)
        gate_w = jax.random.normal(ks[1], (E, DIM), jnp.float32) / np.sqrt(DIM).astype(np.float32)
        gate_b = jax.random.normal(ks[2], (E,), jnp.float32) * 0.01
        w1 = jax.random.normal(ks[3], (E, DIM, MOE_DIM), jnp.float32) / np.sqrt(DIM).astype(np.float32)
        w3 = jax.random.normal(ks[4], (E, DIM, MOE_DIM), jnp.float32) / np.sqrt(DIM).astype(np.float32)
        w2 = jax.random.normal(ks[5], (E, MOE_DIM, DIM), jnp.float32) / np.sqrt(MOE_DIM).astype(np.float32)
        return {'x': x, 'gate_w': gate_w, 'gate_b': gate_b, 'w1': w1, 'w3': w3, 'w2': w2}
    _L1_ffn_all = _L1_ffn_setup()
    _L1_ffn_in = {k: v for k, v in _L1_ffn_all.items() if k in ('gate_w', 'gate_b', 'w1', 'w3', 'w2')}
    del _L1_ffn_all
    return {'x': x, 'L0_conv_conv_w': _L0_conv_in['conv_w'], 'L0_conv_bn1_gamma': _L0_conv_in['bn1_gamma'], 'L0_conv_bn1_beta': _L0_conv_in['bn1_beta'], 'L0_conv_bn2_gamma': _L0_conv_in['bn2_gamma'], 'L0_conv_bn2_beta': _L0_conv_in['bn2_beta'], 'L0_conv_prelu_a': _L0_conv_in['prelu_a'], 'L0_ffn_W_router': _L0_ffn_in['W_router'], 'L0_ffn_W1': _L0_ffn_in['W1'], 'L0_ffn_b1': _L0_ffn_in['b1'], 'L0_ffn_W2': _L0_ffn_in['W2'], 'L0_ffn_b2': _L0_ffn_in['b2'], 'L1_conv_w_v': _L1_conv_in['w_v'], 'L1_conv_w1': _L1_conv_in['w1'], 'L1_conv_gn_gamma': _L1_conv_in['gn_gamma'], 'L1_conv_gn_beta': _L1_conv_in['gn_beta'], 'L1_conv_w2': _L1_conv_in['w2'], 'L1_conv_b2': _L1_conv_in['b2'], 'L1_ffn_gate_w': _L1_ffn_in['gate_w'], 'L1_ffn_gate_b': _L1_ffn_in['gate_b'], 'L1_ffn_w1': _L1_ffn_in['w1'], 'L1_ffn_w3': _L1_ffn_in['w3'], 'L1_ffn_w2': _L1_ffn_in['w2']}

def reference(x, L0_conv_conv_w, L0_conv_bn1_gamma, L0_conv_bn1_beta, L0_conv_bn2_gamma, L0_conv_bn2_beta, L0_conv_prelu_a, L0_ffn_W_router, L0_ffn_W1, L0_ffn_b1, L0_ffn_W2, L0_ffn_b2, L1_conv_w_v, L1_conv_w1, L1_conv_gn_gamma, L1_conv_gn_beta, L1_conv_w2, L1_conv_b2, L1_ffn_gate_w, L1_ffn_gate_b, L1_ffn_w1, L1_ffn_w3, L1_ffn_w2):
    import jax
    import jax.numpy as jnp

    def _L0_conv_ref(x, conv_w, bn1_gamma, bn1_beta, bn2_gamma, bn2_beta, prelu_a):
        import jax, jax.numpy as jnp
        import numpy as np
        from jax import lax
        EPS = 1e-05
        GROUPS = 16

        def _batchnorm(x, gamma, beta):
            m = jnp.mean(x, axis=(0, 2, 3), keepdims=True)
            v = jnp.mean((x - m) ** 2, axis=(0, 2, 3), keepdims=True)
            xhat = (x - m) * lax.rsqrt(v + EPS)
            return xhat * gamma[None, :, None, None] + beta[None, :, None, None]

        @jax.custom_vjp
        def binary_act(x):
            return jnp.sign(x)

        def _ba_fwd(x):
            return (jnp.sign(x), x)

        def _ba_bwd(x, g):
            return (jnp.clip(2.0 - 2.0 * jnp.abs(x), a_min=0.0) * g,)
        binary_act.defvjp(_ba_fwd, _ba_bwd)

        @jax.custom_vjp
        def binary_weight(w):
            return jnp.sign(w)

        def _bw_fwd(w):
            return (jnp.sign(w), w)

        def _bw_bwd(w, g):
            mask = jnp.logical_or(w >= 1.0, w <= -1.0)
            return (jnp.where(mask, 0.0, g),)
        binary_weight.defvjp(_bw_fwd, _bw_bwd)

        def _weight_scale(w):
            co = w.shape[0]
            wf = w.reshape(co, -1)
            bw = wf - jnp.mean(wf, axis=-1, keepdims=True)
            std = jnp.std(wf - jnp.mean(wf, axis=-1, keepdims=True), axis=-1, ddof=1, keepdims=True)
            bw = bw / std
            sw = jnp.mean(jnp.abs(bw), axis=-1).reshape(co, 1, 1, 1)
            return lax.stop_gradient(sw)
        res = x
        h = _batchnorm(x, bn1_gamma, bn1_beta)
        h = binary_act(h)
        sw = _weight_scale(conv_w)
        bw = binary_weight(conv_w) * sw
        h = lax.conv_general_dilated(h, bw, window_strides=(1, 1), padding=((1, 1), (1, 1)), feature_group_count=GROUPS, dimension_numbers=('NCHW', 'OIHW', 'NCHW'))
        h = _batchnorm(h, bn2_gamma, bn2_beta)
        h = h + res
        a = prelu_a[None, :, None, None]
        return jnp.where(h > 0, h, a * h)

    def _L0_ffn_ref(x, W_router, W1, b1, W2, b2):
        import jax, jax.numpy as jnp
        import numpy as np
        TOP_K = 2
        B, T, C = x.shape
        E = W_router.shape[1]
        x_flat = x.reshape(B * T, C)
        logits = x_flat @ W_router
        probs = jax.nn.softmax(logits, axis=-1)
        topk_p, topk_i = jax.lax.top_k(probs, TOP_K)
        topk_p = topk_p / topk_p.sum(axis=-1, keepdims=True)
        combine = (jax.nn.one_hot(topk_i, E, dtype=x_flat.dtype) * topk_p[..., None]).sum(axis=1)
        out = jnp.zeros_like(x_flat)
        for e in range(E):
            h = jax.nn.relu(x_flat @ W1[e] + b1[e])
            y = h @ W2[e] + b2[e]
            out = out + combine[:, e:e + 1] * y
        return out.reshape(B, T, C)

    def _L1_conv_ref(x, w_v, w1, gn_gamma, gn_beta, w2, b2):
        import jax, jax.numpy as jnp
        import numpy as np
        import math
        PERMS = ((0, 1, 2, 3, 4, 5, 6, 7), (3, 0, 1, 2, 5, 6, 7, 4), (2, 3, 0, 1, 6, 7, 4, 5), (1, 2, 3, 0, 7, 4, 5, 6), (4, 5, 6, 7, 0, 1, 2, 3), (5, 6, 7, 4, 3, 0, 1, 2), (6, 7, 4, 5, 2, 3, 0, 1), (7, 4, 5, 6, 1, 2, 3, 0))

        def d4_1x1(x, w):
            b, C, h, ww = x.shape
            cout, cin, _ = w.shape
            W = jnp.stack([w[..., jnp.array(p)] for p in PERMS], axis=1)
            xr = x.reshape(b, cin, 8, h, ww)
            y = jnp.einsum('ogif,bifhw->boghw', W, xr)
            return y.reshape(b, cout * 8, h, ww)

        def group_norm(x, gamma, beta, num_groups, eps=1e-05):
            b, C, h, w = x.shape
            xg = x.reshape(b, num_groups, C // num_groups, h, w)
            mean = xg.mean(axis=(2, 3, 4), keepdims=True)
            var = xg.var(axis=(2, 3, 4), keepdims=True)
            xn = ((xg - mean) / jnp.sqrt(var + eps)).reshape(b, C, h, w)
            return xn * gamma[None, :, None, None] + beta[None, :, None, None]

        def unfold_patches(x, k):
            b, C, h, w = x.shape
            p = (k - 1) // 2
            xp = jnp.pad(x, ((0, 0), (0, 0), (p, p), (p, p)))
            pats = jnp.stack([xp[:, :, i:i + h, j:j + w] for i in range(k) for j in range(k)], axis=2)
            return pats
        k, gc = (3, 16)
        b, _, h, w = x.shape
        cmid = w1.shape[0]
        G = w2.shape[0] // (k * k)
        t = jax.nn.relu(group_norm(d4_1x1(x, w1), gn_gamma, gn_beta, cmid))
        tr = t.reshape(b, cmid, 8, h, w)
        wgt = jnp.einsum('oi,bighw->boghw', w2, tr) + b2[None, :, None, None, None]
        wv = wgt.reshape(b, G, k, k, 8, h, w)
        s = [wv[:, :, :, :, g] for g in range(8)]
        sw = [jnp.swapaxes(s[g], 2, 3) for g in range(4, 8)]
        trans = [s[0], jnp.rot90(s[1], 1, (2, 3)), jnp.rot90(s[2], 2, (2, 3)), jnp.rot90(s[3], 3, (2, 3)), jnp.rot90(sw[0], 3, (2, 3)), jnp.rot90(sw[1], 2, (2, 3)), jnp.rot90(sw[2], 1, (2, 3)), sw[3]]
        wv = jnp.stack(trans, axis=4)
        wv = wv.reshape(b, G, k * k, 8, h, w)[:, :, None]
        wv = jnp.swapaxes(wv, 3, 4)
        xv = d4_1x1(x, w_v)
        pats = unfold_patches(xv, k).reshape(b, G, gc, 8, k * k, h, w)
        out = (wv * pats).sum(axis=4)
        return out.reshape(b, G * gc * 8, h, w)

    def _L1_ffn_ref(x, gate_w, gate_b, w1, w3, w2):
        import jax, jax.numpy as jnp
        import numpy as np
        DIM = 128
        MOE_DIM = 64
        E = 16
        G = 8
        TOPK_G = 4
        K = 8
        SCALE = 2.5
        CAP = 256

        def _gate(x2, gate_w, gate_b):
            T = x2.shape[0]
            scores = jax.nn.sigmoid(x2 @ gate_w.T)
            s = (scores + gate_b).reshape(T, G, E // G)
            group_scores = jax.lax.top_k(s, 2)[0].sum(-1)
            top_groups = jax.lax.top_k(group_scores, TOPK_G)[1]
            gmask = jnp.zeros((T, G), bool).at[jnp.arange(T)[:, None], top_groups].set(True)
            s = jnp.where(gmask[..., None], s, -jnp.inf).reshape(T, E)
            idx = jax.lax.top_k(s, K)[1]
            w = jnp.take_along_axis(scores, idx, axis=1)
            w = w / w.sum(-1, keepdims=True) * SCALE
            return (w, idx)

        def _moe_forward(x, gate_w, gate_b, w1, w3, w2):
            shape = x.shape
            x2 = x.reshape(-1, DIM)
            T = x2.shape[0]
            w, idx = _gate(x2, gate_w, gate_b)
            flat_e = idx.reshape(-1)
            oh = (flat_e[:, None] == jnp.arange(E)[None, :]).astype(jnp.int32)
            pos = (jnp.cumsum(oh, axis=0) * oh).sum(-1) - 1
            x_rep = jnp.repeat(x2, K, axis=0)
            xb = jnp.zeros((E, CAP, DIM), x2.dtype).at[flat_e, pos].set(x_rep, mode='drop')
            h = jax.nn.silu(jnp.einsum('ecd,edm->ecm', xb, w1)) * jnp.einsum('ecd,edm->ecm', xb, w3)
            yb = jnp.einsum('ecm,emd->ecd', h, w2)
            y = yb.at[flat_e, pos].get(mode='fill', fill_value=0.0) * w.reshape(-1)[:, None]
            return y.reshape(T, K, DIM).sum(1).reshape(shape)
        return _moe_forward(x, gate_w, gate_b, w1, w3, w2)

    def _gn(v, G=32, eps=1e-05):
        B_, C_, H_, W_ = v.shape
        g = v.reshape(B_, G, C_ // G, H_, W_)
        m = jnp.mean(g, axis=(2, 3, 4), keepdims=True)
        s = jnp.var(g, axis=(2, 3, 4), keepdims=True)
        return ((g - m) / jnp.sqrt(s + eps)).reshape(v.shape)

    def _ln_c(v, eps=1e-06):
        m = jnp.mean(v, axis=1, keepdims=True)
        s = jnp.var(v, axis=1, keepdims=True)
        return (v - m) / jnp.sqrt(s + eps)

    def _ln_t(v, eps=1e-05):
        m = jnp.mean(v, axis=-1, keepdims=True)
        s = jnp.var(v, axis=-1, keepdims=True)
        return (v - m) / jnp.sqrt(s + eps)

    def _to_tokens(v):
        B_, C_, H_, W_ = v.shape
        return v.reshape(B_, C_, H_ * W_).transpose(0, 2, 1)

    def _from_tokens(t, like):
        B_, C_, H_, W_ = like.shape
        return t.transpose(0, 2, 1).reshape(B_, C_, H_, W_)
    x = x + _L0_conv_ref(_ln_c(x), L0_conv_conv_w, L0_conv_bn1_gamma, L0_conv_bn1_beta, L0_conv_bn2_gamma, L0_conv_bn2_beta, L0_conv_prelu_a)
    t = _to_tokens(x)
    t = t + _L0_ffn_ref(_ln_t(t), L0_ffn_W_router, L0_ffn_W1, L0_ffn_b1, L0_ffn_W2, L0_ffn_b2)
    x = _from_tokens(t, x)
    x = x + _L1_conv_ref(_ln_c(x), L1_conv_w_v, L1_conv_w1, L1_conv_gn_gamma, L1_conv_gn_beta, L1_conv_w2, L1_conv_b2)
    t = _to_tokens(x)
    t = t + _L1_ffn_ref(_ln_t(t), L1_ffn_gate_w, L1_ffn_gate_b, L1_ffn_w1, L1_ffn_w3, L1_ffn_w2)
    x = _from_tokens(t, x)
    return x

_drawn_inputs = setup_inputs


def setup_inputs(seed=0):
    import zlib

    import numpy as np

    out = dict(_drawn_inputs(seed))
    spreads = {'L0_conv_bn1_gamma': (1.0, 0.2),
     'L0_conv_bn1_beta': (0.0, 0.1),
     'L0_conv_bn2_gamma': (1.0, 0.2),
     'L0_conv_bn2_beta': (0.0, 0.1),
     'L0_conv_prelu_a': (0.25, 0.2),
     'L0_ffn_b1': (0.0, 0.501),
     'L0_ffn_b2': (0.0, 0.1),
     'L1_conv_gn_gamma': (1.0, 0.2),
     'L1_conv_gn_beta': (0.0, 0.1),
     'L1_conv_b2': (0.0, 0.1)}
    factors = {'L1_ffn_gate_w': 9.378, 'L1_ffn_gate_b': 47.154}
    for name, (base, spread) in spreads.items():
        noise = np.random.default_rng([zlib.crc32(name.encode()), seed]).standard_normal(out[name].shape)
        drawn = base * np.exp(spread * noise) if base else spread * noise
        out[name] = jnp.asarray(drawn.astype(out[name].dtype))
    for name, factor in factors.items():
        out[name] = (out[name] * factor).astype(out[name].dtype)
    return out
```

```python
from contextlib import ExitStack, contextmanager

import numpy as np

import concourse.bass as bass
from concourse import mybir
from concourse.alu_op_type import AluOpType as ALU

ACT = mybir.ActivationFunctionType
AX = mybir.AxisListType
F32, F16, BF16 = mybir.dt.float32, mybir.dt.float16, mybir.dt.bfloat16
I32, U32 = mybir.dt.int32, mybir.dt.uint32

IMAGES, C, SIDE = 16, 128, 32
PIX = SIDE * SIDE
TOKENS = IMAGES * PIX
HALF = 512
P = 128
TILES = TOKENS // P
TPI = PIX // P
PAD = SIDE + 2
GROUP_IN = 8
TAPS = 9
E0, H0 = 8, 512
KM = H0 // P
PAIRS = E0 * (E0 - 1) // 2
SLOT = 256
SUB = SLOT // P
MAX_TILES = TOKENS // SLOT + PAIRS
ROW = C + 2
CMID, G8 = 8, 8
E1, M1, CAP = 16, 64, 256
EP1 = E1 // 2
TOP_G = 4
SCALE1 = 2.5
G1 = 8
BLOCK = 512
BT, BLOCKS = BLOCK // P, TOKENS // BLOCK
FIRST_BLOCKS = 4
FIRST_IMAGES = FIRST_BLOCKS * BLOCK // PIX
STEPS1 = 19
WSCALE = 32.0
POOL_TAPS = 3
OWN_ADDS = TAPS - POOL_TAPS - 1
STEPS_PER_IMAGE = 9
WCOLS = 4 * H0 + C + 2 * KM
EPS_C, EPS = 1e-6, 1e-5
CLEARED = (MAX_TILES + 1) * SLOT
CLEARS = 6
PERMS = ((0, 1, 2, 3, 4, 5, 6, 7), (3, 0, 1, 2, 5, 6, 7, 4), (2, 3, 0, 1, 6, 7, 4, 5), (1, 2, 3, 0, 7, 4, 5, 6),
         (4, 5, 6, 7, 0, 1, 2, 3), (5, 6, 7, 4, 3, 0, 1, 2), (6, 7, 4, 5, 2, 3, 0, 1), (7, 4, 5, 6, 1, 2, 3, 0))
PAIR_LIST = [(a, b) for a in range(E0) for b in range(a + 1, E0)]


@contextmanager
def by_two(engine, start, end):
    with engine.Fori(start // 2, end // 2) as i:
        yield i * 2


def wait_apart(engine, sem, value, passed):
    engine.wait_ge(sem, value)
    engine.sem_inc(passed, 1)


def image(buf, n):
    return buf[:, bass.ds(n * PIX, PIX)]


def setup_constants(nc, env, a):
    with ExitStack() as ctx:
        got = ctx.enter_context(nc.semaphore("const_loaded"))
        cast = ctx.enter_context(nc.semaphore("const_cast"))
        block = ctx.enter_context(nc.Block())
        loads = [(env.cen[:, :], a["k_center"]), (env.avg[:, :], a["k_average"]), (env.idf[:, :], a["k_identity"]),
                 (env.small[:, :], a["k_small"]), (env.par[:, 0:5], a["chan"]),
                 (env.ltri32[:, :], a["k_lower"])]

        @block.sync
        def _(sp):
            for dst, src in loads:
                sp.dma_start(dst, src).then_inc(got, 16)

        @block.vector
        def _(dve):
            dve.wait_ge(got, 16 * len(loads))
            dve.tensor_copy(env.ltri[:, :], env.ltri32[:, :]).then_inc(cast, 1)
            dve.memset(env.ones16[:, :], 1.0).then_inc(cast, 1)
            dve.tensor_copy(env.idb[:, :], env.idf[:, :]).then_inc(cast, 1)
            dve.memset(env.eps[:, 0:1], EPS_C).then_inc(cast, 1)
            dve.memset(env.eps[:, 1:2], EPS).then_inc(cast, 1)
            dve.memset(env.eps[:, 2:3], 0.0).then_inc(cast, 1)
            dve.memset(env.ones32[:, :], 1.0).then_inc(cast, 1)
            dve.wait_ge(cast, 7)


def chain(engine, sem):
    count = [0]

    def link(instruction):
        count[0] += 1
        instruction.then_inc(sem, 1)
        engine.wait_ge(sem, count[0])
    return link


def phase_norm0(nc, env, a, zero_rows):
    X, Y = env.X, env.Y
    with ExitStack() as ctx:
        sem = lambda n: ctx.enter_context(nc.semaphore(n))
        loaded = [sem(f"n0_loaded{q}") for q in range(2)]
        cent_ready, sq_ready, var_ready = sem("n0_cent_ready"), sem("n0_sq_ready"), sem("n0_var_ready")
        ln_ready, rstd_ready, norm_free = sem("n0_ln_ready"), sem("n0_rstd_ready"), sem("n0_norm_free")
        sq_free = sem("n0_sq_free")
        zeroed, stats = sem("n0_zeroed"), sem("n0_stats")
        sq = [ctx.enter_context(nc.sbuf_tensor(f"n0_sq{q}", [P, PIX], F32)) for q in range(2)]
        rs = [ctx.enter_context(nc.sbuf_tensor(f"n0_rs{q}", [P, PIX], F32)) for q in range(2)]
        cent, var = env.psum[0:2], env.psum[2:4]
        block = ctx.enter_context(nc.Block())

        @block.sync
        def _(sp):
            for q in range(2):
                sp.dma_start(image(X, q), a["x"][:, q, :]).then_inc(loaded[q], 16)
            with by_two(sp, 2, IMAGES) as n:
                for q in range(2):
                    sp.wait_ge(loaded[q], n * 8)
                    sp.dma_start(image(X, n + q), a["x"][:, bass.ds(n + q, 1), :]).then_inc(loaded[q], 16)

        @block.gpsimd
        def _(pool):
            pool.memset(env.zero[:, :], 0.0).then_inc(zeroed, 1)
            pool.wait_ge(zeroed, 1)
            rows = CLEARED // P // CLEARS
            for q in range(2):
                pool.wait_ge(loaded[q], IMAGES * 8)
            for i in range(CLEARS):
                pool.dma_start(zero_rows[i * P * rows:(i + 1) * P * rows, :].rearrange("(p r) c -> p r c", p=P),
                               env.zero[:, :].unsqueeze(1).broadcast_to([P, rows, ROW])).then_inc(env.cleared, 16)

        @block.tensor
        def _(pe):
            def center(n, q):
                pe.wait_ge(loaded[q], (n - q) * 8 + 16)
                pe.wait_ge(norm_free, n + 1)
                for h in range(2):
                    mm = pe.matmul(cent[q][:, h * HALF:(h + 1) * HALF], env.cen[:, :],
                                   X[:, bass.ds(n * PIX + h * HALF, HALF)], start=True, stop=True)
                mm.then_inc(cent_ready, 1)

            def variance(n, q):
                pe.wait_ge(sq_ready, n + 1)
                for h in range(2):
                    mm = pe.matmul(var[q][:, h * HALF:(h + 1) * HALF], env.avg[:, :],
                                   sq[q][:, h * HALF:(h + 1) * HALF], start=True, stop=True)
                mm.then_inc(var_ready, 1)

            center(0, 0)
            center(1, 1)
            variance(0, 0)
            with by_two(pe, 0, IMAGES - 2) as n:
                for q in range(2):
                    variance(n + q + 1, 1 - q)
                    center(n + q + 2, q)
            variance(IMAGES - 1, 1)

        @block.scalar
        def _(act):
            def square(n, q):
                act.wait_ge(cent_ready, n + 1)
                act.activation(sq[q][:, :], cent[q][:, :], ACT.Square).then_inc(sq_ready, 1)

            def rstd(n, q):
                act.wait_ge(var_ready, n + 1)
                act.wait_ge(norm_free, n + 1)
                act.activation(rs[q][:, :], var[q][:, :], ACT.Ln, bias=env.eps[:, 0:1], scale=1.0).then_inc(ln_ready, 1)
                act.wait_ge(ln_ready, n + 1)
                act.activation(rs[q][:, :], rs[q][:, :], ACT.Exp, scale=-0.5).then_inc(rstd_ready, 1)

            act.preload_act_table_set("natural_log_exp_and_others")
            square(0, 0)
            square(1, 1)
            rstd(0, 0)
            with by_two(act, 0, IMAGES - 2) as n:
                for q in range(2):
                    rstd(n + q + 1, 1 - q)
                    square(n + q + 2, q)
            rstd(IMAGES - 1, 1)

        @block.vector
        def _(dve):
            dve.sem_inc(norm_free, 2)
            with by_two(dve, 0, IMAGES) as n:
                for q in range(2):
                    dve.wait_ge(rstd_ready, n + q + 1)
                    dve.tensor_tensor(image(Y, n + q), cent[q][:, :], rs[q][:, :], ALU.mult).then_inc(norm_free, 1)
                    dve.wait_ge(norm_free, n + q + 3)
                    for h in range(2):
                        dve.bn_stats(env.bnst[:, bass.ds((n + q) * 12 + h * 6, 6)],
                                     Y[:, bass.ds((n + q) * PIX + h * HALF, HALF)]).then_inc(stats, 1)
            dve.wait_ge(stats, 2 * IMAGES)


def phase_conv(nc, env, a):
    Y, CONV, par = env.Y, env.CONV, env.par
    with ExitStack() as ctx:
        sem = lambda n: ctx.enter_context(nc.semaphore(n))
        sb = lambda n, s, d=F32: ctx.enter_context(nc.sbuf_tensor(n, s, d))
        w_loaded, w_sign, w_spread, w_turned, w_ready = (sem(f"cv_w_{x}") for x in ("loaded", "sign", "spread", "turned", "ready"))
        var1, rs1, coef1, border = sem("cv_var1"), sem("cv_rs1"), sem("cv_coef1"), sem("cv_border")
        sign_ready, conv_ready, evac_free, stats, steps, asteps = (sem(f"cv_{x}") for x in
            ("sign_ready", "conv_ready", "evac_free", "stats", "steps", "asteps"))
        var2, rs2 = sem("cv_var2"), sem("cv_rs2")
        cw, sg, dev, mag = sb("cv_w", [P, GROUP_IN * TAPS]), sb("cv_sg", [P, GROUP_IN * TAPS]), sb("cv_dev", [P, GROUP_IN * TAPS]), sb("cv_mag", [P, GROUP_IN * TAPS])
        spread = sb("cv_spread", [P, TAPS, P], BF16)
        taps = sb("cv_taps", [P, TAPS, P], BF16)
        t = sb("cv_t", [P, 24])
        padded = [sb(f"cv_padded{q}", [P, PAD, PAD], BF16) for q in range(2)]
        col = lambda k: t[:, k:k + 1]
        mean1, vari1, lnv1, rstd1 = col(0), col(1), col(2), col(3)
        wsum, wmean, wss, wabs, wln, wrs, sw = (col(k) for k in range(4, 11))
        mean2, vari2, sv, lnv2, rstd2, tmp = (col(k) for k in range(12, 18))
        A1, B1 = par[:, 5:6], par[:, 6:7]
        A2, B2 = par[:, 7:8], par[:, 8:9]
        g1, b1, g2, b2 = (par[:, k:k + 1] for k in range(4))
        block = ctx.enter_context(nc.Block())

        @block.sync
        def _(sp):
            sp.dma_start(cw[:, :], a["conv_w"]).then_inc(w_loaded, 16)

        @block.vector
        def _(dve):
            link = chain(dve, steps)
            for q in range(2):
                dve.memset(padded[q][:, :, :], 0.0).then_inc(border, 1)
            dve.bn_aggr(t[:, 0:2], env.bnst[:, :].rearrange("p (n s) -> p n s", s=6)).then_inc(var1, 1)
            dve.wait_ge(w_loaded, 16)
            n = GROUP_IN * TAPS
            link(dve.reduce_sum(wsum, cw[:, :], AX.X))
            link(dve.tensor_scalar(wmean, wsum, 1.0 / n, None, ALU.mult))
            link(dve.tensor_scalar(dev[:, :], cw[:, :], wmean, None, ALU.subtract))
            link(dve.tensor_tensor(mag[:, :], dev[:, :], dev[:, :], ALU.mult))
            link(dve.reduce_sum(wss, mag[:, :], AX.X))
            link(dve.scalar_tensor_tensor(mag[:, :], dev[:, :], -1.0, dev[:, :], ALU.mult, ALU.max))
            link(dve.reduce_sum(wabs, mag[:, :], AX.X))
            dve.wait_ge(w_sign, 1)
            for k in range(TAPS):
                dve.tensor_tensor(
                    spread[:, k, :].rearrange("p (g i) -> p g i", i=GROUP_IN),
                    sg[:, :].rearrange("p (i k) -> p k i", k=TAPS)[:, k:k + 1, :].broadcast_to([P, C // GROUP_IN, GROUP_IN]),
                    env.mask_group[:, :].unsqueeze(2).broadcast_to([P, C // GROUP_IN, GROUP_IN]),
                    ALU.mult).then_inc(w_spread, 1)
            dve.wait_ge(rs1, 1)
            link(dve.tensor_tensor(A1, g1, rstd1, ALU.mult))
            link(dve.tensor_tensor(tmp, mean1, A1, ALU.mult))
            dve.tensor_tensor(B1, b1, tmp, ALU.subtract).then_inc(coef1, 1)
            dve.wait_ge(rs1, 2)
            link(dve.tensor_scalar(wrs, wrs, wabs, 1.0 / n, ALU.mult, ALU.mult))
            for half in range(2):
                dve.wait_ge(w_turned, half + 1)
                k0, k1 = (0, 8) if half == 0 else (8, TAPS)
                dve.tensor_copy(taps[:, k0:k1, :], env.psum[half][:, 0:(k1 - k0) * P]
                                .rearrange("p (k o) -> p k o", o=P)).then_inc(w_ready, 1)
            with dve.Fori(0, IMAGES) as n_:
                dve.wait_ge(evac_free, n_ + 3)
                for h in range(2):
                    dve.bn_stats(env.bnst[:, bass.ds(n_ * 12 + h * 6, 6)],
                                 CONV[:, bass.ds(n_ * PIX + h * HALF, HALF)]).then_inc(stats, 1)
            dve.wait_ge(stats, 2 * IMAGES)
            link(dve.bn_aggr(t[:, 12:14], env.bnst[:, :].rearrange("p (n s) -> p n s", s=6)))
            link(dve.tensor_tensor(sv, vari2, wrs, ALU.mult))
            dve.tensor_tensor(sv, sv, wrs, ALU.mult).then_inc(var2, 1)
            dve.wait_ge(rs2, 1)
            link(dve.tensor_tensor(tmp, g2, wrs, ALU.mult))
            link(dve.tensor_tensor(A2, tmp, rstd2, ALU.mult))
            link(dve.tensor_tensor(tmp, mean2, A2, ALU.mult))
            link(dve.tensor_tensor(B2, b2, tmp, ALU.subtract))

        @block.scalar
        def _(act):
            link = chain(act, asteps)
            act.preload_act_table_set("natural_log_exp_and_others")
            act.sem_inc(evac_free, 2)
            act.wait_ge(w_loaded, 16)
            act.activation(sg[:, :], cw[:, :], ACT.Sign).then_inc(w_sign, 1)
            act.wait_ge(var1, 1)
            link(act.activation(lnv1, vari1, ACT.Ln, bias=env.eps[:, 1:2], scale=1.0))
            act.activation(rstd1, lnv1, ACT.Exp, scale=-0.5).then_inc(rs1, 1)
            act.wait_ge(steps, 7)
            link(act.activation(wln, wss, ACT.Ln, scale=1.0 / (GROUP_IN * TAPS - 1)))
            act.activation(wrs, wln, ACT.Exp, scale=-0.5).then_inc(rs1, 1)
            act.wait_ge(coef1, 1)
            act.wait_ge(border, 2)

            def sign(n, q):
                act.wait_ge(evac_free, n + 1)
                act.activation(padded[q][:, 1:1 + SIDE, 1:1 + SIDE],
                               image(Y, n).rearrange("p (h w) -> p h w", w=SIDE), ACT.Sign, bias=B1, scale=A1)\
                   .then_inc(sign_ready, 1)

            def evacuate(n, q):
                act.wait_ge(conv_ready, n + 1)
                act.activation(image(CONV, n), env.psum[2 + q][:, :], ACT.Copy).then_inc(evac_free, 1)

            sign(0, 0)
            with by_two(act, 0, IMAGES - 2) as n:
                for q in range(2):
                    sign(n + q + 1, 1 - q)
                    evacuate(n + q, q)
            sign(IMAGES - 1, 1)
            evacuate(IMAGES - 2, 0)
            evacuate(IMAGES - 1, 1)
            act.wait_ge(var2, 1)
            link(act.activation(lnv2, sv, ACT.Ln, bias=env.eps[:, 1:2], scale=1.0))
            act.activation(rstd2, lnv2, ACT.Exp, scale=-0.5).then_inc(rs2, 1)

        @block.tensor
        def _(pe):
            pe.wait_ge(w_spread, TAPS)
            for k in range(TAPS):
                mm = pe.matmul(env.psum[k // 8][:, (k % 8) * P:(k % 8 + 1) * P], spread[:, k, :], env.idb[:, :],
                               start=True, stop=True)
                if k in (7, TAPS - 1):
                    mm.then_inc(w_turned, 1)
            pe.wait_ge(w_ready, 2)
            with by_two(pe, 0, IMAGES) as n:
                for q in range(2):
                    pe.wait_ge(sign_ready, n + q + 1)
                    pe.wait_ge(evac_free, n + q + 1)
                    for h in range(2):
                        for k in range(TAPS):
                            dy, dx = divmod(k, 3)
                            mm = pe.matmul(env.psum[2 + q][:, h * HALF:(h + 1) * HALF], taps[:, k, :],
                                           padded[q][:, h * 16 + dy:h * 16 + dy + 16, dx:dx + SIDE],
                                           start=(k == 0), stop=(k == TAPS - 1))
                    mm.then_inc(conv_ready, 1)


def phase_tokens0(nc, env, a):
    X, Y, CONV, par = env.X, env.Y, env.CONV, env.par
    with ExitStack() as ctx:
        sem = lambda n: ctx.enter_context(nc.semaphore(n))
        sb = lambda n, s, d=F32: ctx.enter_context(nc.sbuf_tensor(n, s, d))
        wr_loaded, wr_turned, wr_ready = sem("t0_wr_loaded"), sem("t0_wr_turned"), sem("t0_wr_ready")
        sum_ready, act_ready, x_ready, rows_ready = sem("t0_sum_ready"), sem("t0_act_ready"), sem("t0_x_ready"), sem("t0_rows_ready")
        kept, half_ready, coef = sem("t0_kept"), sem("t0_half_ready"), sem("t0_coef")
        neg = [sb(f"t0_neg{q}", [P, PIX]) for q in range(2)]
        negs = sb("t0_negs", [P, 2])
        negB2, negalpha = negs[:, 0:1], negs[:, 1:2]
        copied_free, stats_free, steps = sem("t0_copied_free"), sem("t0_stats_free"), sem("t0_steps")
        wr, wc = sb("t0_wr", [P, E0]), sb("t0_wc", [P, E0])
        u = [sb(f"t0_u{q}", [P, PIX]) for q in range(2)]
        rows, logits = env.psum[0:2], env.psum[2:4]
        A2, B2, alpha = par[:, 7:8], par[:, 8:9], par[:, 4:5]
        block = ctx.enter_context(nc.Block())

        @block.sync
        def _(sp):
            sp.dma_start(wr[:, :], a["w_router"]).then_inc(wr_loaded, 16)

        @block.tensor
        def _(pe):
            pe.wait_ge(wr_loaded, 16)
            pe.matmul(logits[0][:, 0:E0], env.cen[:, :], wr[:, :], start=True, stop=True).then_inc(wr_turned, 1)
            pe.wait_ge(wr_ready, 1)
            with by_two(pe, 0, IMAGES) as n:
                for q in range(2):
                    pe.wait_ge(x_ready, n + q + 1)
                    pe.wait_ge(copied_free, n + q + 1)
                    pe.wait_ge(stats_free, n + q + 1)
                    for j in range(TPI):
                        pe.transpose(rows[q][:, j * P:(j + 1) * P], u[q][:, j * P:(j + 1) * P], env.idf[:, :])
                    for j in range(TPI):
                        mm = pe.matmul(logits[q][:, j * E0:(j + 1) * E0], u[q][:, j * P:(j + 1) * P], wc[:, :],
                                       start=True, stop=True)
                    mm.then_inc(rows_ready, 1)

        @block.vector
        def _(dve):
            dve.wait_ge(wr_turned, 1)
            dve.tensor_copy(wc[:, :], logits[0][:, 0:E0]).then_inc(wr_ready, 1)
            dve.sem_inc(stats_free, 2)
            dve.tensor_scalar(negB2, B2, -1.0, None, ALU.mult).then_inc(coef, 1)
            dve.tensor_scalar(negalpha, alpha, -1.0, None, ALU.mult).then_inc(coef, 1)

            def residual(n, q, first=False):
                if not first:
                    dve.wait_ge(rows_ready, n - 1)
                    dve.wait_ge(kept, n - 1)
                dve.scalar_tensor_tensor(u[q][:, :], image(CONV, n), A2, image(Y, n), ALU.mult, ALU.add).then_inc(sum_ready, 1)

            def add(n, q):
                dve.wait_ge(half_ready, n + 1)
                dve.scalar_tensor_tensor(u[q][:, :], neg[q][:, :], negalpha, u[q][:, :], ALU.mult, ALU.add).then_inc(x_ready, 1)

            def statistics(n, q):
                dve.wait_ge(rows_ready, n + 1)
                dve.tensor_copy(env.logit[:, bass.ds(n * TPI * E0, TPI * E0)], logits[q][:, 0:TPI * E0])
                dve.wait_ge(copied_free, n + 3)
                for j in range(TPI):
                    st = dve.bn_stats(env.rowst[:, bass.ds((n * TPI + j) * 6, 6)], Y[:, bass.ds(n * PIX + j * P, P)])
                st.then_inc(stats_free, 1)

            for n in range(2):
                residual(n, n, first=True)
            add(0, 0)
            with by_two(dve, 0, IMAGES - 2) as n:
                for q in range(2):
                    add(n + q + 1, 1 - q)
                    statistics(n + q, q)
                    residual(n + q + 2, q)
            add(IMAGES - 1, 1)
            statistics(IMAGES - 2, 0)
            statistics(IMAGES - 1, 1)
            dve.wait_ge(stats_free, IMAGES + 2)

        @block.gpsimd
        def _(pool):
            def add_x(n, q):
                pool.wait_ge(act_ready, n * 2 + 2)
                pool.tensor_tensor(u[q][:, :], image(X, n), u[q][:, :], ALU.add).then_inc(half_ready, 1)

            def keep(n, q):
                wait_apart(pool, x_ready, n + 1, env.passed["pool"])
                pool.tensor_copy(image(X, n), u[q][:, :]).then_inc(kept, 1)

            add_x(0, 0)
            with by_two(pool, 0, IMAGES - 2) as n:
                for q in range(2):
                    add_x(n + q + 1, 1 - q)
                    keep(n + q, q)
            add_x(IMAGES - 1, 1)
            keep(IMAGES - 2, 0)
            keep(IMAGES - 1, 1)
            pool.wait_ge(kept, IMAGES)

        @block.scalar
        def _(act):
            act.preload_act_table_set("natural_log_exp_and_others")
            act.sem_inc(copied_free, 2)
            act.wait_ge(coef, 2)

            def prelu(n, q):
                act.wait_ge(sum_ready, n + 1)
                act.activation(neg[q][:, :], u[q][:, :], ACT.Relu, bias=negB2, scale=-1.0).then_inc(act_ready, 1)
                act.activation(u[q][:, :], u[q][:, :], ACT.Relu, bias=B2, scale=1.0).then_inc(act_ready, 1)

            def copy(n, q):
                act.wait_ge(rows_ready, n + 1)
                act.activation(image(Y, n), rows[q][:, :], ACT.Copy).then_inc(copied_free, 1)

            prelu(0, 0)
            prelu(1, 1)
            with by_two(act, 0, IMAGES - 2) as n:
                for q in range(2):
                    copy(n + q, q)
                    prelu(n + q + 2, q)
            copy(IMAGES - 2, 0)
            copy(IMAGES - 1, 1)
            act.wait_ge(copied_free, IMAGES + 2)


def phase_route0(nc, env):
    with ExitStack() as ctx:
        sem = lambda n: ctx.enter_context(nc.semaphore(n))
        sb = lambda n, s, d=F32: ctx.enter_context(nc.sbuf_tensor(n, s, d))
        steps, var_ready, rstd_ready, logs = sem("r0_steps"), sem("r0_var_ready"), sem("r0_rstd_ready"), sem("r0_logs")
        gap_ready, exp_ready, hot_ready = sem("r0_gap_ready"), sem("r0_exp_ready"), sem("r0_hot_ready")
        total_ready, total_copied, prefix_ready = sem("r0_total_ready"), sem("r0_total_copied"), sem("r0_prefix_ready")
        small = {k: sb(f"r0_{k}", [P, TILES]) for k in
                 ("mean2", "dm", "m2", "var", "ln", "top1", "top2", "rev1", "rev2", "gap", "ex", "g1", "g2", "swap", "hi", "lo", "pid", "slot")}
        v = {k: x[:, :] for k, x in small.items()}
        wide = [sb(f"r0_wide{k}", [P, TILES, E0]) for k in range(3)]
        hot = sb("r0_hot", [P, PAIRS, TILES], BF16)
        total, where = (sb(f"r0_{k}", [P, PAIRS * TILES]) for k in ("total", "where"))
        pc = {k: sb(f"r0_p{k}", [P, PAIRS]) for k in ("cum", "count", "tiles", "cumt", "adj")}
        pi = sb("r0_pi", [P, PAIRS], I32)
        st = env.rowst[:, :].rearrange("p (t s) -> p t s", s=6)
        over_e = lambda x: x.unsqueeze(2).broadcast_to([P, TILES, E0])
        rev = env.rev.unsqueeze(1).broadcast_to([P, TILES, E0])
        chunks = PAIRS * TILES // HALF
        bank = lambda c: env.psum[c // 2][:, (c % 2) * HALF:(c % 2 + 1) * HALF]
        block = ctx.enter_context(nc.Block())

        @block.scalar
        def _(act):
            act.preload_act_table_set("natural_log_exp_and_others")
            act.wait_ge(var_ready, 1)
            act.activation(v["ln"], v["var"], ACT.Ln, bias=env.eps[:, 1:2], scale=1.0 / C).then_inc(logs, 1)
            act.wait_ge(logs, 1)
            act.activation(env.rstd[:, :], v["ln"], ACT.Exp, scale=-0.5).then_inc(rstd_ready, 1)
            act.wait_ge(gap_ready, 1)
            act.activation(v["ex"], v["gap"], ACT.Exp).then_inc(exp_ready, 1)
            for c in range(chunks):
                act.wait_ge(total_ready, c + 1)
                act.activation(total[:, c * HALF:(c + 1) * HALF], bank(c), ACT.Copy).then_inc(total_copied, 1)

        @block.tensor
        def _(pe):
            pe.wait_ge(hot_ready, 1)
            cols = hot[:, :, :].rearrange("p a t -> p (a t)")
            for c in range(chunks):
                pe.matmul(bank(c), env.ones16[:, :], cols[:, c * HALF:(c + 1) * HALF], start=True, stop=True)\
                  .then_inc(total_ready, 1)
            for c in range(chunks):
                pe.wait_ge(total_copied, c + 1)
                pe.matmul(bank(c), env.ltri[:, :], cols[:, c * HALF:(c + 1) * HALF], start=True, stop=True)\
                  .then_inc(prefix_ready, 1)

        @block.vector
        def _(dve):
            link = chain(dve, steps)
            link(dve.tensor_tensor(v["dm"], st[:, :, 1], st[:, :, 4], ALU.subtract))
            link(dve.tensor_tensor(v["m2"], st[:, :, 2], st[:, :, 5], ALU.add))
            link(dve.tensor_tensor(v["dm"], v["dm"], v["dm"], ALU.mult))
            dve.scalar_tensor_tensor(v["var"], v["dm"], C / 4.0, v["m2"], ALU.mult, ALU.add).then_inc(var_ready, 1)
            link(dve.tensor_tensor(v["mean2"], st[:, :, 1], st[:, :, 4], ALU.add))
            dve.wait_ge(rstd_ready, 1)
            link(dve.scalar_tensor_tensor(env.shift[:, :], v["mean2"], -0.5, env.rstd[:, :], ALU.mult, ALU.mult))
            l, hit, l2 = (w[:, :, :] for w in wide)
            link(dve.tensor_tensor(l, env.logit[:, :].rearrange("p (t e) -> p t e", e=E0), over_e(env.rstd[:, :]), ALU.mult))
            link(dve.tensor_reduce(v["top1"], l, AX.X, ALU.max))
            link(dve.tensor_tensor(hit, l, over_e(v["top1"]), ALU.is_equal))
            link(dve.tensor_tensor(hit, hit, rev, ALU.mult))
            link(dve.tensor_reduce(v["rev1"], hit, AX.X, ALU.max))
            link(dve.tensor_tensor(hit, hit, over_e(v["rev1"]), ALU.is_equal))
            link(dve.scalar_tensor_tensor(l2.rearrange("p t e -> p (t e)"), hit.rearrange("p t e -> p (t e)"), -1e30,
                                          l.rearrange("p t e -> p (t e)"), ALU.mult, ALU.add))
            link(dve.tensor_reduce(v["top2"], l2, AX.X, ALU.max))
            link(dve.tensor_tensor(hit, l2, over_e(v["top2"]), ALU.is_equal))
            link(dve.tensor_tensor(hit, hit, rev, ALU.mult))
            link(dve.tensor_reduce(v["rev2"], hit, AX.X, ALU.max))
            dve.tensor_tensor(v["gap"], v["top2"], v["top1"], ALU.subtract).then_inc(gap_ready, 1)
            link(dve.tensor_tensor(v["lo"], v["rev1"], v["rev2"], ALU.max))
            link(dve.tensor_tensor(v["hi"], v["rev1"], v["rev2"], ALU.min))
            link(dve.tensor_scalar(v["pid"], v["lo"], -1.0, float(E0), ALU.mult, ALU.add))
            link(dve.scalar_tensor_tensor(v["pid"], v["lo"], float(E0 - 1), v["pid"], ALU.add, ALU.mult))
            link(dve.tensor_tensor(v["hi"], v["lo"], v["hi"], ALU.subtract))
            link(dve.scalar_tensor_tensor(v["pid"], v["pid"], 0.5, v["hi"], ALU.mult, ALU.add))
            link(dve.tensor_scalar(v["pid"], v["pid"], -1.0, None, ALU.add))
            dve.tensor_tensor(hot[:, :, :], v["pid"].unsqueeze(1).broadcast_to([P, PAIRS, TILES]),
                              env.pair_no.unsqueeze(2).broadcast_to([P, PAIRS, TILES]), ALU.is_equal).then_inc(hot_ready, 1)
            dve.wait_ge(exp_ready, 1)
            link(dve.tensor_scalar(v["g1"], v["ex"], 1.0, None, ALU.add))
            link(dve.reciprocal(v["g1"], v["g1"]))
            link(dve.tensor_tensor(v["g2"], v["ex"], v["g1"], ALU.mult))
            link(dve.tensor_tensor(v["swap"], v["rev1"], v["rev2"], ALU.is_gt))
            link(dve.tensor_tensor(v["lo"], v["g1"], v["g2"], ALU.subtract))
            link(dve.tensor_tensor(v["swap"], v["swap"], v["lo"], ALU.mult))
            link(dve.tensor_tensor(v["lo"], v["g2"], v["swap"], ALU.add))
            link(dve.tensor_tensor(v["hi"], v["g1"], v["swap"], ALU.subtract))
            gates = env.gates[:, :].rearrange("p (t g) -> p t g", g=2)
            link(dve.tensor_scalar(gates[:, :, 0], v["lo"], 1.0 / WSCALE ** 2, None, ALU.mult))
            link(dve.tensor_scalar(gates[:, :, 1], v["hi"], 1.0 / WSCALE ** 2, None, ALU.mult))
            dve.wait_ge(total_copied, chunks)
            link(dve.tensor_tensor_scan(where[:, :], total[:, :], env.eps[:, 2:3].broadcast_to([P, PAIRS * TILES]), 0.0, ALU.add, ALU.add))
            cum, count, tiles, cumt, adj = (pc[k][:, :] for k in ("cum", "count", "tiles", "cumt", "adj"))
            link(dve.tensor_copy(cum, where[:, :].rearrange("p (a t) -> p a t", t=TILES)[:, :, TILES - 1]))
            link(dve.tensor_tensor(where[:, :], where[:, :], total[:, :], ALU.subtract))
            link(dve.tensor_copy(count[:, 0:1], cum[:, 0:1]))
            link(dve.tensor_tensor(count[:, 1:PAIRS], cum[:, 1:PAIRS], cum[:, 0:PAIRS - 1], ALU.subtract))
            link(dve.tensor_scalar(tiles, count, float(SLOT - 1), float(SLOT), ALU.add, ALU.max))
            link(dve.tensor_copy(pi[:, :], tiles))
            link(dve.tensor_scalar(pi[:, :], pi[:, :], SLOT.bit_length() - 1, None, ALU.arith_shift_right))
            link(dve.tensor_copy(tiles, pi[:, :]))
            link(dve.tensor_tensor_scan(cumt, tiles, env.eps[:, 2:3].broadcast_to([P, PAIRS]), 0.0, ALU.add, ALU.add))
            link(dve.memset(env.starts[:, 0:1], 0))
            link(dve.tensor_copy(env.starts[:, 1:PAIRS + 1], cumt[0:1, :]))
            link(dve.tensor_scalar(env.starts[:, PAIRS + 1:PAIRS + 2], cumt[0:1, PAIRS - 1:PAIRS], -1.0, float(MAX_TILES + 1),
                                   ALU.mult, ALU.add))
            link(dve.tensor_tensor(adj, cumt, tiles, ALU.subtract))
            link(dve.scalar_tensor_tensor(adj, adj, float(SLOT), cum, ALU.mult, ALU.subtract))
            link(dve.tensor_tensor(adj, adj, count, ALU.add))
            grid = lambda x: x.rearrange("p (a t) -> p a t", t=TILES)
            link(dve.tensor_tensor(grid(where[:, :]), grid(where[:, :]), adj.unsqueeze(2).broadcast_to([P, PAIRS, TILES]), ALU.add))
            for c in range(chunks):
                dve.wait_ge(prefix_ready, c + 1)
                part = slice(c * HALF, (c + 1) * HALF)
                link(dve.tensor_tensor(where[:, part], bank(c), where[:, part], ALU.add))
            link(dve.tensor_tensor(where[:, :], where[:, :], hot[:, :, :].rearrange("p a t -> p (a t)"), ALU.mult))
            link(dve.tensor_reduce(v["slot"], where[:, :].rearrange("p (a t) -> p t a", t=TILES), AX.X, ALU.add))
            link(dve.tensor_copy(env.slot[:, :], v["slot"]))


def phase_dispatch(nc, env):
    Y = env.Y
    with ExitStack() as ctx:
        sem = lambda n: ctx.enter_context(nc.semaphore(n))
        depth = 4
        rows = [ctx.enter_context(nc.sbuf_tensor(f"d0_rows{k}", [P, ROW], F32)) for k in range(depth)]
        index = [ctx.enter_context(nc.sbuf_tensor(f"d0_index{k}", [P, 1], U32)) for k in range(depth)]
        ready = sem("d0_ready")
        sent = [sem(f"d0_sent{k}") for k in range(depth)]
        block = ctx.enter_context(nc.Block())

        def fill(dve, i, k):
            dve.tensor_scalar(rows[k][:, 0:C], Y[:, bass.ds(i * P, P)], env.rstd[:, bass.ds(i, 1)],
                              env.shift[:, bass.ds(i, 1)], ALU.mult, ALU.add).then_inc(ready, 1)
            dve.tensor_copy(rows[k][:, C:ROW], env.gates[:, bass.ds(i * 2, 2)]).then_inc(ready, 1)
            dve.tensor_copy(index[k][:, :], env.slot[:, bass.ds(i, 1)]).then_inc(ready, 1)

        def send(pool, i, k):
            wait_apart(pool, ready, i * 3 + 3, env.passed["pool"])
            pool.indirect_dma_start(env.xg, bass.IndirectOffsetOnAxis(ap=index[k][:, :], axis=0), rows[k][:, :], None)\
                .then_inc(sent[k], 16)

        @block.vector
        def _(dve):
            for k in range(depth):
                fill(dve, k, k)
            with dve.Fori(1, TILES // depth) as j:
                for k in range(depth):
                    dve.wait_ge(sent[k], j * 16)
                    fill(dve, j * depth + k, k)

        @block.gpsimd
        def _(pool):
            pool.wait_ge(env.cleared, CLEARS * 16)
            with pool.Fori(0, TILES // depth) as j:
                for k in range(depth):
                    send(pool, j * depth + k, k)
            for k in range(depth):
                pool.wait_ge(sent[k], TILES // depth * 16)


def split_weights0(nc, env, a):
    W = env.weights
    half2 = lambda e, part: W[:, e * WCOLS:e * WCOLS + 4 * H0].rearrange("p (w s n) -> p w s n", w=2, s=2)[:, :, part, :]
    with ExitStack() as ctx:
        sem = lambda n: ctx.enter_context(nc.semaphore(n))
        sb = lambda n, s, d=F32: ctx.enter_context(nc.sbuf_tensor(n, s, d))
        loaded, biases = [sem(f"w0_loaded{q}") for q in range(2)], sem("w0_biases")
        high, low, steps = sem("w0_high"), sem("w0_low"), sem("w0_steps")
        raw = [sb(f"w0_raw{q}", [P, 2 * H0]) for q in range(2)]
        b1, b2, rest = sb("w0_b1", [P, E0 * KM]), sb("w0_b2", [P, E0 * C]), sb("w0_rest", [P, E0 * C])
        parts = [sb(f"w0_part{k}", [P, E0 * C], BF16) for k in range(3)]
        block = ctx.enter_context(nc.Block())

        @block.sync
        def _(sp):
            sp.dma_start(b1[:, :], a["b1"]).then_inc(biases, 16)
            sp.dma_start(b2[:, :], a["b2"].broadcast_to([P, E0 * C])).then_inc(biases, 16)
            for e in range(E0):
                if e >= 2:
                    sp.wait_ge(low, e - 1)
                sp.dma_start(raw[e % 2][:, :], a["w_moe0"][e, :, :]).then_inc(loaded[e % 2], 16)

        @block.scalar
        def _(act):
            act.preload_act_table_set("natural_log_exp_and_others")
            for e in range(E0):
                act.wait_ge(loaded[e % 2], 16 * (e // 2 + 1))
                act.activation(half2(e, 0), raw[e % 2][:, :].rearrange("p (w n) -> p w n", w=2), ACT.Copy, scale=WSCALE)\
                   .then_inc(high, 1)

        @block.vector
        def _(dve):
            link = chain(dve, steps)
            dve.wait_ge(biases, 32)
            link(dve.tensor_scalar(b2[:, :], b2[:, :], WSCALE ** 2, None, ALU.mult))
            link(dve.tensor_copy(parts[0][:, :], b2[:, :]))
            link(dve.tensor_tensor(rest[:, :], b2[:, :], parts[0][:, :], ALU.subtract))
            link(dve.tensor_copy(parts[1][:, :], rest[:, :]))
            link(dve.tensor_tensor(rest[:, :], rest[:, :], parts[1][:, :], ALU.subtract))
            link(dve.tensor_copy(parts[2][:, :], rest[:, :]))
            blocks = W[:, :].rearrange("p (e n) -> p e n", n=WCOLS)
            biasrow = blocks[:, :, 4 * H0:4 * H0 + C].bitcast(BF16)
            link(dve.memset(biasrow, 0.0))
            for k in range(3):
                link(dve.tensor_copy(biasrow[32 * k:32 * k + 1, :, :],
                                     parts[k][32 * k:32 * k + 1, :].rearrange("p (e n) -> p e n", e=E0)))
            for e in range(E0):
                at = e * WCOLS + 4 * H0 + C
                link(dve.tensor_scalar(W[:, at:at + 2 * KM].bitcast(F32), b1[:, e * KM:(e + 1) * KM], WSCALE, None, ALU.mult))
            for e in range(E0):
                dve.wait_ge(high, e + 1)
                for w in range(2):
                    at = e * WCOLS + w * 2 * H0
                    ins = dve.scalar_tensor_tensor(W[:, at + H0:at + 2 * H0], raw[e % 2][:, w * H0:(w + 1) * H0], WSCALE,
                                                   W[:, at:at + H0], ALU.mult, ALU.subtract)
                ins.then_inc(low, 1)
            dve.wait_ge(low, E0)


def phase_experts0(nc, env, a):
    with ExitStack() as ctx:
        sem = lambda n: ctx.enter_context(nc.semaphore(n))
        sb = lambda n, s, d=F32: ctx.enter_context(nc.sbuf_tensor(n, s, d))
        staged = [sem(f"m0_staged{q}") for q in range(2)]
        rows_loaded, turned, x_split = sem("m0_rows_loaded"), sem("m0_turned"), sem("m0_x_split")
        x_high, h_ready, relu_ready, h_split = sem("m0_x_high"), sem("m0_h_ready"), sem("m0_relu_ready"), sem("m0_h_split")
        filled = sem("m0_filled")
        hh_ready, result_free = sem("m0_hh_ready"), sem("m0_result_free")
        lo_ready, hi_ready, part_ready, out_ready = (sem(f"m0_{x}") for x in ("lo_ready", "hi_ready", "part_ready", "out_ready"))
        gates_ready, stored, table_loaded, next_gates = sem("m0_gates_ready"), sem("m0_stored"), sem("m0_table_loaded"), sem("m0_next_gates")
        stage = [[sb(f"m0_stage{q}{e}", [P, WCOLS], F16) for e in range(2)] for q in range(2)]
        table = sb("m0_table", [1, 2 * PAIRS + 2], I32)
        rows = sb("m0_rows", [P, SUB, ROW])
        xh, xl = sb("m0_xh", [P, SLOT], F16), sb("m0_xl", [P, SLOT], F16)
        hf = [sb(f"m0_hf{e}", [P, KM, SLOT]) for e in range(2)]
        hh = [sb(f"m0_hh{e}", [P, KM, SLOT], F16) for e in range(2)]
        hl = [sb(f"m0_hl{e}", [P, KM, SLOT], F16) for e in range(2)]
        gates, coming = sb("m0_gates", [P, SUB, 2]), sb("m0_coming", [P, SUB, 2])
        part, result = sb("m0_part", [P, SUB, C]), sb("m0_result", [P, SUB, C])
        hidden, turn = env.psum[0:2], env.psum[2][:, 0:SLOT]
        y = [env.psum[3][:, e * HALF:e * HALF + SUB * C].rearrange("p (s c) -> p s c", s=SUB) for e in range(2)]
        block = ctx.enter_context(nc.Block())

        def pairs(engine):
            with engine.Fori(0, PAIRS // 2) as half:
                for q in range(2):
                    p = half * 2 + q
                    first = engine.value_load(env.starts[0:1, bass.ds(p, 1)], min_val=0, max_val=MAX_TILES - 1)
                    last = engine.value_load(env.starts[0:1, bass.ds(p + 1, 1)], min_val=1, max_val=MAX_TILES)
                    yield half, q, p, first, last

        @block.sync
        def _(sp):
            sp.dma_start(table[:, :], a["k_pairs"]).then_inc(table_loaded, 16)
            sp.wait_ge(table_loaded, 16)

            def load(i):
                sp.dma_start(rows[:, :, :], env.xg[bass.ds(i * SLOT, SLOT), :].rearrange("(s p) c -> p s c", p=P))\
                  .then_inc(rows_loaded, 16)

            def stage_pair(p, q):
                for e in range(2):
                    expert = sp.value_load(table[0:1, bass.ds(p * 2 + e, 1)], min_val=0, max_val=E0 - 1)
                    sp.dma_start(stage[q][e][:, :].bitcast(U32),
                                 env.weights[:, :].bitcast(U32)[:, bass.ds(expert * (WCOLS // 2), WCOLS // 2)]).then_inc(staged[q], 16)

            load(0)
            stage_pair(0, 0)
            with sp.Fori(0, PAIRS // 2) as half:
                for q in range(2):
                    p = half * 2 + q
                    first = sp.value_load(env.starts[0:1, bass.ds(p, 1)], min_val=0, max_val=MAX_TILES - 1)
                    last = sp.value_load(env.starts[0:1, bass.ds(p + 1, 1)], min_val=1, max_val=MAX_TILES)
                    sp.wait_ge(hi_ready, first + 1)
                    stage_pair(p + 1, 1 - q)
                    with sp.Fori(first, last) as i:
                        sp.wait_ge(x_split, i + 2)
                        load(i + 1)
            total = sp.value_load(env.starts[0:1, PAIRS:PAIRS + 1], min_val=PAIRS, max_val=MAX_TILES)
            wait_apart(sp, rows_loaded, total * 16 + 16, env.passed["sp"])
            sp.wait_ge(staged[0], 16 * (PAIRS + 2))

        @block.gpsimd
        def _(pool):
            pool.sem_inc(result_free, 1)
            total = pool.value_load(env.starts[0:1, PAIRS:PAIRS + 1], min_val=PAIRS, max_val=MAX_TILES)
            with pool.Fori(total, MAX_TILES + 1) as i:
                pool.dma_start(env.yg[bass.ds(i * SLOT, SLOT), :].rearrange("(s p) c -> p s c", p=P),
                               env.zero[:, 0:C].unsqueeze(1).broadcast_to([P, SUB, C])).then_inc(filled, 16)
            spare = pool.value_load(env.starts[0:1, PAIRS + 1:PAIRS + 2], min_val=1, max_val=MAX_TILES + 1 - PAIRS)
            wait_apart(pool, filled, spare * 16, env.passed["pool"])
            for half, q, p, first, last in pairs(pool):
                with pool.Fori(first, last) as i:
                    pool.wait_ge(out_ready, i + 2)
                    pool.dma_start(env.yg[bass.ds(i * SLOT, SLOT), :].rearrange("(s p) c -> p s c", p=P), result[:, :, :])\
                        .then_inc(stored, 16)
                    pool.wait_ge(stored, i * 16 + 16)
                    pool.sem_inc(result_free, 1)

        @block.tensor
        def _(pe):
            def transpose(i):
                pe.wait_ge(rows_loaded, i * 16 + 16)
                pe.wait_ge(x_split, i + 1)
                for s in range(SUB):
                    mm = pe.transpose(turn[:, s * P:(s + 1) * P], rows[:, s, 0:C], env.idf[:, :])
                mm.then_inc(turned, 1)

            def up(w, e):
                for m in range(KM):
                    out = hidden[e][:, m * SLOT:(m + 1) * SLOT]
                    high, low = w[:, m * P:(m + 1) * P], w[:, H0 + m * P:H0 + (m + 1) * P]
                    pe.matmul(out, high, xh[:, :], start=True, stop=False)
                    pe.matmul(out, high, xl[:, :], start=False, stop=False)
                    mm = pe.matmul(out, low, xh[:, :], start=False, stop=True)
                    if m % 2:
                        mm.then_inc(h_ready, 1)

            def down(w, e):
                for s in range(SUB):
                    cols = slice(s * P, (s + 1) * P)
                    for k in range(KM):
                        high, low = w[:, 2 * H0 + k * P:2 * H0 + (k + 1) * P], w[:, 3 * H0 + k * P:3 * H0 + (k + 1) * P]
                        pe.matmul(y[e][:, s, :], hh[e][:, k, cols], high, start=(k == 0), stop=False)
                        pe.matmul(y[e][:, s, :], hh[e][:, k, cols], low, start=False, stop=False)
                        pe.matmul(y[e][:, s, :], hl[e][:, k, cols], high, start=False, stop=False)
                    mm = pe.matmul(y[e][:, s, :], env.ones16[:, :], w[:, 4 * H0:4 * H0 + C].bitcast(BF16), start=False, stop=True)
                mm.then_inc((lo_ready, hi_ready)[e], 1)

            pe.sem_inc(hi_ready, 1)
            transpose(0)
            for half, q, p, first, last in pairs(pe):
                wait_apart(pe, staged[q], half * 32 + 32, env.passed["pe"])
                with pe.Fori(first, last) as i:
                    pe.wait_ge(x_split, i + 2)
                    up(stage[q][0], 0)
                    up(stage[q][1], 1)
                    transpose(i + 1)
                    pe.wait_ge(h_split, i * 4 + 6)
                    pe.wait_ge(out_ready, i + 1)
                    down(stage[q][0], 0)
                    pe.wait_ge(h_split, i * 4 + 8)
                    down(stage[q][1], 1)

        @block.scalar
        def _(act):
            act.preload_act_table_set("natural_log_exp_and_others")

            def high_x(i):
                act.wait_ge(turned, i + 1)
                act.activation(xh[:, :], turn, ACT.Copy).then_inc(x_high, 1)

            high_x(0)
            for half, q, p, first, last in pairs(act):
                act.wait_ge(staged[q], half * 32 + 32)
                with act.Fori(first, last) as i:
                    for e in range(2):
                        bias = stage[q][e][:, 4 * H0 + C:4 * H0 + C + 2 * KM].bitcast(F32)
                        for b in range(2):
                            act.wait_ge(h_ready, i * 4 + (2 * e + b + 1))
                            act.wait_ge(h_split, i * 4 + (2 * e + b + 1))
                            for m in (2 * b, 2 * b + 1):
                                ins = act.activation(hf[e][:, m, :], hidden[e][:, m * SLOT:(m + 1) * SLOT], ACT.Relu,
                                                     bias=bias[:, m:m + 1], scale=1.0)
                            ins.then_inc(relu_ready, 1)
                    high_x(i + 1)
                    act.wait_ge(lo_ready, i + 1)
                    act.wait_ge(gates_ready, i + 1)
                    act.wait_ge(out_ready, i + 1)
                    for s in range(SUB):
                        ins = act.activation(part[:, s, :], y[0][:, s, :], ACT.Copy, scale=gates[:, s, 0:1])
                    ins.then_inc(part_ready, 1)

        @block.vector
        def _(dve):
            dve.sem_inc(x_split, 1)
            dve.sem_inc(h_split, 4)
            dve.sem_inc(out_ready, 1)

            def low_x(i):
                dve.wait_ge(x_high, i + 1)
                dve.tensor_copy(coming[:, :, :], rows[:, :, C:ROW]).then_inc(next_gates, 1)
                dve.tensor_tensor(xl[:, :], turn, xh[:, :], ALU.subtract).then_inc(x_split, 1)

            def take_gates(i):
                dve.wait_ge(next_gates, i + 1)
                dve.tensor_copy(gates[:, :, :], coming[:, :, :]).then_inc(gates_ready, 1)

            dve.wait_ge(turned, 1)
            low_x(0)
            take_gates(0)
            for half, q, p, first, last in pairs(dve):
                with dve.Fori(first, last) as i:
                    for e in range(2):
                        for b in range(2):
                            dve.wait_ge(relu_ready, i * 4 + (2 * e + b + 1))
                            m = slice(2 * b, 2 * b + 2)
                            dve.tensor_copy(hh[e][:, m, :], hf[e][:, m, :]).then_inc(hh_ready, 1)
                            dve.wait_ge(hh_ready, i * 4 + (2 * e + b + 1))
                            dve.tensor_tensor(hl[e][:, m, :], hf[e][:, m, :], hh[e][:, m, :], ALU.subtract).then_inc(h_split, 1)
                    low_x(i + 1)
                    dve.wait_ge(hi_ready, i + 2)
                    dve.wait_ge(part_ready, i + 1)
                    dve.wait_ge(result_free, i + 1)
                    for s in range(SUB):
                        ins = dve.scalar_tensor_tensor(result[:, s, :], y[1][:, s, :], gates[:, s, 1:2], part[:, s, :], ALU.mult, ALU.add)
                    ins.then_inc(out_ready, 1)
                    dve.wait_ge(out_ready, i + 2)
                    take_gates(i + 1)


def phase_involution(nc, env, a, out):
    X, par = env.X, env.par
    with ExitStack() as ctx:
        names = ("gathered turned x_added cent_ready sq_ready var_ready ln_ready rstd_ready y_ready t_ready v_ready "
                 "padded_ready e2_ready group_ready gvar_ready gln_ready grstd_ready coef_ready relu_ready split_ready "
                 "tap_ready product_ready summed pool_summed done steps w_loaded w_ready border sent index_ready").split()
        S = {n: ctx.enter_context(nc.semaphore(f"iv_{n}")) for n in names}
        sb = lambda n, s, d=F32: ctx.enter_context(nc.sbuf_tensor(f"iv_{n}", s, d))
        wv, w1, gavg = sb("wv", [P, C]), sb("w1", [P, P]), sb("gavg", [P, P])
        w2, w2b, gn = sb("w2", [P, TAPS, P]), sb("w2b", [P, TAPS]), sb("gn", [P, 2])
        wa, wb = sb("wa", [P, TAPS, P], F16), sb("wb", [P, TAPS, P], F16)
        got = [sb(f"got{k}", [P, C]) for k in range(TPI)]
        index = [sb(f"index{k}", [P, 1], U32) for k in range(TPI)]
        sq, rs, y, tf = (sb(n, [P, PIX]) for n in ("sq", "rs", "y", "tf"))
        ct = [sb(f"ct{q}", [P, PIX], F16) for q in range(2)]
        xv = [sb(f"xv{q}", [P, PAD, PAD]) for q in range(2)]
        pool_part = [sb(f"pool_part{k}", [P, SIDE, SIDE]) for k in range(POOL_TAPS)]
        own_part = [sb(f"own_part{k}", [P, SIDE, SIDE]) for k in range(2)]
        own_sum, pool_sum = sb("own_sum", [P, SIDE, SIDE]), sb("pool_sum", [P, SIDE, SIDE])
        t = sb("t", [P, 32])
        D = env.psum
        halves = [slice(0, HALF), slice(HALF, PIX)]
        grid = lambda ap: ap.rearrange("p (h w) -> p h w", w=SIDE)
        loads = [(wv[:, :], a["w_v"]), (w1[:, :], a["w1_d4"]), (gavg[:, :], a["k_groups"]), (w2[:, :, :], a["w2_taps"]),
                 (w2b[:, :], a["b2_taps"]), (gn[:, :], a["gn"])]
        block = ctx.enter_context(nc.Block())

        def images(engine, body):
            with by_two(engine, 0, IMAGES - 2) as n:
                for q in range(2):
                    body(n + q, q, True, True)
            body(IMAGES - 2, 0, True, False)
            body(IMAGES - 1, 1, False, False)

        @block.sync
        def _(sp):
            for dst, src in loads:
                sp.dma_start(dst, src).then_inc(S["w_loaded"], 16)

            with sp.Fori(FIRST_IMAGES, IMAGES) as n:
                sp.wait_ge(S["done"], n + 3)
                sp.dma_start(out[:, bass.ds(n * PIX, PIX)], image(X, n)).then_inc(S["sent"], 16)
            sp.wait_ge(S["sent"], 16 * (IMAGES - FIRST_IMAGES))

        @block.gpsimd
        def _(pool):
            pool.sem_inc(S["pool_summed"], POOL_TAPS)

            def gather(n, first=False):
                if not first:
                    pool.wait_ge(S["turned"], n)
                for k in range(TPI):
                    pool.tensor_copy(index[k][:, :], env.slot[:, bass.ds(n * TPI + k, 1)]).then_inc(S["index_ready"], 1)
                for k in range(TPI):
                    wait_apart(pool, S["index_ready"], n * TPI + k + 1, env.passed["pool"])
                    pool.indirect_dma_start(got[k][:, :], None, env.yg, bass.IndirectOffsetOnAxis(ap=index[k][:, :], axis=0))\
                        .then_inc(S["gathered"], 16)

            def body(n, q, ahead, turn):
                for k in range(POOL_TAPS):
                    pool.wait_ge(S["product_ready"], n * TAPS + k + 3)
                    if k == 0:
                        pool.wait_ge(S["done"], n + 2)
                    else:
                        pool.wait_ge(S["pool_summed"], n * POOL_TAPS + k + POOL_TAPS)
                    pool.tensor_tensor(pool_sum[:, :, :], grid(image(X, n)) if k == 0 else pool_sum[:, :, :],
                                       pool_part[k][:, :, :], ALU.add).then_inc(S["pool_summed"], 1)
                if turn:
                    gather(n + 2)

            gather(0, first=True)
            gather(1)
            images(pool, body)

        @block.tensor
        def _(pe):
            def turn(n):
                pe.wait_ge(S["gathered"], n * 16 * TPI + 16 * TPI)
                pe.wait_ge(S["relu_ready"], n + 1)
                for k in range(TPI):
                    mm = pe.transpose(D[0][:, k * P:(k + 1) * P], got[k][:, :], env.idf[:, :])
                mm.then_inc(S["turned"], 1)

            def product(dst, w, src, done):
                for h in halves:
                    mm = pe.matmul(dst[:, h], w, src[:, h], start=True, stop=True)
                mm.then_inc(done, 1)

            def center(n):
                pe.wait_ge(S["x_added"], n + 1)
                pe.wait_ge(S["coef_ready"], n + 1)
                product(D[1], env.cen[:, :], image(X, n), S["cent_ready"])

            def variance(n):
                pe.wait_ge(S["sq_ready"], n + 1)
                product(D[0], env.avg[:, :], sq[:, :], S["var_ready"])

            def project(n):
                pe.wait_ge(S["y_ready"], n + 2)
                product(D[0], w1[:, :], y[:, :], S["t_ready"])
                product(D[1], wv[:, :], y[:, :], S["v_ready"])

            def group(n):
                pe.wait_ge(S["e2_ready"], n + 1)
                pe.wait_ge(S["padded_ready"], n + 1)
                pe.matmul(D[1][:, 0:2], gavg[:, :], t[:, 0:2], start=True, stop=True).then_inc(S["group_ready"], 1)

            def tap(n, q, k):
                if k == 0:
                    pe.wait_ge(S["split_ready"], n + 2)
                pe.wait_ge(S["product_ready"], n * TAPS + k + 1)
                dst = D[2 + (q * TAPS + k) % 2]
                for h in halves:
                    pe.matmul(dst[:, h], wa[:, k, :], ct[q][:, h], start=True, stop=False)
                    mm = pe.matmul(dst[:, h], wb[:, k, :], ct[q][:, h], start=False, stop=True)
                mm.then_inc(S["tap_ready"], 1)

            def body(n, q, ahead, turn_next):
                for k in range(TAPS):
                    tap(n, q, k)
                    if ahead and k == 1:
                        center(n + 1)
                    if ahead and k == 2:
                        variance(n + 1)
                    if ahead and k == 5:
                        project(n + 1)
                    if ahead and k == 7:
                        group(n + 1)
                if turn_next:
                    turn(n + 2)

            pe.wait_ge(S["w_loaded"], 16 * len(loads))
            pe.wait_ge(S["w_ready"], 3)
            turn(0)
            center(0)
            variance(0)
            project(0)
            group(0)
            turn(1)
            images(pe, body)

        @block.scalar
        def _(act):
            act.preload_act_table_set("natural_log_exp_and_others")
            act.sem_inc(S["relu_ready"], 1)

            def norm(n):
                act.wait_ge(S["cent_ready"], n + 1)
                act.activation(sq[:, :], D[1][:, :], ACT.Square).then_inc(S["sq_ready"], 1)
                act.wait_ge(S["var_ready"], n + 1)
                act.wait_ge(S["y_ready"], n + 1)
                act.activation(rs[:, :], D[0][:, :], ACT.Ln, bias=env.eps[:, 0:1], scale=1.0).then_inc(S["ln_ready"], 1)
                act.wait_ge(S["ln_ready"], n + 1)
                act.activation(rs[:, :], rs[:, :], ACT.Exp, scale=-0.5).then_inc(S["rstd_ready"], 1)

            def values(n, q):
                act.wait_ge(S["v_ready"], n + 1)
                act.wait_ge(S["done"], n + 1)
                act.activation(xv[q][:, 1:1 + SIDE, 1:1 + SIDE], grid(D[1][:, :]), ACT.Copy).then_inc(S["padded_ready"], 1)

            def relu(n, q):
                act.wait_ge(S["gvar_ready"], n + 1)
                act.activation(t[:, 8:9], t[:, 7:8], ACT.Ln, bias=env.eps[:, 1:2], scale=1.0).then_inc(S["gln_ready"], 1)
                act.wait_ge(S["gln_ready"], n + 1)
                act.activation(t[:, 9:10], t[:, 8:9], ACT.Exp, scale=-0.5).then_inc(S["grstd_ready"], 1)
                act.wait_ge(S["coef_ready"], n + 2)
                act.wait_ge(S["split_ready"], n + 1)
                act.activation(tf[:, :], D[0][:, :], ACT.Relu, bias=t[:, 11:12], scale=t[:, 10:11])
                act.activation(ct[q][:, :], D[0][:, :], ACT.Relu, bias=t[:, 11:12], scale=t[:, 10:11]).then_inc(S["relu_ready"], 1)

            def stage_a(n, q):
                norm(n)
                values(n, q)
                relu(n, q)

            act.wait_ge(S["border"], 2)
            stage_a(0, 0)
            images(act, lambda n, q, ahead, turn: stage_a(n + 1, 1 - q) if ahead else None)

        @block.vector
        def _(dve):
            dve.sem_inc(S["coef_ready"], 1)
            dve.sem_inc(S["y_ready"], 1)
            dve.sem_inc(S["split_ready"], 1)
            dve.sem_inc(S["done"], 2)
            dve.sem_inc(S["product_ready"], 2)
            for q in range(2):
                dve.memset(xv[q][:, :, :], 0.0).then_inc(S["border"], 1)
            dve.wait_ge(S["w_loaded"], 16 * len(loads))
            dve.tensor_copy(wa[:, :, :], w2[:, :, :]).then_inc(S["w_ready"], 1)
            dve.memset(wb[64:128, :, :], 0.0).then_inc(S["w_ready"], 1)
            dve.wait_ge(S["w_ready"], 1)
            dve.tensor_tensor(wb[0:64, :, :], w2[0:64, :, :], wa[0:64, :, :], ALU.subtract).then_inc(S["w_ready"], 1)

            steps = STEPS_PER_IMAGE
            def step(n, k, ins):
                ins.then_inc(S["steps"], 1)
                wait_apart(dve, S["steps"], n * steps + k + 1, env.passed["dve"])

            def add_x(n):
                dve.wait_ge(S["turned"], n + 1)
                dve.tensor_tensor(image(X, n), D[0][:, :], image(X, n), ALU.add).then_inc(S["x_added"], 1)

            def norm(n):
                dve.wait_ge(S["rstd_ready"], n + 1)
                dve.tensor_tensor(y[:, :], D[1][:, :], rs[:, :], ALU.mult).then_inc(S["y_ready"], 1)

            def statistics(n):
                dve.wait_ge(S["t_ready"], n + 1)
                step(n, 0, dve.bn_stats(t[:, 12:18], D[0][:, halves[0]]))
                step(n, 1, dve.bn_stats(t[:, 18:24], D[0][:, halves[1]]))
                step(n, 2, dve.bn_aggr(t[:, 24:26], t[:, 12:24].rearrange("p (n s) -> p n s", s=6)))
                step(n, 3, dve.tensor_copy(t[:, 0:1], t[:, 24:25]))
                step(n, 4, dve.tensor_tensor(t[:, 2:3], t[:, 24:25], t[:, 24:25], ALU.mult))
                dve.tensor_tensor(t[:, 1:2], t[:, 2:3], t[:, 25:26], ALU.add).then_inc(S["e2_ready"], 1)

            def group_variance(n):
                dve.wait_ge(S["group_ready"], n + 1)
                step(n, 5, dve.tensor_copy(t[:, 4:6], D[1][:, 0:2]))
                step(n, 6, dve.tensor_tensor(t[:, 6:7], t[:, 4:5], t[:, 4:5], ALU.mult))
                dve.tensor_tensor(t[:, 7:8], t[:, 5:6], t[:, 6:7], ALU.subtract).then_inc(S["gvar_ready"], 1)

            def coefficients(n):
                dve.wait_ge(S["grstd_ready"], n + 1)
                step(n, 7, dve.tensor_tensor(t[:, 10:11], gn[:, 0:1], t[:, 9:10], ALU.mult))
                step(n, 8, dve.tensor_tensor(t[:, 6:7], t[:, 4:5], t[:, 10:11], ALU.mult))
                dve.tensor_tensor(t[:, 11:12], gn[:, 1:2], t[:, 6:7], ALU.subtract).then_inc(S["coef_ready"], 1)

            def split(n, q):
                dve.wait_ge(S["relu_ready"], n + 2)
                dve.tensor_tensor(ct[q][64:128, :], tf[64:128, :], ct[q][64:128, :], ALU.subtract).then_inc(S["split_ready"], 1)

            def product(n, q, k):
                dve.wait_ge(S["tap_ready"], n * TAPS + k + 1)
                if k == 0:
                    dve.wait_ge(S["padded_ready"], n + 1)
                dy, dx = divmod(k, 3)
                if k < POOL_TAPS:
                    dve.wait_ge(S["pool_summed"], n * POOL_TAPS + k + 1)
                    dst = pool_part[k]
                else:
                    dst = own_sum if k == POOL_TAPS else own_part[k % 2]
                    if k == POOL_TAPS:
                        dve.wait_ge(S["done"], n + 2)
                    if k > POOL_TAPS + 2:
                        dve.wait_ge(S["summed"], n * OWN_ADDS + k - POOL_TAPS - 2)
                dve.scalar_tensor_tensor(dst[:, :, :], grid(D[2 + (q * TAPS + k) % 2][:, :]), w2b[:, k:k + 1],
                                         xv[q][:, dy:dy + SIDE, dx:dx + SIDE], ALU.add, ALU.mult).then_inc(S["product_ready"], 1)

            def add(n, k):
                dve.wait_ge(S["product_ready"], n * TAPS + k + 3)
                if k > POOL_TAPS + 1:
                    dve.wait_ge(S["summed"], n * OWN_ADDS + k - POOL_TAPS - 1)
                dve.tensor_tensor(own_sum[:, :, :], own_sum[:, :, :], own_part[k % 2][:, :, :], ALU.add).then_inc(S["summed"], 1)

            def body(n, q, ahead, turn):
                if ahead:
                    add_x(n + 1)
                for k in range(TAPS):
                    product(n, q, k)
                    if k > POOL_TAPS + 1:
                        add(n, k - 1)
                    if ahead and k == 2:
                        norm(n + 1)
                    if ahead and k == 5:
                        statistics(n + 1)
                    if ahead and k == 6:
                        group_variance(n + 1)
                    if ahead and k == 7:
                        coefficients(n + 1)
                add(n, TAPS - 1)
                dve.wait_ge(S["summed"], n * OWN_ADDS + OWN_ADDS)
                dve.wait_ge(S["pool_summed"], n * POOL_TAPS + 2 * POOL_TAPS)
                dve.tensor_tensor(grid(image(X, n)), own_sum[:, :, :], pool_sum[:, :, :], ALU.add).then_inc(S["done"], 1)
                if ahead:
                    split(n + 1, 1 - q)

            add_x(0)
            norm(0)
            statistics(0)
            group_variance(0)
            coefficients(0)
            split(0, 0)
            images(dve, body)


def phase_experts1(nc, env, a, out):
    X = env.X
    with ExitStack() as ctx:
        names = ("w_loaded cleared cent_ready sq_ready var_ready ln_ready rs_ready xn_ready logits_ready ex_ready sel_ready "
                 "rank_ready ranked wg_ready a_ready b_ready wb_ready exp_ready softplus_ready sig_ready u_ready g_ready "
                 "h_ready wg_turned wt_ready down_done y_ready x_done steps ends_ready sent decided").split()
        S = {n: ctx.enter_context(nc.semaphore(f"e1_{n}")) for n in names}
        sb = lambda n, s, d=F32: ctx.enter_context(nc.sbuf_tensor(f"e1_{n}", s, d))
        w1, w3, w2 = (sb(n, [P, EP1, P]) for n in ("w1", "w3", "w2"))
        gate_w, gate_b = sb("gate_w", [P, E1]), sb("gate_b", [P, E1])
        before_mask = sb("before_mask", [P, G1, G1])
        sq, rs = sb("sq", [P, BLOCK]), sb("rs", [P, BLOCK])
        xn = [sb(f"xn{q}", [P, BLOCK]) for q in range(2)]
        wg, spreader = sb("wg", [P, BT, G1, 2]), sb("spreader", [P, EP1, P])
        wt = [sb(f"wt{q}", [P, BLOCK]) for q in range(2)]
        sig, u, h = ([sb(f"{n}{q}", [P, BLOCK]) for q in range(2)] for n in ("sig", "u", "h"))
        scores, biased, masked = (sb(n, [P, BT, G1, 2]) for n in ("scores", "biased", "masked"))
        group = sb("group", [P, BT, G1])
        above, tie = sb("above", [P, BT, G1, G1]), sb("tie", [P, BT, G1, G1])
        place, selected = sb("place", [P, BT, G1]), sb("selected", [P, BT, G1])
        sel = sb("sel", [P, BT, G1], BF16)
        keep, total, taken, taken_before = sb("keep", [P, BT, G1]), sb("total", [P, BT]), sb("taken", [P, G1]), sb("taken_before", [P, G1])
        least = sb("least", [1, 2])
        ends = sb("ends", [1, 3], I32)
        A = [env.psum[q][:, 0:HALF] for q in range(2)]
        B = [env.psum[q][:, HALF:PIX] for q in range(2)]
        wb, y = env.psum[2][:, 0:HALF], env.psum[2][:, HALF:PIX]
        cent, var = env.psum[3][:, 0:HALF], env.psum[3][:, HALF:PIX]
        logits = var[:, 0:BT * E1]
        rank = var[:, 64:64 + BT * G1].rearrange("p (s g) -> p s g", g=G1)
        tot = var[:, 96:96 + G1]
        loads = [(w1[:, :, :], a["w1_moe1"]), (w3[:, :, :], a["w3_moe1"]), (w2[:, :, :], a["w2_moe1"]),
                 (gate_w[:, :], a["gate_w"]), (gate_b[:, :], a["gate_b"].broadcast_to([P, E1])),
                 (spreader[:, :, :], a["k_spread"]),
                 (before_mask[:, :, :], a["k_before"].broadcast_to([P, G1, G1]))]
        block = ctx.enter_context(nc.Block())

        def cols(buf, n):
            return buf[:, bass.ds(n * BLOCK, BLOCK)]

        def blocks(engine, body, last=None):
            with engine.Fori(0, 2) as r:
                engine.wait_ge(S["ends_ready"], r + 1)
                end = engine.value_load(ends[0:1, bass.ds(r, 1)], min_val=FIRST_BLOCKS // 2, max_val=BLOCKS // 2)
                with engine.Fori(r * (FIRST_BLOCKS // 2), end) as i:
                    for q in range(2):
                        body(i * 2 + q, q)
                if last is not None:
                    last(r)

        @block.sync
        def _(sp):
            for dst, src in loads:
                sp.dma_start(dst, src).then_inc(S["w_loaded"], 16)

            def send(n, q):
                sp.wait_ge(S["x_done"], n + 2)
                sp.dma_start(cols(out, n), cols(X, n)).then_inc(S["sent"], 16)
                wait_apart(sp, S["sent"], n * 16 + 16, env.passed["sp"])
            blocks(sp, send)

        @block.tensor
        def _(pe):
            def center(n):
                pe.matmul(cent, env.cen[:, :], cols(X, n % BLOCKS), start=True, stop=True).then_inc(S["cent_ready"], 1)

            def variance(n):
                pe.wait_ge(S["sq_ready"], n + 1)
                pe.wait_ge(S["wt_ready"], n + 1)
                pe.matmul(var, env.avg[:, :], sq[:, :], start=True, stop=True).then_inc(S["var_ready"], 1)

            def gate(n, q):
                pe.wait_ge(S["xn_ready"], n + 1)
                for s in range(BT):
                    mm = pe.matmul(logits[:, s * E1:(s + 1) * E1], xn[q][:, s * P:(s + 1) * P], gate_w[:, :],
                                   start=True, stop=True)
                mm.then_inc(S["logits_ready"], 1)

            def ranks(n):
                pe.wait_ge(S["sel_ready"], n + 1)
                for s in range(BT):
                    for before in range(s):
                        pe.matmul(rank[:, s, :], env.ones16[:, :], sel[:, before, :], start=(before == 0), stop=False)
                    pe.matmul(rank[:, s, :], env.ltri[:, :], sel[:, s, :], start=(s == 0), stop=True)
                for s in range(BT):
                    mm = pe.matmul(tot, env.ones16[:, :], sel[:, s, :], start=(s == 0), stop=(s == BT - 1))
                mm.then_inc(S["rank_ready"], 1)

            def turn_weights(n):
                pe.wait_ge(S["wg_ready"], n + 1)
                for s in range(BT):
                    mm = pe.transpose(var[0:E1, s * P:(s + 1) * P], wg[:, s, :, :].rearrange("p g e -> p (g e)"), env.idf[:, :])
                mm.then_inc(S["wg_turned"], 1)

            def up(n, q, k):
                pe.wait_ge(S["h_ready"], n * EP1 + k + 1)
                if k == 0:
                    pe.wait_ge(S["xn_ready"], n + 1)
                pe.matmul(A[k % 2], w1[:, k, :], xn[q][:, :], start=True, stop=True).then_inc(S["a_ready"], 1)
                pe.matmul(B[k % 2], w3[:, k, :], xn[q][:, :], start=True, stop=True).then_inc(S["b_ready"], 1)

            def spread(n, q, k):
                if k == 0:
                    pe.wait_ge(S["wt_ready"], n + 2)
                pe.wait_ge(S["h_ready"], n * EP1 + k + 2)
                pe.matmul(wb, spreader[:, k, :], wt[q][:, :], start=True, stop=True).then_inc(S["wb_ready"], 1)

            def down(n, k):
                pe.wait_ge(S["h_ready"], n * EP1 + k + 3)
                if k == 0:
                    pe.wait_ge(S["x_done"], n + 1)
                mm = pe.matmul(y, w2[:, k, :], h[k % 2][:, :], start=(k == 0), stop=(k == EP1 - 1))
                mm.then_inc(S["down_done"], 1)

            def body(n, q):
                for k in range(EP1):
                    up(*((n, q, k + 1) if k + 1 < EP1 else (n + 1, 1 - q, 0)))
                    if k == 0:
                        center(n + 1)
                    if k == 1:
                        variance(n + 1)
                    if k == 3:
                        gate(n + 1, 1 - q)
                    if k == 5:
                        ranks(n + 1)
                    if k == 7:
                        turn_weights(n + 1)
                    down(n, k)
                    spread(*((n, q, k + 1) if k + 1 < EP1 else (n + 1, 1 - q, 0)))

            pe.wait_ge(S["w_loaded"], 16 * len(loads))
            center(0)
            variance(0)
            gate(0, 0)
            ranks(0)
            turn_weights(0)
            up(0, 0, 0)
            spread(0, 0, 0)
            blocks(pe, body)

        @block.scalar
        def _(act):
            act.preload_act_table_set("natural_log_exp_and_others")

            def square(n):
                act.wait_ge(S["cent_ready"], n + 1)
                act.activation(sq[:, :], cent, ACT.Square).then_inc(S["sq_ready"], 1)

            def rstd(n):
                act.wait_ge(S["var_ready"], n + 1)
                act.activation(rs[:, :], var, ACT.Ln, bias=env.eps[:, 1:2], scale=1.0).then_inc(S["ln_ready"], 1)
                act.wait_ge(S["ln_ready"], n + 1)
                act.activation(rs[:, :], rs[:, :], ACT.Exp, scale=-0.5).then_inc(S["rs_ready"], 1)

            def gate(n):
                act.wait_ge(S["logits_ready"], n + 1)
                act.wait_ge(S["ranked"], n + 1)
                act.activation(scores[:, :, :, :].rearrange("p s g e -> p (s g e)"), logits, ACT.Exp, scale=-1.0)\
                    .then_inc(S["ex_ready"], 1)

            def take_weights(n, q):
                act.wait_ge(S["wg_turned"], n + 1)
                act.activation(wt[q][0:E1, :], var[0:E1, :], ACT.Copy).then_inc(S["wt_ready"], 1)

            def sigmoid(n, k):
                j, s = n * EP1 + k + 1, sig[k % 2]
                act.wait_ge(S["a_ready"], j)
                act.activation(s[:, :], A[k % 2], ACT.Exp, scale=-1.0).then_inc(S["exp_ready"], 1)
                act.wait_ge(S["exp_ready"], j)
                act.activation(s[:, :], s[:, :], ACT.Ln, bias=env.ones32[:, 0:1], scale=1.0).then_inc(S["softplus_ready"], 1)
                act.wait_ge(S["softplus_ready"], j)
                act.activation(s[:, :], s[:, :], ACT.Exp, scale=-1.0).then_inc(S["sig_ready"], 1)

            def body(n, q):
                for k in range(EP1):
                    sigmoid(n, k)
                    if k == 1:
                        square(n + 1)
                    if k == 2:
                        rstd(n + 1)
                    if k == 4:
                        gate(n + 1)
                take_weights(n + 1, 1 - q)

            act.sem_inc(S["wt_ready"], 1)
            square(0)
            rstd(0)
            gate(0)
            act.wait_ge(S["cleared"], 2)
            take_weights(0, 0)
            blocks(act, body)

        @block.vector
        def _(dve):
            dve.sem_inc(S["ranked"], 1)
            dve.sem_inc(S["h_ready"], 2)
            dve.sem_inc(S["x_done"], 1)
            dve.sem_inc(S["down_done"], 2)
            wide = lambda ap: ap.unsqueeze(3).broadcast_to([P, BT, G1, 2])

            def step(n, k, ins):
                ins.then_inc(S["steps"], 1)
                dve.wait_ge(S["steps"], n * STEPS1 + k + 1)

            def norm(n, q):
                dve.wait_ge(S["rs_ready"], n + 1)
                dve.tensor_tensor(xn[q][:, :], cent, rs[:, :], ALU.mult).then_inc(S["xn_ready"], 1)

            def select(n):
                dve.wait_ge(S["ex_ready"], n + 1)
                f = lambda t: t[:, :, :, :].rearrange("p s g e -> p (s g e)")
                step(n, 0, dve.tensor_scalar(f(scores), f(scores), 1.0, None, ALU.add))
                step(n, 1, dve.reciprocal(f(scores), f(scores)))
                step(n, 2, dve.tensor_tensor(biased[:, :, :, :].rearrange("p s g e -> p s (g e)"),
                                             scores[:, :, :, :].rearrange("p s g e -> p s (g e)"),
                                             gate_b[:, :].unsqueeze(1).broadcast_to([P, BT, E1]), ALU.add))
                step(n, 3, dve.tensor_tensor(group[:, :, :], biased[:, :, :, 0], biased[:, :, :, 1], ALU.add))
                own = group[:, :, :].unsqueeze(3).broadcast_to([P, BT, G1, G1])
                other = group[:, :, :].unsqueeze(2).broadcast_to([P, BT, G1, G1])
                step(n, 4, dve.tensor_tensor(above[:, :, :, :], other, own, ALU.is_gt))
                step(n, 5, dve.tensor_tensor(tie[:, :, :, :], other, own, ALU.is_equal))
                flat = lambda t: t[:, :, :, :].rearrange("p s g h -> p s (g h)")
                step(n, 6, dve.tensor_tensor(flat(tie), flat(tie), before_mask[:, :, :].rearrange("p g h -> p (g h)")
                                             .unsqueeze(1).broadcast_to([P, BT, G1 * G1]), ALU.mult))
                step(n, 7, dve.tensor_tensor(flat(above), flat(above), flat(tie), ALU.add))
                step(n, 8, dve.tensor_reduce(place[:, :, :], above[:, :, :, :], AX.X, ALU.add))
                step(n, 9, dve.tensor_scalar(selected[:, :, :], place[:, :, :], float(TOP_G), None, ALU.is_lt))
                dve.tensor_copy(sel[:, :, :], selected[:, :, :]).then_inc(S["sel_ready"], 1)

            def weigh(n):
                step(n, 10, dve.tensor_tensor(masked[:, :, :, :], scores[:, :, :, :], wide(selected[:, :, :]), ALU.mult))
                step(n, 11, dve.tensor_reduce(total[:, :], masked[:, :, :, :].rearrange("p s g e -> p s (g e)"), AX.X, ALU.add))
                step(n, 12, dve.reciprocal(total[:, :], total[:, :]))
                step(n, 13, dve.tensor_scalar(total[:, :], total[:, :], SCALE1, None, ALU.mult))
                dve.wait_ge(S["rank_ready"], n + 1)
                step(n, 14, dve.tensor_tensor(keep[:, :, :], rank, taken[:, :].unsqueeze(1).broadcast_to([P, BT, G1]), ALU.add))
                step(n, 15, dve.tensor_copy(taken_before[:, :], taken[:, :]))
                step(n, 16, dve.tensor_tensor(taken[:, :], taken[:, :], tot, ALU.add))
                step(n, 17, dve.tensor_scalar(keep[:, :, :], keep[:, :, :], float(CAP), None, ALU.is_lt))
                step(n, 18, dve.tensor_tensor(keep[:, :, :], keep[:, :, :], total[:, :].unsqueeze(2).broadcast_to([P, BT, G1]), ALU.mult))
                dve.tensor_tensor(wg[:, :, :, :], masked[:, :, :, :], wide(keep[:, :, :]), ALU.mult).then_inc(S["wg_ready"], 1)
                dve.sem_inc(S["ranked"], 1)

            def pair(n, k):
                j, q = n * EP1 + k + 1, k % 2
                dve.wait_ge(S["sig_ready"], j)
                dve.tensor_tensor(u[q][:, :], sig[q][:, :], A[q], ALU.mult).then_inc(S["u_ready"], 1)
                dve.wait_ge(S["u_ready"], j)
                dve.wait_ge(S["b_ready"], j)
                dve.tensor_tensor(u[q][:, :], u[q][:, :], B[q], ALU.mult).then_inc(S["g_ready"], 1)
                dve.wait_ge(S["g_ready"], j)
                dve.wait_ge(S["wb_ready"], j)
                dve.wait_ge(S["down_done"], j)
                dve.tensor_tensor(h[q][:, :], u[q][:, :], wb, ALU.mult).then_inc(S["h_ready"], 1)

            def body(n, q):
                for k in range(EP1):
                    pair(n, k)
                    if k == 2:
                        norm(n + 1, 1 - q)
                    if k == 4:
                        select(n + 1)
                    if k == 6:
                        weigh(n + 1)
                dve.wait_ge(S["down_done"], n * EP1 + EP1 + 2)
                dve.tensor_tensor(cols(X, n), cols(X, n), y, ALU.add).then_inc(S["x_done"], 1)

            def decide(r):
                room = lambda j, ins: (ins.then_inc(S["decided"], 1), dve.wait_ge(S["decided"], r * 2 + j))
                room(2, dve.tensor_reduce(least[0:1, 0:1], taken_before[0:1, :], AX.X, ALU.min))
                room(3, dve.tensor_scalar(least[0:1, 1:2], least[0:1, 0:1], float(CAP), float((BLOCKS - FIRST_BLOCKS) // 2),
                                          ALU.is_lt, ALU.mult))
                dve.tensor_scalar(ends[0:1, bass.ds(r + 1, 1)], least[0:1, 1:2], float(FIRST_BLOCKS // 2), None, ALU.add)\
                    .then_inc(S["ends_ready"], 1)

            for q in range(2):
                dve.memset(wt[q][:, :], 0.0).then_inc(S["cleared"], 1)
            dve.memset(taken[:, :], 0.0).then_inc(S["decided"], 1)
            dve.wait_ge(S["decided"], 1)
            dve.wait_ge(S["w_loaded"], 16 * len(loads))
            norm(0, 0)
            select(0)
            weigh(0)
            dve.memset(ends[0:1, 0:1], FIRST_BLOCKS // 2).then_inc(S["ends_ready"], 1)
            blocks(dve, body, last=decide)


class Env:
    pass


def build(nc, a, out):
    env = Env()
    with ExitStack() as ctx:
        sb = lambda n, s, d=F32: ctx.enter_context(nc.sbuf_tensor(n, s, d))
        env.X = sb("X", [P, TOKENS])
        env.cen, env.avg, env.idf, env.ltri32 = sb("cen", [P, P]), sb("avg", [P, P]), sb("idf", [P, P]), sb("ltri32", [P, P])
        env.ltri, env.ones16, env.idb = sb("ltri", [P, P], BF16), sb("ones16", [P, P], BF16), sb("idb", [P, P], BF16)
        env.ones32 = sb("ones32", [P, 1])
        env.small = sb("small", [P, SMALL])
        env.mask_group = env.small[:, 0:16]
        env.rev = env.small[:, 16:24]
        env.pair_no = env.small[:, 24:24 + PAIRS]
        env.lane = env.small[:, 52:53]
        env.par, env.eps = sb("par", [P, 9]), sb("eps", [P, 3])
        env.slot, env.starts = sb("slot", [P, TILES], I32), sb("starts", [1, PAIRS + 2], I32)
        env.zero = sb("zero_row", [P, ROW])
        env.passed = {name: ctx.enter_context(nc.semaphore(f"passed_{name}")) for name in ("pool", "pe", "sp", "dve")}
        env.cleared = ctx.enter_context(nc.semaphore("rows_cleared"))
        env.bnst = sb("bnst", [P, IMAGES * 12])
        env.psum = [ctx.enter_context(nc.psum_tensor(f"ps{i}", [P, 2 * HALF], F32)) for i in range(4)]
        xg = nc.dram_tensor("dispatched", (CLEARED, ROW), F32, kind="Internal").ap()
        yg = nc.dram_tensor("expert_out", ((MAX_TILES + 1) * SLOT, C), F32, kind="Internal").ap()
        env.xg, env.yg = xg, yg
        setup_constants(nc, env, a)
        with ExitStack() as first:
            sb1 = lambda n, s, d=F32: first.enter_context(nc.sbuf_tensor(n, s, d))
            env.Y = sb1("Y", [P, TOKENS])
            env.rstd, env.shift, env.gates = sb1("rstd", [P, TILES]), sb1("shift", [P, TILES]), sb1("gates", [P, 2 * TILES])
            env.logit, env.rowst = sb1("logit", [P, TILES * E0]), sb1("rowst", [P, TILES * 6])
            phase_norm0(nc, env, a, xg)
            with nc.sbuf_tensor("CONV", [P, TOKENS], BF16) as CONV:
                env.CONV = CONV
                phase_conv(nc, env, a)
                phase_tokens0(nc, env, a)
            phase_route0(nc, env)
            phase_dispatch(nc, env)
        with ExitStack() as second:
            sb2 = lambda n, s, d=F32: second.enter_context(nc.sbuf_tensor(n, s, d))
            env.weights = sb2("weights", [P, E0 * WCOLS], F16)
            split_weights0(nc, env, a)
            phase_experts0(nc, env, a)
        phase_involution(nc, env, a, out)
        phase_experts1(nc, env, a, out)


SMALL = 53


def constants():
    small = np.zeros((P, SMALL), np.float32)
    small[np.arange(P), np.arange(P) // GROUP_IN] = 1.0
    small[:, 16:24] = E0 - np.arange(E0)
    small[:, 24:24 + PAIRS] = np.arange(PAIRS)
    small[:, 52] = np.arange(P)
    return {
        "k_center": np.eye(P, dtype=np.float32) - np.float32(1 / C),
        "k_average": np.full((P, P), 1 / C, np.float32),
        "k_identity": np.eye(P, dtype=np.float32),
        "k_lower": np.triu(np.ones((P, P), np.float32), 1),
        "k_small": small,
        "k_groups": np.where((np.arange(P)[:, None] < 64) & (np.arange(P)[:, None] // G8 == np.arange(P)[None, :] % 64 // G8),
                             np.float32(1 / G8), np.float32(0)),
        "k_before": np.tril(np.ones((G1, G1), np.float32), -1).reshape(1, G1, G1),
        "k_spread": (np.arange(P)[:, None, None] == 2 * np.arange(EP1)[None, :, None] + np.arange(P)[None, None, :] // M1)
                    .astype(np.float32),
        "k_pairs": np.array(PAIR_LIST + PAIR_LIST[-1:], np.int32).reshape(1, 2 * PAIRS + 2),
    }


def layout(i):
    i = {k: np.asarray(v) for k, v in i.items()}
    a = dict(constants())
    a["x"] = i["x"].transpose(1, 0, 2, 3).reshape(C, IMAGES, PIX)
    a["chan"] = np.stack([i["L0_conv_bn1_gamma"], i["L0_conv_bn1_beta"], i["L0_conv_bn2_gamma"],
                          i["L0_conv_bn2_beta"], i["L0_conv_prelu_a"]], axis=1)
    a["conv_w"] = i["L0_conv_conv_w"].reshape(C, GROUP_IN * TAPS)
    a["w_router"] = i["L0_ffn_W_router"]
    w1 = i["L0_ffn_W1"]
    w2 = i["L0_ffn_W2"].reshape(E0, KM, P, C).transpose(0, 2, 1, 3).reshape(E0, P, H0)
    a["w_moe0"] = np.concatenate([w1, w2], axis=2)
    a["b1"] = i["L0_ffn_b1"].reshape(E0, KM, P).transpose(2, 0, 1).reshape(P, E0 * KM)
    a["b2"] = i["L0_ffn_b2"].reshape(1, E0 * C)
    d4 = lambda w: w[:, :, np.array(PERMS)].transpose(1, 3, 0, 2).reshape(C, -1)
    a["w_v"] = d4(i["L1_conv_w_v"])
    a["w1_d4"] = np.concatenate([d4(i["L1_conv_w1"])] * 2, axis=1)
    a["gn"] = np.concatenate([np.stack([i["L1_conv_gn_gamma"], i["L1_conv_gn_beta"]], axis=1)] * 2)
    base = np.arange(TAPS).reshape(3, 3)
    source = np.stack([base, np.rot90(base, 1), np.rot90(base, 2), np.rot90(base, 3), np.rot90(base.T, 3),
                       np.rot90(base.T, 2), np.rot90(base.T, 1), base.T]).reshape(G8, TAPS)
    w2 = np.zeros((2, CMID, G8, TAPS, C // G8, G8), np.float32)
    for g in range(G8):
        w2[:, :, g, :, :, g] = i["L1_conv_w2"][source[g]].T[None, :, :, None]
    a["w2_taps"] = w2.reshape(P, TAPS, P)
    a["b2_taps"] = np.tile(i["L1_conv_b2"][source], (C // G8, 1))
    a["w1_moe1"] = i["L1_ffn_w1"].transpose(1, 0, 2).reshape(P, EP1, P)
    a["w3_moe1"] = i["L1_ffn_w3"].transpose(1, 0, 2).reshape(P, EP1, P)
    a["w2_moe1"] = i["L1_ffn_w2"].reshape(EP1, P, C).transpose(1, 0, 2)
    a["gate_w"] = i["L1_ffn_gate_w"].T
    a["gate_b"] = i["L1_ffn_gate_b"].reshape(1, E1)
    return {k: np.ascontiguousarray(v) for k, v in a.items()}


def kernel(**inputs):
    import concourse.bacc as bacc
    from concourse.bass_utils import run_bass_kernel_spmd
    arrays = layout(inputs)
    nc = bacc.Bacc("TRN2", target_bir_lowering=False, num_devices=1)
    a = {name: nc.dram_tensor(name, value.shape, mybir.dt.from_np(value.dtype), kind="ExternalInput").ap()
         for name, value in arrays.items()}
    out = nc.dram_tensor("out", (P, TOKENS), F32, kind="ExternalOutput").ap()
    build(nc, a, out)
    result = run_bass_kernel_spmd(nc, [arrays], core_ids=[0])
    return result.results[0]["out"].reshape(C, IMAGES, SIDE, SIDE).transpose(1, 0, 2, 3)
```

```python
from contextlib import ExitStack, contextmanager

import numpy as np

import concourse.bass as bass
from concourse import mybir
from concourse.alu_op_type import AluOpType as ALU

ACT = mybir.ActivationFunctionType
AX = mybir.AxisListType
F32, F16, BF16 = mybir.dt.float32, mybir.dt.float16, mybir.dt.bfloat16
I32, U32 = mybir.dt.int32, mybir.dt.uint32

IMAGES, C, SIDE = 16, 128, 32
PIX = SIDE * SIDE
TOKENS = IMAGES * PIX
HALF = 512
P = 128
TILES = TOKENS // P
FLIGHT = 4
TPI = PIX // P
PAD = SIDE + 2
GROUP_IN = 8
TAPS = 9
E0, H0 = 8, 512
KM = H0 // P
PAIRS = E0 * (E0 - 1) // 2
SLOT = 256
SUB = SLOT // P
MAX_TILES = TOKENS // SLOT + PAIRS
ROW = C + 2
CMID, G8 = 8, 8
E1, M1, CAP = 16, 64, 256
EP1 = E1 // 2
TOP_G = 4
SCALE1 = 2.5
G1 = 8
BLOCK = 512
BT, BLOCKS = BLOCK // P, TOKENS // BLOCK
FIRST_BLOCKS = 4
FIRST_IMAGES = FIRST_BLOCKS * BLOCK // PIX
STEPS1 = 19
WSCALE = 32.0
POOL_TAPS = 4
OWN_ADDS = TAPS - POOL_TAPS - 1
STEPS_PER_IMAGE = 5
WCOLS = 4 * H0 + C + 2 * KM
EPS_C, EPS = 1e-6, 1e-5
CLEARED = (MAX_TILES + 2) * SLOT
CLEARS = 4
PERMS = ((0, 1, 2, 3, 4, 5, 6, 7), (3, 0, 1, 2, 5, 6, 7, 4), (2, 3, 0, 1, 6, 7, 4, 5), (1, 2, 3, 0, 7, 4, 5, 6),
         (4, 5, 6, 7, 0, 1, 2, 3), (5, 6, 7, 4, 3, 0, 1, 2), (6, 7, 4, 5, 2, 3, 0, 1), (7, 4, 5, 6, 1, 2, 3, 0))
PAIR_LIST = [(a, b) for a in range(E0) for b in range(a + 1, E0)]


@contextmanager
def by_two(engine, start, end):
    with engine.Fori(start // 2, end // 2) as i:
        yield i * 2


def wait_apart(engine, sem, value, passed):
    engine.wait_ge(sem, value)
    engine.sem_inc(passed, 1)


def image(buf, n):
    return buf[:, bass.ds(n * PIX, PIX)]


def setup_constants(nc, env, a):
    with ExitStack() as ctx:
        got = ctx.enter_context(nc.semaphore("const_loaded"))
        cast = ctx.enter_context(nc.semaphore("const_cast"))
        block = ctx.enter_context(nc.Block())
        loads = [(env.cen[:, :], a["k_center"]), (env.avg[:, :], a["k_average"]), (env.idf[:, :], a["k_identity"]),
                 (env.small[:, :], a["k_small"]), (env.par[:, 0:5], a["chan"]),
                 (env.ltri32[:, :], a["k_lower"])]

        @block.sync
        def _(sp):
            for dst, src in loads:
                sp.dma_start(dst, src).then_inc(got, 16)

        @block.vector
        def _(dve):
            dve.wait_ge(got, 16 * len(loads))
            dve.tensor_copy(env.ltri[:, :], env.ltri32[:, :]).then_inc(cast, 1)
            dve.memset(env.ones16[:, :], 1.0).then_inc(cast, 1)
            dve.tensor_copy(env.idb[:, :], env.idf[:, :]).then_inc(cast, 1)
            dve.memset(env.eps[:, 0:1], EPS_C).then_inc(cast, 1)
            dve.memset(env.eps[:, 1:2], EPS).then_inc(cast, 1)
            dve.memset(env.eps[:, 2:3], 0.0).then_inc(cast, 1)
            dve.memset(env.ones32[:, :], 1.0).then_inc(cast, 1)
            dve.wait_ge(cast, 7)


def chain(engine, sem):
    count = [0]

    def link(instruction):
        count[0] += 1
        instruction.then_inc(sem, 1)
        engine.wait_ge(sem, count[0])
    return link


def phase_norm0(nc, env, a, zero_rows):
    X, Y = env.X, env.Y
    with ExitStack() as ctx:
        sem = lambda n: ctx.enter_context(nc.semaphore(n))
        loaded = [sem(f"n0_loaded{q}") for q in range(2)]
        cent_ready, sq_ready, var_ready = sem("n0_cent_ready"), sem("n0_sq_ready"), sem("n0_var_ready")
        ln_ready, rstd_ready, norm_free = sem("n0_ln_ready"), sem("n0_rstd_ready"), sem("n0_norm_free")
        sq_free = sem("n0_sq_free")
        zeroed, stats = sem("n0_zeroed"), sem("n0_stats")
        sq = [ctx.enter_context(nc.sbuf_tensor(f"n0_sq{q}", [P, PIX], F32)) for q in range(2)]
        rs = [ctx.enter_context(nc.sbuf_tensor(f"n0_rs{q}", [P, PIX], F32)) for q in range(2)]
        cent, var = env.psum[0:2], env.psum[2:4]
        block = ctx.enter_context(nc.Block())

        @block.sync
        def _(sp):
            for q in range(2):
                sp.dma_start(image(X, q), a["x"][:, q, :]).then_inc(loaded[q], 16)
            with by_two(sp, 2, IMAGES) as n:
                for q in range(2):
                    sp.wait_ge(loaded[q], n * 8)
                    sp.dma_start(image(X, n + q), a["x"][:, bass.ds(n + q, 1), :]).then_inc(loaded[q], 16)

        @block.gpsimd
        def _(pool):
            pool.memset(env.zero[:, :], 0.0).then_inc(zeroed, 1)
            pool.wait_ge(zeroed, 1)
            rows = CLEARED // P // CLEARS
            for q in range(2):
                pool.wait_ge(loaded[q], IMAGES * 8)
            for i in range(CLEARS):
                pool.dma_start(zero_rows[i * P * rows:(i + 1) * P * rows, :].rearrange("(p r) c -> p r c", p=P),
                               env.zero[:, :].unsqueeze(1).broadcast_to([P, rows, ROW])).then_inc(env.cleared, 16)

        @block.tensor
        def _(pe):
            def center(n, q):
                pe.wait_ge(loaded[q], (n - q) * 8 + 16)
                pe.wait_ge(norm_free, n + 1)
                for h in range(2):
                    mm = pe.matmul(cent[q][:, h * HALF:(h + 1) * HALF], env.cen[:, :],
                                   X[:, bass.ds(n * PIX + h * HALF, HALF)], start=True, stop=True)
                mm.then_inc(cent_ready, 1)

            def variance(n, q):
                pe.wait_ge(sq_ready, n + 1)
                for h in range(2):
                    mm = pe.matmul(var[q][:, h * HALF:(h + 1) * HALF], env.avg[:, :],
                                   sq[q][:, h * HALF:(h + 1) * HALF], start=True, stop=True)
                mm.then_inc(var_ready, 1)

            center(0, 0)
            center(1, 1)
            variance(0, 0)
            with by_two(pe, 0, IMAGES - 2) as n:
                for q in range(2):
                    variance(n + q + 1, 1 - q)
                    center(n + q + 2, q)
            variance(IMAGES - 1, 1)

        @block.scalar
        def _(act):
            def square(n, q):
                act.wait_ge(cent_ready, n + 1)
                act.activation(sq[q][:, :], cent[q][:, :], ACT.Square).then_inc(sq_ready, 1)

            def rstd(n, q):
                act.wait_ge(var_ready, n + 1)
                act.wait_ge(norm_free, n + 1)
                act.activation(rs[q][:, :], var[q][:, :], ACT.Ln, bias=env.eps[:, 0:1], scale=1.0).then_inc(ln_ready, 1)
                act.wait_ge(ln_ready, n + 1)
                act.activation(rs[q][:, :], rs[q][:, :], ACT.Exp, scale=-0.5).then_inc(rstd_ready, 1)

            act.preload_act_table_set("natural_log_exp_and_others")
            square(0, 0)
            square(1, 1)
            rstd(0, 0)
            with by_two(act, 0, IMAGES - 2) as n:
                for q in range(2):
                    rstd(n + q + 1, 1 - q)
                    square(n + q + 2, q)
            rstd(IMAGES - 1, 1)

        @block.vector
        def _(dve):
            dve.sem_inc(norm_free, 2)
            with by_two(dve, 0, IMAGES) as n:
                for q in range(2):
                    dve.wait_ge(rstd_ready, n + q + 1)
                    dve.tensor_tensor(image(Y, n + q), cent[q][:, :], rs[q][:, :], ALU.mult).then_inc(norm_free, 1)
                    dve.wait_ge(norm_free, n + q + 3)
                    for h in range(2):
                        dve.bn_stats(env.bnst[:, bass.ds((n + q) * 12 + h * 6, 6)],
                                     Y[:, bass.ds((n + q) * PIX + h * HALF, HALF)]).then_inc(stats, 1)
            dve.wait_ge(stats, 2 * IMAGES)


def phase_conv(nc, env, a):
    Y, CONV, par = env.Y, env.CONV, env.par
    with ExitStack() as ctx:
        sem = lambda n: ctx.enter_context(nc.semaphore(n))
        sb = lambda n, s, d=F32: ctx.enter_context(nc.sbuf_tensor(n, s, d))
        w_loaded, w_sign, w_spread, w_turned, w_ready = (sem(f"cv_w_{x}") for x in ("loaded", "sign", "spread", "turned", "ready"))
        var1, rs1, coef1, border = sem("cv_var1"), sem("cv_rs1"), sem("cv_coef1"), sem("cv_border")
        sign_ready, conv_ready, evac_free, stats, steps, asteps = (sem(f"cv_{x}") for x in
            ("sign_ready", "conv_ready", "evac_free", "stats", "steps", "asteps"))
        var2, rs2 = sem("cv_var2"), sem("cv_rs2")
        cw, sg, dev, mag = sb("cv_w", [P, GROUP_IN * TAPS]), sb("cv_sg", [P, GROUP_IN * TAPS]), sb("cv_dev", [P, GROUP_IN * TAPS]), sb("cv_mag", [P, GROUP_IN * TAPS])
        spread = sb("cv_spread", [P, TAPS, P], BF16)
        taps = sb("cv_taps", [P, TAPS, P], BF16)
        t = sb("cv_t", [P, 24])
        padded = [sb(f"cv_padded{q}", [P, PAD, PAD], BF16) for q in range(2)]
        col = lambda k: t[:, k:k + 1]
        mean1, vari1, lnv1, rstd1 = col(0), col(1), col(2), col(3)
        wsum, wmean, wss, wabs, wln, wrs, sw = (col(k) for k in range(4, 11))
        mean2, vari2, sv, lnv2, rstd2, tmp = (col(k) for k in range(12, 18))
        A1, B1 = par[:, 5:6], par[:, 6:7]
        A2, B2 = par[:, 7:8], par[:, 8:9]
        g1, b1, g2, b2 = (par[:, k:k + 1] for k in range(4))
        block = ctx.enter_context(nc.Block())

        @block.sync
        def _(sp):
            sp.dma_start(cw[:, :], a["conv_w"]).then_inc(w_loaded, 16)

        @block.vector
        def _(dve):
            link = chain(dve, steps)
            for q in range(2):
                dve.memset(padded[q][:, :, :], 0.0).then_inc(border, 1)
            dve.bn_aggr(t[:, 0:2], env.bnst[:, :].rearrange("p (n s) -> p n s", s=6)).then_inc(var1, 1)
            dve.wait_ge(w_loaded, 16)
            n = GROUP_IN * TAPS
            link(dve.reduce_sum(wsum, cw[:, :], AX.X))
            link(dve.tensor_scalar(wmean, wsum, 1.0 / n, None, ALU.mult))
            link(dve.tensor_scalar(dev[:, :], cw[:, :], wmean, None, ALU.subtract))
            link(dve.tensor_tensor(mag[:, :], dev[:, :], dev[:, :], ALU.mult))
            link(dve.reduce_sum(wss, mag[:, :], AX.X))
            link(dve.scalar_tensor_tensor(mag[:, :], dev[:, :], -1.0, dev[:, :], ALU.mult, ALU.max))
            link(dve.reduce_sum(wabs, mag[:, :], AX.X))
            dve.wait_ge(w_sign, 1)
            for k in range(TAPS):
                dve.tensor_tensor(
                    spread[:, k, :].rearrange("p (g i) -> p g i", i=GROUP_IN),
                    sg[:, :].rearrange("p (i k) -> p k i", k=TAPS)[:, k:k + 1, :].broadcast_to([P, C // GROUP_IN, GROUP_IN]),
                    env.mask_group[:, :].unsqueeze(2).broadcast_to([P, C // GROUP_IN, GROUP_IN]),
                    ALU.mult).then_inc(w_spread, 1)
            dve.wait_ge(rs1, 1)
            link(dve.tensor_tensor(A1, g1, rstd1, ALU.mult))
            link(dve.tensor_tensor(tmp, mean1, A1, ALU.mult))
            dve.tensor_tensor(B1, b1, tmp, ALU.subtract).then_inc(coef1, 1)
            dve.wait_ge(rs1, 2)
            link(dve.tensor_scalar(wrs, wrs, wabs, 1.0 / n, ALU.mult, ALU.mult))
            for half in range(2):
                dve.wait_ge(w_turned, half + 1)
                k0, k1 = (0, 8) if half == 0 else (8, TAPS)
                dve.tensor_copy(taps[:, k0:k1, :], env.psum[half][:, 0:(k1 - k0) * P]
                                .rearrange("p (k o) -> p k o", o=P)).then_inc(w_ready, 1)
            with dve.Fori(0, IMAGES) as n_:
                dve.wait_ge(evac_free, n_ + 3)
                for h in range(2):
                    dve.bn_stats(env.bnst[:, bass.ds(n_ * 12 + h * 6, 6)],
                                 CONV[:, bass.ds(n_ * PIX + h * HALF, HALF)]).then_inc(stats, 1)
            dve.wait_ge(stats, 2 * IMAGES)
            link(dve.bn_aggr(t[:, 12:14], env.bnst[:, :].rearrange("p (n s) -> p n s", s=6)))
            link(dve.tensor_tensor(sv, vari2, wrs, ALU.mult))
            dve.tensor_tensor(sv, sv, wrs, ALU.mult).then_inc(var2, 1)
            dve.wait_ge(rs2, 1)
            link(dve.tensor_tensor(tmp, g2, wrs, ALU.mult))
            link(dve.tensor_tensor(A2, tmp, rstd2, ALU.mult))
            link(dve.tensor_tensor(tmp, mean2, A2, ALU.mult))
            link(dve.tensor_tensor(B2, b2, tmp, ALU.subtract))

        @block.scalar
        def _(act):
            link = chain(act, asteps)
            act.preload_act_table_set("natural_log_exp_and_others")
            act.sem_inc(evac_free, 2)
            act.wait_ge(w_loaded, 16)
            act.activation(sg[:, :], cw[:, :], ACT.Sign).then_inc(w_sign, 1)
            act.wait_ge(var1, 1)
            link(act.activation(lnv1, vari1, ACT.Ln, bias=env.eps[:, 1:2], scale=1.0))
            act.activation(rstd1, lnv1, ACT.Exp, scale=-0.5).then_inc(rs1, 1)
            act.wait_ge(steps, 7)
            link(act.activation(wln, wss, ACT.Ln, scale=1.0 / (GROUP_IN * TAPS - 1)))
            act.activation(wrs, wln, ACT.Exp, scale=-0.5).then_inc(rs1, 1)
            act.wait_ge(coef1, 1)
            act.wait_ge(border, 2)

            def sign(n, q):
                act.wait_ge(evac_free, n + 1)
                act.activation(padded[q][:, 1:1 + SIDE, 1:1 + SIDE],
                               image(Y, n).rearrange("p (h w) -> p h w", w=SIDE), ACT.Sign, bias=B1, scale=A1)\
                   .then_inc(sign_ready, 1)

            def evacuate(n, q):
                act.wait_ge(conv_ready, n + 1)
                act.activation(image(CONV, n), env.psum[2 + q][:, :], ACT.Copy).then_inc(evac_free, 1)

            sign(0, 0)
            with by_two(act, 0, IMAGES - 2) as n:
                for q in range(2):
                    sign(n + q + 1, 1 - q)
                    evacuate(n + q, q)
            sign(IMAGES - 1, 1)
            evacuate(IMAGES - 2, 0)
            evacuate(IMAGES - 1, 1)
            act.wait_ge(var2, 1)
            link(act.activation(lnv2, sv, ACT.Ln, bias=env.eps[:, 1:2], scale=1.0))
            act.activation(rstd2, lnv2, ACT.Exp, scale=-0.5).then_inc(rs2, 1)

        @block.tensor
        def _(pe):
            pe.wait_ge(w_spread, TAPS)
            for k in range(TAPS):
                mm = pe.matmul(env.psum[k // 8][:, (k % 8) * P:(k % 8 + 1) * P], spread[:, k, :], env.idb[:, :],
                               start=True, stop=True)
                if k in (7, TAPS - 1):
                    mm.then_inc(w_turned, 1)
            pe.wait_ge(w_ready, 2)
            with by_two(pe, 0, IMAGES) as n:
                for q in range(2):
                    pe.wait_ge(sign_ready, n + q + 1)
                    pe.wait_ge(evac_free, n + q + 1)
                    for h in range(2):
                        for k in range(TAPS):
                            dy, dx = divmod(k, 3)
                            mm = pe.matmul(env.psum[2 + q][:, h * HALF:(h + 1) * HALF], taps[:, k, :],
                                           padded[q][:, h * 16 + dy:h * 16 + dy + 16, dx:dx + SIDE],
                                           start=(k == 0), stop=(k == TAPS - 1))
                    mm.then_inc(conv_ready, 1)


def phase_tokens0(nc, env, a):
    X, Y, CONV, par = env.X, env.Y, env.CONV, env.par
    with ExitStack() as ctx:
        sem = lambda n: ctx.enter_context(nc.semaphore(n))
        sb = lambda n, s, d=F32: ctx.enter_context(nc.sbuf_tensor(n, s, d))
        wr_loaded, wr_turned, wr_ready, coef = sem("t0_wr_loaded"), sem("t0_wr_turned"), sem("t0_wr_ready"), sem("t0_coef")
        sum_ready, act_ready, half_ready, x_ready = sem("t0_sum_ready"), sem("t0_act_ready"), sem("t0_half_ready"), sem("t0_x_ready")
        rows_free, kept_free, copied_free, stats_free = (sem(f"t0_{x}_free") for x in ("rows", "kept", "copied", "stats"))
        negs = sb("t0_negs", [P, 2])
        negB2, negalpha = negs[:, 0:1], negs[:, 1:2]
        wr, wc = sb("t0_wr", [P, E0]), sb("t0_wc", [P, E0])
        u = [sb(f"t0_u{k}", [P, HALF]) for k in range(FLIGHT)]
        neg = [sb(f"t0_neg{k}", [P, HALF]) for k in range(FLIGHT)]
        bank = lambda i: env.psum[i // 2][:, i % 2 * HALF:(i % 2 + 1) * HALF]
        rows, logits = [bank(k) for k in range(FLIGHT)], [bank(FLIGHT + k) for k in range(FLIGHT)]
        A2, B2, alpha = par[:, 7:8], par[:, 8:9], par[:, 4:5]
        units, per = TOKENS // HALF, HALF // P
        half = lambda buf, n: buf[:, bass.ds(n * HALF, HALF)]
        block = ctx.enter_context(nc.Block())

        def each(engine, body):
            for k in range(FLIGHT):
                body(k, k, 3)
            with engine.Fori(1, units // FLIGHT - 1) as i:
                for k in range(FLIGHT):
                    body(i * FLIGHT + k, k, 3)
            for k in range(FLIGHT):
                body(units - FLIGHT + k, k, FLIGHT - 1 - k)

        @block.sync
        def _(sp):
            sp.dma_start(wr[:, :], a["w_router"]).then_inc(wr_loaded, 16)

        @block.tensor
        def _(pe):
            pe.wait_ge(wr_loaded, 16)
            pe.matmul(logits[0][:, 0:E0], env.cen[:, :], wr[:, :], start=True, stop=True).then_inc(wr_turned, 1)
            pe.wait_ge(wr_ready, 1)
            pe.sem_inc(rows_free, FLIGHT)

            def turn(n, k, ahead):
                pe.wait_ge(x_ready, n + 1)
                pe.wait_ge(copied_free, n + 1)
                pe.wait_ge(stats_free, n + 1)
                for j in range(per):
                    pe.transpose(rows[k][:, j * P:(j + 1) * P], u[k][:, j * P:(j + 1) * P], env.idf[:, :])
                for j in range(per):
                    mm = pe.matmul(logits[k][:, j * E0:(j + 1) * E0], u[k][:, j * P:(j + 1) * P], wc[:, :], start=True, stop=True)
                mm.then_inc(rows_free, 1)
            each(pe, turn)

        @block.vector
        def _(dve):
            dve.wait_ge(wr_turned, 1)
            dve.tensor_copy(wc[:, :], logits[0][:, 0:E0]).then_inc(wr_ready, 1)
            dve.sem_inc(stats_free, FLIGHT)
            dve.tensor_scalar(negB2, B2, -1.0, None, ALU.mult).then_inc(coef, 1)
            dve.tensor_scalar(negalpha, alpha, -1.0, None, ALU.mult).then_inc(coef, 1)

            def residual(n, k):
                dve.wait_ge(rows_free, n + 1)
                dve.wait_ge(kept_free, n + 1)
                dve.scalar_tensor_tensor(u[k][:, :], half(CONV, n), A2, half(Y, n), ALU.mult, ALU.add).then_inc(sum_ready, 1)

            def add(n, k):
                dve.wait_ge(half_ready, n + 1)
                dve.scalar_tensor_tensor(u[k][:, :], neg[k][:, :], negalpha, u[k][:, :], ALU.mult, ALU.add).then_inc(x_ready, 1)

            def statistics(n, k):
                dve.wait_ge(rows_free, n + FLIGHT + 1)
                dve.tensor_copy(env.logit[:, bass.ds(n * (per * E0), per * E0)], logits[k][:, 0:per * E0])
                dve.wait_ge(copied_free, n + FLIGHT + 1)
                for j in range(per):
                    st = dve.bn_stats(env.rowst[:, bass.ds((n * per + j) * 6, 6)], Y[:, bass.ds(n * HALF + j * P, P)])
                st.then_inc(stats_free, 1)

            def unit(n, k, ahead):
                if ahead >= 3:
                    residual(n + 3, (k + 3) % FLIGHT)
                if ahead >= 1:
                    add(n + 1, (k + 1) % FLIGHT)
                if not isinstance(n, int) or n > 0:
                    statistics(n - 1, (k - 1) % FLIGHT)

            for k in range(3):
                residual(k, k)
            add(0, 0)
            each(dve, unit)
            statistics(units - 1, FLIGHT - 1)
            dve.wait_ge(stats_free, units + FLIGHT)

        @block.gpsimd
        def _(pool):
            def add_x(n, k, ahead):
                pool.wait_ge(act_ready, n * 2 + 2)
                pool.tensor_tensor(u[k][:, :], half(X, n), u[k][:, :], ALU.add).then_inc(half_ready, 1)
            each(pool, add_x)

        @block.scalar
        def _(act):
            act.preload_act_table_set("natural_log_exp_and_others")
            act.sem_inc(copied_free, FLIGHT)
            act.sem_inc(kept_free, FLIGHT)
            act.wait_ge(coef, 2)

            def prelu(n, k):
                act.wait_ge(sum_ready, n + 1)
                act.activation(neg[k][:, :], u[k][:, :], ACT.Relu, bias=negB2, scale=-1.0).then_inc(act_ready, 1)
                act.activation(u[k][:, :], u[k][:, :], ACT.Relu, bias=B2, scale=1.0).then_inc(act_ready, 1)

            def keep(n, k):
                act.wait_ge(x_ready, n + 1)
                act.activation(half(X, n), u[k][:, :], ACT.Copy).then_inc(kept_free, 1)

            def copy(n, k):
                act.wait_ge(rows_free, n + FLIGHT + 1)
                act.activation(half(Y, n), rows[k][:, :], ACT.Copy).then_inc(copied_free, 1)

            def unit(n, k, ahead):
                if not isinstance(n, int) or n > 0:
                    copy(n - 1, (k - 1) % FLIGHT)
                if ahead >= 3:
                    prelu(n + 3, (k + 3) % FLIGHT)
                if ahead >= 1:
                    keep(n + 1, (k + 1) % FLIGHT)

            for k in range(3):
                prelu(k, k)
            keep(0, 0)
            each(act, unit)
            copy(units - 1, FLIGHT - 1)


def phase_route0(nc, env):
    with ExitStack() as ctx:
        sem = lambda n: ctx.enter_context(nc.semaphore(n))
        sb = lambda n, s, d=F32: ctx.enter_context(nc.sbuf_tensor(n, s, d))
        steps, var_ready, rstd_ready, logs = sem("r0_steps"), sem("r0_var_ready"), sem("r0_rstd_ready"), sem("r0_logs")
        gap_ready, exp_ready, hot_ready = sem("r0_gap_ready"), sem("r0_exp_ready"), sem("r0_hot_ready")
        total_ready, total_copied, prefix_ready = sem("r0_total_ready"), sem("r0_total_copied"), sem("r0_prefix_ready")
        small = {k: sb(f"r0_{k}", [P, TILES]) for k in
                 ("mean2", "dm", "m2", "var", "ln", "top1", "top2", "rev1", "rev2", "gap", "ex", "g1", "g2", "swap", "hi", "lo", "pid", "slot")}
        v = {k: x[:, :] for k, x in small.items()}
        wide = [sb(f"r0_wide{k}", [P, TILES, E0]) for k in range(3)]
        hot = sb("r0_hot", [P, PAIRS, TILES], BF16)
        total, where = (sb(f"r0_{k}", [P, PAIRS * TILES]) for k in ("total", "where"))
        pc = {k: sb(f"r0_p{k}", [P, PAIRS]) for k in ("cum", "count", "tiles", "cumt", "adj")}
        pi = sb("r0_pi", [P, PAIRS], I32)
        st = env.rowst[:, :].rearrange("p (t s) -> p t s", s=6)
        over_e = lambda x: x.unsqueeze(2).broadcast_to([P, TILES, E0])
        rev = env.rev.unsqueeze(1).broadcast_to([P, TILES, E0])
        chunks = PAIRS * TILES // HALF
        bank = lambda c: env.psum[c // 2][:, (c % 2) * HALF:(c % 2 + 1) * HALF]
        block = ctx.enter_context(nc.Block())

        @block.scalar
        def _(act):
            act.preload_act_table_set("natural_log_exp_and_others")
            act.wait_ge(var_ready, 1)
            act.activation(v["ln"], v["var"], ACT.Ln, bias=env.eps[:, 1:2], scale=1.0 / C).then_inc(logs, 1)
            act.wait_ge(logs, 1)
            act.activation(env.rstd[:, :], v["ln"], ACT.Exp, scale=-0.5).then_inc(rstd_ready, 1)
            act.wait_ge(gap_ready, 1)
            act.activation(v["ex"], v["gap"], ACT.Exp).then_inc(exp_ready, 1)
            for c in range(chunks):
                act.wait_ge(total_ready, c + 1)
                act.activation(total[:, c * HALF:(c + 1) * HALF], bank(c), ACT.Copy).then_inc(total_copied, 1)

        @block.tensor
        def _(pe):
            pe.wait_ge(hot_ready, 1)
            cols = hot[:, :, :].rearrange("p a t -> p (a t)")
            for c in range(chunks):
                pe.matmul(bank(c), env.ones16[:, :], cols[:, c * HALF:(c + 1) * HALF], start=True, stop=True)\
                  .then_inc(total_ready, 1)
            for c in range(chunks):
                pe.wait_ge(total_copied, c + 1)
                pe.matmul(bank(c), env.ltri[:, :], cols[:, c * HALF:(c + 1) * HALF], start=True, stop=True)\
                  .then_inc(prefix_ready, 1)

        @block.vector
        def _(dve):
            link = chain(dve, steps)
            link(dve.tensor_tensor(v["dm"], st[:, :, 1], st[:, :, 4], ALU.subtract))
            link(dve.tensor_tensor(v["m2"], st[:, :, 2], st[:, :, 5], ALU.add))
            link(dve.tensor_tensor(v["dm"], v["dm"], v["dm"], ALU.mult))
            dve.scalar_tensor_tensor(v["var"], v["dm"], C / 4.0, v["m2"], ALU.mult, ALU.add).then_inc(var_ready, 1)
            link(dve.tensor_tensor(v["mean2"], st[:, :, 1], st[:, :, 4], ALU.add))
            dve.wait_ge(rstd_ready, 1)
            link(dve.scalar_tensor_tensor(env.shift[:, :], v["mean2"], -0.5, env.rstd[:, :], ALU.mult, ALU.mult))
            l, hit, l2 = (w[:, :, :] for w in wide)
            link(dve.tensor_tensor(l, env.logit[:, :].rearrange("p (t e) -> p t e", e=E0), over_e(env.rstd[:, :]), ALU.mult))
            link(dve.tensor_reduce(v["top1"], l, AX.X, ALU.max))
            link(dve.tensor_tensor(hit, l, over_e(v["top1"]), ALU.is_equal))
            link(dve.tensor_tensor(hit, hit, rev, ALU.mult))
            link(dve.tensor_reduce(v["rev1"], hit, AX.X, ALU.max))
            link(dve.tensor_tensor(hit, hit, over_e(v["rev1"]), ALU.is_equal))
            link(dve.scalar_tensor_tensor(l2.rearrange("p t e -> p (t e)"), hit.rearrange("p t e -> p (t e)"), -1e30,
                                          l.rearrange("p t e -> p (t e)"), ALU.mult, ALU.add))
            link(dve.tensor_reduce(v["top2"], l2, AX.X, ALU.max))
            link(dve.tensor_tensor(hit, l2, over_e(v["top2"]), ALU.is_equal))
            link(dve.tensor_tensor(hit, hit, rev, ALU.mult))
            link(dve.tensor_reduce(v["rev2"], hit, AX.X, ALU.max))
            dve.tensor_tensor(v["gap"], v["top2"], v["top1"], ALU.subtract).then_inc(gap_ready, 1)
            link(dve.tensor_tensor(v["lo"], v["rev1"], v["rev2"], ALU.max))
            link(dve.tensor_tensor(v["hi"], v["rev1"], v["rev2"], ALU.min))
            link(dve.tensor_scalar(v["pid"], v["lo"], -1.0, float(E0), ALU.mult, ALU.add))
            link(dve.scalar_tensor_tensor(v["pid"], v["lo"], float(E0 - 1), v["pid"], ALU.add, ALU.mult))
            link(dve.tensor_tensor(v["hi"], v["lo"], v["hi"], ALU.subtract))
            link(dve.scalar_tensor_tensor(v["pid"], v["pid"], 0.5, v["hi"], ALU.mult, ALU.add))
            link(dve.tensor_scalar(v["pid"], v["pid"], -1.0, None, ALU.add))
            dve.tensor_tensor(hot[:, :, :], v["pid"].unsqueeze(1).broadcast_to([P, PAIRS, TILES]),
                              env.pair_no.unsqueeze(2).broadcast_to([P, PAIRS, TILES]), ALU.is_equal).then_inc(hot_ready, 1)
            dve.wait_ge(exp_ready, 1)
            link(dve.tensor_scalar(v["g1"], v["ex"], 1.0, None, ALU.add))
            link(dve.reciprocal(v["g1"], v["g1"]))
            link(dve.tensor_tensor(v["g2"], v["ex"], v["g1"], ALU.mult))
            link(dve.tensor_tensor(v["swap"], v["rev1"], v["rev2"], ALU.is_gt))
            link(dve.tensor_tensor(v["lo"], v["g1"], v["g2"], ALU.subtract))
            link(dve.tensor_tensor(v["swap"], v["swap"], v["lo"], ALU.mult))
            link(dve.tensor_tensor(v["lo"], v["g2"], v["swap"], ALU.add))
            link(dve.tensor_tensor(v["hi"], v["g1"], v["swap"], ALU.subtract))
            gates = env.gates[:, :].rearrange("p (t g) -> p t g", g=2)
            link(dve.tensor_scalar(gates[:, :, 0], v["lo"], 1.0 / WSCALE ** 2, None, ALU.mult))
            link(dve.tensor_scalar(gates[:, :, 1], v["hi"], 1.0 / WSCALE ** 2, None, ALU.mult))
            dve.wait_ge(total_copied, chunks)
            link(dve.tensor_tensor_scan(where[:, :], total[:, :], env.eps[:, 2:3].broadcast_to([P, PAIRS * TILES]), 0.0, ALU.add, ALU.add))
            cum, count, tiles, cumt, adj = (pc[k][:, :] for k in ("cum", "count", "tiles", "cumt", "adj"))
            link(dve.tensor_copy(cum, where[:, :].rearrange("p (a t) -> p a t", t=TILES)[:, :, TILES - 1]))
            link(dve.tensor_tensor(where[:, :], where[:, :], total[:, :], ALU.subtract))
            link(dve.tensor_copy(count[:, 0:1], cum[:, 0:1]))
            link(dve.tensor_tensor(count[:, 1:PAIRS], cum[:, 1:PAIRS], cum[:, 0:PAIRS - 1], ALU.subtract))
            link(dve.tensor_scalar(tiles, count, float(SLOT - 1), float(SLOT), ALU.add, ALU.max))
            link(dve.tensor_copy(pi[:, :], tiles))
            link(dve.tensor_scalar(pi[:, :], pi[:, :], SLOT.bit_length() - 1, None, ALU.arith_shift_right))
            link(dve.tensor_copy(tiles, pi[:, :]))
            link(dve.tensor_tensor_scan(cumt, tiles, env.eps[:, 2:3].broadcast_to([P, PAIRS]), 0.0, ALU.add, ALU.add))
            link(dve.memset(env.starts[:, 0:1], 0))
            link(dve.tensor_copy(env.starts[:, 1:PAIRS + 1], cumt[0:1, :]))
            link(dve.tensor_scalar(env.finals[:, :], cumt[0:1, :], -1.0, None, ALU.add))
            link(dve.tensor_scalar(env.starts[:, PAIRS + 1:PAIRS + 2], cumt[0:1, PAIRS - 1:PAIRS], -1.0, float(MAX_TILES + 1),
                                   ALU.mult, ALU.add))
            link(dve.tensor_tensor(adj, cumt, tiles, ALU.subtract))
            link(dve.scalar_tensor_tensor(adj, adj, float(SLOT), cum, ALU.mult, ALU.subtract))
            link(dve.tensor_tensor(adj, adj, count, ALU.add))
            grid = lambda x: x.rearrange("p (a t) -> p a t", t=TILES)
            link(dve.tensor_tensor(grid(where[:, :]), grid(where[:, :]), adj.unsqueeze(2).broadcast_to([P, PAIRS, TILES]), ALU.add))
            for c in range(chunks):
                dve.wait_ge(prefix_ready, c + 1)
                part = slice(c * HALF, (c + 1) * HALF)
                link(dve.tensor_tensor(where[:, part], bank(c), where[:, part], ALU.add))
            link(dve.tensor_tensor(where[:, :], where[:, :], hot[:, :, :].rearrange("p a t -> p (a t)"), ALU.mult))
            link(dve.tensor_reduce(v["slot"], where[:, :].rearrange("p (a t) -> p t a", t=TILES), AX.X, ALU.add))
            link(dve.tensor_copy(env.slot[:, :], v["slot"]))


def phase_dispatch(nc, env):
    Y = env.Y
    with ExitStack() as ctx:
        sem = lambda n: ctx.enter_context(nc.semaphore(n))
        depth = 4
        rows = [ctx.enter_context(nc.sbuf_tensor(f"d0_rows{k}", [P, ROW], F32)) for k in range(depth)]
        index = [ctx.enter_context(nc.sbuf_tensor(f"d0_index{k}", [P, 1], U32)) for k in range(depth)]
        ready = sem("d0_ready")
        sent = [sem(f"d0_sent{k}") for k in range(depth)]
        block = ctx.enter_context(nc.Block())

        def fill(dve, i, k):
            dve.tensor_scalar(rows[k][:, 0:C], Y[:, bass.ds(i * P, P)], env.rstd[:, bass.ds(i, 1)],
                              env.shift[:, bass.ds(i, 1)], ALU.mult, ALU.add).then_inc(ready, 1)
            dve.tensor_copy(rows[k][:, C:ROW], env.gates[:, bass.ds(i * 2, 2)]).then_inc(ready, 1)
            dve.tensor_copy(index[k][:, :], env.slot[:, bass.ds(i, 1)]).then_inc(ready, 1)

        def send(pool, i, k):
            wait_apart(pool, ready, i * 3 + 3, env.passed["pool"])
            pool.indirect_dma_start(env.xg, bass.IndirectOffsetOnAxis(ap=index[k][:, :], axis=0), rows[k][:, :], None)\
                .then_inc(sent[k], 16)

        @block.vector
        def _(dve):
            for k in range(depth):
                fill(dve, k, k)
            with dve.Fori(1, TILES // depth) as j:
                for k in range(depth):
                    dve.wait_ge(sent[k], j * 16)
                    fill(dve, j * depth + k, k)

        @block.gpsimd
        def _(pool):
            pool.wait_ge(env.cleared, CLEARS * 16)
            with pool.Fori(0, TILES // depth) as j:
                for k in range(depth):
                    send(pool, j * depth + k, k)
            for k in range(depth):
                pool.wait_ge(sent[k], TILES // depth * 16)


def split_weights0(nc, env, a):
    W = env.weights
    half2 = lambda e, part: W[:, e * WCOLS:e * WCOLS + 4 * H0].rearrange("p (w s n) -> p w s n", w=2, s=2)[:, :, part, :]
    with ExitStack() as ctx:
        sem = lambda n: ctx.enter_context(nc.semaphore(n))
        sb = lambda n, s, d=F32: ctx.enter_context(nc.sbuf_tensor(n, s, d))
        loaded, biases = [sem(f"w0_loaded{q}") for q in range(2)], sem("w0_biases")
        high, low, steps = sem("w0_high"), sem("w0_low"), sem("w0_steps")
        raw = [sb(f"w0_raw{q}", [P, 2 * H0]) for q in range(2)]
        b1, b2, rest = sb("w0_b1", [P, E0 * KM]), sb("w0_b2", [P, E0 * C]), sb("w0_rest", [P, E0 * C])
        parts = [sb(f"w0_part{k}", [P, E0 * C], BF16) for k in range(3)]
        block = ctx.enter_context(nc.Block())

        @block.sync
        def _(sp):
            sp.dma_start(b1[:, :], a["b1"]).then_inc(biases, 16)
            sp.dma_start(b2[:, :], a["b2"].broadcast_to([P, E0 * C])).then_inc(biases, 16)
            for e in range(E0):
                if e >= 2:
                    sp.wait_ge(low, e - 1)
                sp.dma_start(raw[e % 2][:, :], a["w_moe0"][e, :, :]).then_inc(loaded[e % 2], 16)

        @block.scalar
        def _(act):
            act.preload_act_table_set("natural_log_exp_and_others")
            for e in range(E0):
                act.wait_ge(loaded[e % 2], 16 * (e // 2 + 1))
                act.activation(half2(e, 0), raw[e % 2][:, :].rearrange("p (w n) -> p w n", w=2), ACT.Copy, scale=WSCALE)\
                   .then_inc(high, 1)

        @block.vector
        def _(dve):
            link = chain(dve, steps)
            dve.wait_ge(biases, 32)
            link(dve.tensor_scalar(b2[:, :], b2[:, :], WSCALE ** 2, None, ALU.mult))
            link(dve.tensor_copy(parts[0][:, :], b2[:, :]))
            link(dve.tensor_tensor(rest[:, :], b2[:, :], parts[0][:, :], ALU.subtract))
            link(dve.tensor_copy(parts[1][:, :], rest[:, :]))
            link(dve.tensor_tensor(rest[:, :], rest[:, :], parts[1][:, :], ALU.subtract))
            link(dve.tensor_copy(parts[2][:, :], rest[:, :]))
            blocks = W[:, :].rearrange("p (e n) -> p e n", n=WCOLS)
            biasrow = blocks[:, :, 4 * H0:4 * H0 + C].bitcast(BF16)
            link(dve.memset(biasrow, 0.0))
            for k in range(3):
                link(dve.tensor_copy(biasrow[32 * k:32 * k + 1, :, :],
                                     parts[k][32 * k:32 * k + 1, :].rearrange("p (e n) -> p e n", e=E0)))
            for e in range(E0):
                at = e * WCOLS + 4 * H0 + C
                link(dve.tensor_scalar(W[:, at:at + 2 * KM].bitcast(F32), b1[:, e * KM:(e + 1) * KM], WSCALE, None, ALU.mult))
            for e in range(E0):
                dve.wait_ge(high, e + 1)
                for w in range(2):
                    at = e * WCOLS + w * 2 * H0
                    ins = dve.scalar_tensor_tensor(W[:, at + H0:at + 2 * H0], raw[e % 2][:, w * H0:(w + 1) * H0], WSCALE,
                                                   W[:, at:at + H0], ALU.mult, ALU.subtract)
                ins.then_inc(low, 1)
            dve.wait_ge(low, E0)


def phase_experts0(nc, env, a):
    with ExitStack() as ctx:
        sem = lambda n: ctx.enter_context(nc.semaphore(n))
        sb = lambda n, s, d=F32: ctx.enter_context(nc.sbuf_tensor(n, s, d))
        staged = [sem(f"m0_staged{q}") for q in range(2)]
        rows_loaded, turned, x_split = sem("m0_rows_loaded"), sem("m0_turned"), sem("m0_x_split")
        x_high, h_ready, relu_ready, h_split = sem("m0_x_high"), sem("m0_h_ready"), sem("m0_relu_ready"), sem("m0_h_split")
        filled = sem("m0_filled")
        hh_ready, result_free = sem("m0_hh_ready"), sem("m0_result_free")
        lo_ready, hi_ready, part_ready, out_ready = (sem(f"m0_{x}") for x in ("lo_ready", "hi_ready", "part_ready", "out_ready"))
        x_taken = sem("m0_x_taken")
        gates_ready, stored, table_loaded, next_gates = sem("m0_gates_ready"), sem("m0_stored"), sem("m0_table_loaded"), sem("m0_next_gates")
        stage = [[sb(f"m0_stage{q}{e}", [P, WCOLS], F16) for e in range(2)] for q in range(2)]
        table = sb("m0_table", [1, 2 * PAIRS + 2], I32)
        rows = sb("m0_rows", [P, SUB, ROW])
        x = sb("m0_x", [P, 2, SLOT], F16)
        coming_x = sb("m0_coming_x", [P, 2, SLOT], F16)
        xh, xl = x[:, 0, :], x[:, 1, :]
        hf = [sb(f"m0_hf{e}", [P, KM, SLOT]) for e in range(2)]
        hh = [sb(f"m0_hh{e}", [P, KM, SLOT], F16) for e in range(2)]
        hl = [sb(f"m0_hl{e}", [P, KM, SLOT], F16) for e in range(2)]
        gates, coming = sb("m0_gates", [P, SUB, 2]), sb("m0_coming", [P, SUB, 2])
        part, result = sb("m0_part", [P, SUB, C]), sb("m0_result", [P, SUB, C])
        hidden, turn = env.psum[0:2], env.psum[2][:, 0:SLOT]
        y = [env.psum[3][:, e * HALF:e * HALF + SUB * C].rearrange("p (s c) -> p s c", s=SUB) for e in range(2)]
        block = ctx.enter_context(nc.Block())

        def pairs(engine):
            with engine.Fori(0, PAIRS // 2) as half:
                for q in range(2):
                    p = half * 2 + q
                    first = engine.value_load(env.starts[0:1, bass.ds(p, 1)], min_val=0, max_val=MAX_TILES - 1)
                    last = engine.value_load(env.finals[0:1, bass.ds(p, 1)], min_val=0, max_val=MAX_TILES - 1)
                    yield half, q, p, first, last

        @block.sync
        def _(sp):
            sp.dma_start(table[:, :], a["k_pairs"]).then_inc(table_loaded, 16)
            sp.wait_ge(table_loaded, 16)

            def load(i):
                sp.dma_start(rows[:, :, :], env.xg[bass.ds(i * SLOT, SLOT), :].rearrange("(s p) c -> p s c", p=P))\
                  .then_inc(rows_loaded, 16)

            def stage_pair(p, q):
                for e in range(2):
                    expert = sp.value_load(table[0:1, bass.ds(p * 2 + e, 1)], min_val=0, max_val=E0 - 1)
                    sp.dma_start(stage[q][e][:, :].bitcast(U32),
                                 env.weights[:, :].bitcast(U32)[:, bass.ds(expert * (WCOLS // 2), WCOLS // 2)]).then_inc(staged[q], 16)

            load(0)
            stage_pair(0, 0)
            sp.wait_ge(x_split, 2)
            load(1)
            for half, q, p, first, last in pairs(sp):
                sp.wait_ge(x_split, first + 3)
                load(first + 2)
                sp.wait_ge(hi_ready, first + 1)
                stage_pair(p + 1, 1 - q)
                with sp.Fori(first + 1, last + 1) as i:
                    sp.wait_ge(x_split, i + 3)
                    load(i + 2)
            total = sp.value_load(env.starts[0:1, PAIRS:PAIRS + 1], min_val=PAIRS, max_val=MAX_TILES)
            wait_apart(sp, rows_loaded, total * 16 + 32, env.passed["sp"])
            sp.wait_ge(staged[0], 16 * (PAIRS + 2))

        @block.gpsimd
        def _(pool):
            pool.sem_inc(result_free, 1)
            total = pool.value_load(env.starts[0:1, PAIRS:PAIRS + 1], min_val=PAIRS, max_val=MAX_TILES)
            with pool.Fori(total, MAX_TILES + 1) as i:
                pool.dma_start(env.yg[bass.ds(i * SLOT, SLOT), :].rearrange("(s p) c -> p s c", p=P),
                               env.zero[:, 0:C].unsqueeze(1).broadcast_to([P, SUB, C])).then_inc(filled, 16)
            spare = pool.value_load(env.starts[0:1, PAIRS + 1:PAIRS + 2], min_val=1, max_val=MAX_TILES + 1 - PAIRS)
            wait_apart(pool, filled, spare * 16, env.passed["pool"])
            with pool.Fori(0, total) as i:
                pool.wait_ge(out_ready, i + 2)
                pool.dma_start(env.yg[bass.ds(i * SLOT, SLOT), :].rearrange("(s p) c -> p s c", p=P), result[:, :, :])\
                    .then_inc(stored, 16)
                pool.wait_ge(stored, i * 16 + 16)
                pool.sem_inc(result_free, 1)

        @block.tensor
        def _(pe):
            def transpose(i):
                pe.wait_ge(rows_loaded, i * 16 + 16)
                pe.wait_ge(x_split, i + 1)
                for s in range(SUB):
                    mm = pe.transpose(turn[:, s * P:(s + 1) * P], rows[:, s, 0:C], env.idf[:, :])
                mm.then_inc(turned, 1)

            def up(w, e):
                for m in range(KM):
                    out = hidden[e][:, m * SLOT:(m + 1) * SLOT]
                    high, low = w[:, m * P:(m + 1) * P], w[:, H0 + m * P:H0 + (m + 1) * P]
                    pe.matmul(out, high, xh, start=True, stop=False)
                    pe.matmul(out, high, xl, start=False, stop=False)
                    mm = pe.matmul(out, low, xh, start=False, stop=True)
                    if m % 2:
                        mm.then_inc(h_ready, 1)

            def down(w, e):
                for s in range(SUB):
                    cols = slice(s * P, (s + 1) * P)
                    for k in range(KM):
                        high, low = w[:, 2 * H0 + k * P:2 * H0 + (k + 1) * P], w[:, 3 * H0 + k * P:3 * H0 + (k + 1) * P]
                        pe.matmul(y[e][:, s, :], hh[e][:, k, cols], high, start=(k == 0), stop=False)
                        pe.matmul(y[e][:, s, :], hh[e][:, k, cols], low, start=False, stop=False)
                        pe.matmul(y[e][:, s, :], hl[e][:, k, cols], high, start=False, stop=False)
                    mm = pe.matmul(y[e][:, s, :], env.ones16[:, :], w[:, 4 * H0:4 * H0 + C].bitcast(BF16), start=False, stop=True)
                mm.then_inc((lo_ready, hi_ready)[e], 1)

            def tile(i, w, following, weights_here=None):
                up(w[1], 1)
                pe.wait_ge(h_split, i * 4 + 6)
                pe.wait_ge(part_ready, i + 1)
                down(w[0], 0)
                if weights_here is not None:
                    pe.wait_ge(*weights_here)
                pe.wait_ge(x_taken, i + 2)
                up(following[0], 0)
                transpose(i + 2)
                pe.wait_ge(h_split, i * 4 + 8)
                pe.wait_ge(out_ready, i + 1)
                down(w[1], 1)

            pe.sem_inc(hi_ready, 1)
            transpose(0)
            pe.wait_ge(x_taken, 1)
            transpose(1)
            pe.wait_ge(staged[0], 32)
            up(stage[0][0], 0)
            for half, q, p, first, last in pairs(pe):
                with pe.Fori(first, last) as i:
                    tile(i, stage[q], stage[q])
                tile(last, stage[q], stage[1 - q], (staged[1 - q], half * 32 + 32 + 32 * q))

        @block.scalar
        def _(act):
            act.preload_act_table_set("natural_log_exp_and_others")

            def high_x(i):
                act.wait_ge(turned, i + 1)
                if not isinstance(i, int) or i > 0:
                    act.wait_ge(x_taken, i)
                act.activation(coming_x[:, 0, :], turn, ACT.Copy).then_inc(x_high, 1)

            def relu(i, w, e, b):
                bias = w[e][:, 4 * H0 + C:4 * H0 + C + 2 * KM].bitcast(F32)
                act.wait_ge(h_ready, i * 4 + (2 * e + b + 1))
                act.wait_ge(h_split, i * 4 + (2 * e + b + 1))
                for m in (2 * b, 2 * b + 1):
                    ins = act.activation(hf[e][:, m, :], hidden[e][:, m * SLOT:(m + 1) * SLOT], ACT.Relu,
                                         bias=bias[:, m:m + 1], scale=1.0)
                ins.then_inc(relu_ready, 1)

            def tile(i, w, following, weights_here=None):
                relu(i, w, 1, 0)
                relu(i, w, 1, 1)
                act.wait_ge(lo_ready, i + 1)
                act.wait_ge(gates_ready, i + 1)
                act.wait_ge(out_ready, i + 1)
                for s in range(SUB):
                    ins = act.activation(part[:, s, :], y[0][:, s, :], ACT.Copy, scale=gates[:, s, 0:1])
                ins.then_inc(part_ready, 1)
                if weights_here is not None:
                    act.wait_ge(*weights_here)
                relu(i + 1, following, 0, 0)
                relu(i + 1, following, 0, 1)
                high_x(i + 2)

            act.sem_inc(part_ready, 1)
            high_x(0)
            act.wait_ge(staged[0], 32)
            high_x(1)
            relu(0, stage[0], 0, 0)
            relu(0, stage[0], 0, 1)
            for half, q, p, first, last in pairs(act):
                with act.Fori(first, last) as i:
                    tile(i, stage[q], stage[q])
                tile(last, stage[q], stage[1 - q], (staged[1 - q], half * 32 + 32 + 32 * q))

        @block.vector
        def _(dve):
            dve.sem_inc(x_split, 1)
            dve.sem_inc(h_split, 4)
            dve.sem_inc(out_ready, 1)

            def low_x(i):
                dve.wait_ge(x_high, i + 1)
                dve.tensor_copy(coming[:, :, :], rows[:, :, C:ROW]).then_inc(next_gates, 1)
                dve.tensor_tensor(coming_x[:, 1, :], turn, coming_x[:, 0, :], ALU.subtract).then_inc(x_split, 1)

            def take_x(i):
                dve.wait_ge(x_split, i + 2)
                dve.tensor_copy(x[:, :, :], coming_x[:, :, :]).then_inc(x_taken, 1)

            def take_gates(i):
                dve.wait_ge(next_gates, i + 1)
                dve.tensor_copy(gates[:, :, :], coming[:, :, :]).then_inc(gates_ready, 1)

            def split(i, e, b):
                m = slice(2 * b, 2 * b + 2)
                dve.wait_ge(relu_ready, i * 4 + (2 * e + b + 1))
                dve.tensor_copy(hh[e][:, m, :], hf[e][:, m, :]).then_inc(hh_ready, 1)
                dve.wait_ge(hh_ready, i * 4 + (2 * e + b + 1))
                dve.tensor_tensor(hl[e][:, m, :], hf[e][:, m, :], hh[e][:, m, :], ALU.subtract).then_inc(h_split, 1)

            dve.wait_ge(turned, 1)
            low_x(0)
            take_x(0)
            take_gates(0)
            dve.wait_ge(gates_ready, 1)
            low_x(1)
            split(0, 0, 0)
            split(0, 0, 1)
            total = dve.value_load(env.starts[0:1, PAIRS:PAIRS + 1], min_val=PAIRS, max_val=MAX_TILES)
            with dve.Fori(0, total) as i:
                dve.wait_ge(h_ready, i * 4 + 4)
                take_x(i + 1)
                split(i, 1, 0)
                split(i, 1, 1)
                split(i + 1, 0, 0)
                split(i + 1, 0, 1)
                dve.wait_ge(hi_ready, i + 2)
                dve.wait_ge(part_ready, i + 2)
                dve.wait_ge(result_free, i + 1)
                for s in range(SUB):
                    ins = dve.scalar_tensor_tensor(result[:, s, :], y[1][:, s, :], gates[:, s, 1:2], part[:, s, :], ALU.mult, ALU.add)
                ins.then_inc(out_ready, 1)
                dve.wait_ge(out_ready, i + 2)
                take_gates(i + 1)
                dve.wait_ge(gates_ready, i + 2)
                low_x(i + 2)


def phase_involution(nc, env, a, out):
    X, par = env.X, env.par
    with ExitStack() as ctx:
        names = ("gathered turned x_added cent_ready sq_ready var_ready ln_ready rstd_ready y_ready t_ready v_ready "
                 "padded_ready e2_ready group_ready gvar_ready gln_ready grstd_ready coef_ready relu_ready split_ready "
                 "tap_ready product_ready summed pool_summed done steps w_loaded w_ready border sent index_ready").split()
        S = {n: ctx.enter_context(nc.semaphore(f"iv_{n}")) for n in names}
        sb = lambda n, s, d=F32: ctx.enter_context(nc.sbuf_tensor(f"iv_{n}", s, d))
        wv, w1, gavg = sb("wv", [P, C]), sb("w1", [P, P]), sb("gavg", [P, P])
        w2, w2b, gn = sb("w2", [P, TAPS, P]), sb("w2b", [P, TAPS]), sb("gn", [P, 2])
        wa, wb = sb("wa", [P, TAPS, P], F16), sb("wb", [P, TAPS, P], F16)
        got = [sb(f"got{k}", [P, C]) for k in range(TPI)]
        index = [sb(f"index{k}", [P, 1], U32) for k in range(TPI)]
        sq, rs, y, tf = (sb(n, [P, PIX]) for n in ("sq", "rs", "y", "tf"))
        ct = [sb(f"ct{q}", [P, PIX], F16) for q in range(2)]
        xv = [sb(f"xv{q}", [P, PAD, PAD]) for q in range(2)]
        pool_part = [sb(f"pool_part{k}", [P, SIDE, SIDE]) for k in range(POOL_TAPS)]
        own_part = [sb(f"own_part{k}", [P, SIDE, SIDE]) for k in range(2)]
        own_sum, pool_sum = sb("own_sum", [P, SIDE, SIDE]), sb("pool_sum", [P, SIDE, SIDE])
        t = sb("t", [P, 32])
        D = env.psum
        cent = [D[1][:, HALF:PIX], D[1][:, 0:HALF]]
        halves = [slice(0, HALF), slice(HALF, PIX)]
        grid = lambda ap: ap.rearrange("p (h w) -> p h w", w=SIDE)
        loads = [(wv[:, :], a["w_v"]), (w1[:, :], a["w1_d4"]), (gavg[:, :], a["k_groups"]), (w2[:, :, :], a["w2_taps"]),
                 (w2b[:, :], a["b2_taps"]), (gn[:, :], a["gn"])]
        block = ctx.enter_context(nc.Block())

        def images(engine, body):
            with by_two(engine, 0, IMAGES - 4) as n:
                for q in range(2):
                    body(n + q, q, 3)
            for n in range(IMAGES - 4, IMAGES):
                body(n, n % 2, min(3, IMAGES - 1 - n))

        def half(buf, n, h):
            return buf[:, bass.ds(n * PIX + h * HALF, HALF)]

        @block.sync
        def _(sp):
            for dst, src in loads:
                sp.dma_start(dst, src).then_inc(S["w_loaded"], 16)

            with sp.Fori(FIRST_IMAGES, IMAGES) as n:
                sp.wait_ge(S["done"], n + 3)
                sp.dma_start(out[:, bass.ds(n * PIX, PIX)], image(X, n)).then_inc(S["sent"], 16)
            sp.wait_ge(S["sent"], 16 * (IMAGES - FIRST_IMAGES))

        @block.gpsimd
        def _(pool):
            pool.sem_inc(S["pool_summed"], POOL_TAPS)

            def gather(n, first=False):
                if not first:
                    pool.wait_ge(S["turned"], n * 2)
                for k in range(TPI):
                    pool.tensor_copy(index[k][:, :], env.slot[:, bass.ds(n * TPI + k, 1)]).then_inc(S["index_ready"], 1)
                for k in range(TPI):
                    wait_apart(pool, S["index_ready"], n * TPI + k + 1, env.passed["pool"])
                    pool.indirect_dma_start(got[k][:, :], None, env.yg, bass.IndirectOffsetOnAxis(ap=index[k][:, :], axis=0))\
                        .then_inc(S["gathered"], 16)

            def body(n, q, ahead):
                for k in range(POOL_TAPS):
                    pool.wait_ge(S["product_ready"], n * TAPS + k + 3)
                    if k == 0:
                        pool.wait_ge(S["done"], n + 2)
                    else:
                        pool.wait_ge(S["pool_summed"], n * POOL_TAPS + k + POOL_TAPS)
                    pool.tensor_tensor(pool_sum[:, :, :], grid(image(X, n)) if k == 0 else pool_sum[:, :, :],
                                       pool_part[k][:, :, :], ALU.add).then_inc(S["pool_summed"], 1)
                if ahead >= 3:
                    gather(n + 3)

            gather(0, first=True)
            gather(1)
            gather(2)
            images(pool, body)

        @block.tensor
        def _(pe):
            def turn(n, h):
                if h == 0:
                    pe.wait_ge(S["gathered"], n * 16 * TPI + 16 * TPI)
                    if not isinstance(n, int) or n > 0:
                        pe.wait_ge(S["gvar_ready"], n)
                else:
                    pe.wait_ge(S["x_added"], n * 2 + 1)
                for k in range(TPI // 2):
                    mm = pe.transpose(D[1][:, k * P:(k + 1) * P], got[h * TPI // 2 + k][:, :], env.idf[:, :])
                mm.then_inc(S["turned"], 1)

            def center(n, h):
                pe.wait_ge(S["x_added"], n * 2 + h + 1)
                if h == 0 and (not isinstance(n, int) or n > 0):
                    pe.wait_ge(S["padded_ready"], n * 2)
                pe.matmul(cent[h], env.cen[:, :], half(X, n, h), start=True, stop=True).then_inc(S["cent_ready"], 1)

            def variance(n, h):
                pe.wait_ge(S["sq_ready"], n * 2 + h + 1)
                pe.wait_ge(S["relu_ready"], n + 1)
                pe.matmul(D[0][:, halves[h]], env.avg[:, :], sq[:, halves[h]], start=True, stop=True).then_inc(S["var_ready"], 1)

            def kernels(n):
                pe.wait_ge(S["y_ready"], n * 2 + 4)
                for h in halves:
                    mm = pe.matmul(D[0][:, h], w1[:, :], y[:, h], start=True, stop=True)
                mm.then_inc(S["t_ready"], 1)

            def values(n):
                for h in halves:
                    pe.matmul(D[1][:, h], wv[:, :], y[:, h], start=True, stop=True).then_inc(S["v_ready"], 1)

            def group(n):
                pe.wait_ge(S["e2_ready"], n + 1)
                pe.wait_ge(S["padded_ready"], n * 2 + 1)
                pe.matmul(D[1][:, 0:2], gavg[:, :], t[:, 0:2], start=True, stop=True).then_inc(S["group_ready"], 1)

            def tap(n, q, k):
                if k == 0:
                    pe.wait_ge(S["split_ready"], n + 2)
                pe.wait_ge(S["product_ready"], n * TAPS + k + 1)
                dst = D[2 + (q * TAPS + k) % 2]
                for h in halves:
                    pe.matmul(dst[:, h], wa[:, k, :], ct[q][:, h], start=True, stop=False)
                    mm = pe.matmul(dst[:, h], wb[:, k, :], ct[q][:, h], start=False, stop=True)
                mm.then_inc(S["tap_ready"], 1)

            def body(n, q, ahead):
                tap(n, q, 0)
                if ahead >= 1:
                    kernels(n + 1)
                tap(n, q, 1)
                if ahead >= 1:
                    values(n + 1)
                tap(n, q, 2)
                tap(n, q, 3)
                if ahead >= 1:
                    group(n + 1)
                tap(n, q, 4)
                if ahead >= 2:
                    turn(n + 2, 0)
                tap(n, q, 5)
                if ahead >= 2:
                    center(n + 2, 0)
                    turn(n + 2, 1)
                tap(n, q, 6)
                if ahead >= 2:
                    variance(n + 2, 0)
                    center(n + 2, 1)
                tap(n, q, 7)
                if ahead >= 2:
                    variance(n + 2, 1)
                tap(n, q, 8)

            def norm(n):
                turn(n, 0)
                center(n, 0)
                turn(n, 1)
                variance(n, 0)
                center(n, 1)
                variance(n, 1)

            pe.wait_ge(S["w_loaded"], 16 * len(loads))
            pe.wait_ge(S["w_ready"], 3)
            norm(0)
            kernels(0)
            values(0)
            group(0)
            norm(1)
            images(pe, body)

        @block.scalar
        def _(act):
            act.preload_act_table_set("natural_log_exp_and_others")
            act.sem_inc(S["relu_ready"], 1)

            def square(n, h):
                act.wait_ge(S["cent_ready"], n * 2 + h + 1)
                act.activation(sq[:, halves[h]], cent[h], ACT.Square).then_inc(S["sq_ready"], 1)

            def rstd(n, h):
                j, part = n * 2 + h + 1, rs[:, halves[h]]
                act.wait_ge(S["var_ready"], j)
                act.wait_ge(S["y_ready"], j)
                act.activation(part, D[0][:, halves[h]], ACT.Ln, bias=env.eps[:, 0:1], scale=1.0).then_inc(S["ln_ready"], 1)
                act.wait_ge(S["ln_ready"], j)
                act.activation(part, part, ACT.Exp, scale=-0.5).then_inc(S["rstd_ready"], 1)

            def values(n, q):
                act.wait_ge(S["done"], n + 1)
                for h in range(2):
                    act.wait_ge(S["v_ready"], n * 2 + h + 1)
                    act.activation(xv[q][:, 1 + 16 * h:17 + 16 * h, 1:1 + SIDE], D[1][:, halves[h]].rearrange("p (h w) -> p h w", w=SIDE),
                                   ACT.Copy).then_inc(S["padded_ready"], 1)

            def relu(n, q):
                act.wait_ge(S["gvar_ready"], n + 1)
                act.activation(t[:, 8:9], t[:, 7:8], ACT.Ln, bias=env.eps[:, 1:2], scale=-1.0).then_inc(S["gln_ready"], 1)
                act.wait_ge(S["gln_ready"], n + 1)
                act.activation(t[:, 9:10], t[:, 8:9], ACT.Exp, scale=-0.5).then_inc(S["grstd_ready"], 1)
                act.wait_ge(S["coef_ready"], n + 2)
                act.wait_ge(S["split_ready"], n + 1)
                act.activation(tf[:, :], D[0][:, :], ACT.Relu, bias=t[:, 11:12], scale=t[:, 10:11])
                act.activation(ct[q][:, :], D[0][:, :], ACT.Relu, bias=t[:, 11:12], scale=t[:, 10:11]).then_inc(S["relu_ready"], 1)

            def norm(n):
                for h in range(2):
                    square(n, h)
                    rstd(n, h)

            def body(n, q, ahead):
                if ahead >= 1:
                    values(n + 1, 1 - q)
                    relu(n + 1, 1 - q)
                if ahead >= 2:
                    norm(n + 2)

            act.wait_ge(S["border"], 2)
            norm(0)
            values(0, 0)
            relu(0, 0)
            norm(1)
            images(act, body)

        @block.vector
        def _(dve):
            dve.sem_inc(S["coef_ready"], 1)
            dve.sem_inc(S["y_ready"], 2)
            dve.sem_inc(S["split_ready"], 1)
            dve.sem_inc(S["done"], 2)
            dve.sem_inc(S["product_ready"], 2)
            for q in range(2):
                dve.memset(xv[q][:, :, :], 0.0).then_inc(S["border"], 1)
            dve.wait_ge(S["w_loaded"], 16 * len(loads))
            dve.tensor_copy(wa[:, :, :], w2[:, :, :]).then_inc(S["w_ready"], 1)
            dve.memset(wb[64:128, :, :], 0.0).then_inc(S["w_ready"], 1)
            dve.wait_ge(S["w_ready"], 1)
            dve.tensor_tensor(wb[0:64, :, :], w2[0:64, :, :], wa[0:64, :, :], ALU.subtract).then_inc(S["w_ready"], 1)

            def step(n, k, ins, apart=False):
                ins.then_inc(S["steps"], 1)
                if apart:
                    wait_apart(dve, S["steps"], n * STEPS_PER_IMAGE + k + 1, env.passed["dve"])
                else:
                    dve.wait_ge(S["steps"], n * STEPS_PER_IMAGE + k + 1)

            def add_x(n, h):
                dve.wait_ge(S["turned"], n * 2 + h + 1)
                dve.tensor_tensor(half(X, n, h), D[1][:, 0:HALF], half(X, n, h), ALU.add).then_inc(S["x_added"], 1)

            def norm(n, h):
                dve.wait_ge(S["rstd_ready"], n * 2 + h + 1)
                if not isinstance(n, int) or n > 0:
                    dve.wait_ge(S["v_ready"], n * 2)
                dve.tensor_tensor(y[:, halves[h]], cent[h], rs[:, halves[h]], ALU.mult).then_inc(S["y_ready"], 1)

            def statistics(n):
                dve.wait_ge(S["t_ready"], n + 1)
                step(n, 0, dve.bn_stats(t[:, 12:18], D[0][:, halves[0]]))
                step(n, 1, dve.bn_stats(t[:, 18:24], D[0][:, halves[1]]), apart=True)
                step(n, 2, dve.bn_aggr(t[:, 0:2], t[:, 12:24].rearrange("p (n s) -> p n s", s=6)))
                dve.scalar_tensor_tensor(t[:, 1:2], t[:, 0:1], t[:, 0:1], t[:, 1:2], ALU.mult, ALU.add).then_inc(S["e2_ready"], 1)

            def group_variance(n):
                dve.wait_ge(S["group_ready"], n + 1)
                step(n, 3, dve.tensor_scalar(t[:, 4:6], D[1][:, 0:2], -1.0, None, ALU.mult))
                dve.scalar_tensor_tensor(t[:, 7:8], t[:, 4:5], t[:, 4:5], t[:, 5:6], ALU.mult, ALU.add).then_inc(S["gvar_ready"], 1)

            def coefficients(n):
                dve.wait_ge(S["grstd_ready"], n + 1)
                step(n, 4, dve.tensor_tensor(t[:, 10:11], gn[:, 0:1], t[:, 9:10], ALU.mult))
                dve.scalar_tensor_tensor(t[:, 11:12], t[:, 4:5], t[:, 10:11], gn[:, 1:2], ALU.mult, ALU.add).then_inc(S["coef_ready"], 1)

            def split(n, q):
                dve.wait_ge(S["relu_ready"], n + 2)
                dve.tensor_tensor(ct[q][64:128, :], tf[64:128, :], ct[q][64:128, :], ALU.subtract).then_inc(S["split_ready"], 1)

            def product(n, q, k):
                dve.wait_ge(S["tap_ready"], n * TAPS + k + 1)
                if k == 0:
                    dve.wait_ge(S["padded_ready"], n * 2 + 2)
                dy, dx = divmod(k, 3)
                if k < POOL_TAPS:
                    dve.wait_ge(S["pool_summed"], n * POOL_TAPS + k + 1)
                    dst = pool_part[k]
                else:
                    dst = own_sum if k == POOL_TAPS else own_part[k % 2]
                    if k == POOL_TAPS:
                        dve.wait_ge(S["done"], n + 2)
                    if k > POOL_TAPS + 2:
                        dve.wait_ge(S["summed"], n * OWN_ADDS + k - POOL_TAPS - 2)
                dve.scalar_tensor_tensor(dst[:, :, :], grid(D[2 + (q * TAPS + k) % 2][:, :]), w2b[:, k:k + 1],
                                         xv[q][:, dy:dy + SIDE, dx:dx + SIDE], ALU.add, ALU.mult).then_inc(S["product_ready"], 1)

            def add(n, k):
                dve.wait_ge(S["product_ready"], n * TAPS + k + 3)
                if k > POOL_TAPS + 1:
                    dve.wait_ge(S["summed"], n * OWN_ADDS + k - POOL_TAPS - 1)
                dve.tensor_tensor(own_sum[:, :, :], own_sum[:, :, :], own_part[k % 2][:, :, :], ALU.add).then_inc(S["summed"], 1)

            def finish(n):
                dve.wait_ge(S["summed"], n * OWN_ADDS + OWN_ADDS)
                dve.wait_ge(S["pool_summed"], n * POOL_TAPS + 2 * POOL_TAPS)
                dve.tensor_tensor(grid(image(X, n)), own_sum[:, :, :], pool_sum[:, :, :], ALU.add).then_inc(S["done"], 1)

            def body(n, q, ahead):
                for k in range(TAPS):
                    product(n, q, k)
                    if k == 1 and ahead >= 1:
                        statistics(n + 1)
                    if k == 2 and ahead >= 1:
                        group_variance(n + 1)
                    if k == 3 and ahead >= 1:
                        coefficients(n + 1)
                    if k in (4, 5) and ahead >= 2:
                        add_x(n + 2, k - 4)
                    if k == 6 and ahead >= 1:
                        split(n + 1, 1 - q)
                    if k in (6, 7) and ahead >= 2:
                        norm(n + 2, k - 6)
                    if k > POOL_TAPS + 1:
                        add(n, k - 1)
                add(n, TAPS - 1)
                finish(n)

            for h in range(2):
                add_x(0, h)
            for h in range(2):
                norm(0, h)
            statistics(0)
            group_variance(0)
            coefficients(0)
            split(0, 0)
            for h in range(2):
                add_x(1, h)
            for h in range(2):
                norm(1, h)
            images(dve, body)


def phase_experts1(nc, env, a, out):
    X = env.X
    with ExitStack() as ctx:
        names = ("w_loaded cleared cent_ready sq_ready var_ready ln_ready rs_ready xn_ready logits_ready ex_ready sel_ready "
                 "rank_ready ranked wg_ready a_ready b_ready wb_ready exp_ready softplus_ready sig_ready u_ready g_ready "
                 "h_ready wg_turned wt_ready down_done y_ready x_done steps ends_ready sent decided").split()
        S = {n: ctx.enter_context(nc.semaphore(f"e1_{n}")) for n in names}
        sb = lambda n, s, d=F32: ctx.enter_context(nc.sbuf_tensor(f"e1_{n}", s, d))
        w1, w3, w2 = (sb(n, [P, EP1, P]) for n in ("w1", "w3", "w2"))
        gate_w, gate_b = sb("gate_w", [P, E1]), sb("gate_b", [P, E1])
        before_mask = sb("before_mask", [P, G1, G1])
        sq, rs = sb("sq", [P, BLOCK]), sb("rs", [P, BLOCK])
        xn = [sb(f"xn{q}", [P, BLOCK]) for q in range(2)]
        wg, spreader = sb("wg", [P, BT, G1, 2]), sb("spreader", [P, EP1, P])
        wt = [sb(f"wt{q}", [P, BLOCK]) for q in range(2)]
        sig, u, h = ([sb(f"{n}{q}", [P, BLOCK]) for q in range(2)] for n in ("sig", "u", "h"))
        scores, biased, masked = (sb(n, [P, BT, G1, 2]) for n in ("scores", "biased", "masked"))
        group = sb("group", [P, BT, G1])
        above, tie = sb("above", [P, BT, G1, G1]), sb("tie", [P, BT, G1, G1])
        place, selected = sb("place", [P, BT, G1]), sb("selected", [P, BT, G1])
        sel = sb("sel", [P, BT, G1], BF16)
        keep, total, taken, taken_before = sb("keep", [P, BT, G1]), sb("total", [P, BT]), sb("taken", [P, G1]), sb("taken_before", [P, G1])
        least = sb("least", [1, 2])
        ends = sb("ends", [1, 3], I32)
        A = [env.psum[q][:, 0:HALF] for q in range(2)]
        B = [env.psum[q][:, HALF:PIX] for q in range(2)]
        wb, y = env.psum[2][:, 0:HALF], env.psum[2][:, HALF:PIX]
        cent, var = env.psum[3][:, 0:HALF], env.psum[3][:, HALF:PIX]
        logits = var[:, 0:BT * E1]
        rank = var[:, 64:64 + BT * G1].rearrange("p (s g) -> p s g", g=G1)
        tot = var[:, 96:96 + G1]
        loads = [(w1[:, :, :], a["w1_moe1"]), (w3[:, :, :], a["w3_moe1"]), (w2[:, :, :], a["w2_moe1"]),
                 (gate_w[:, :], a["gate_w"]), (gate_b[:, :], a["gate_b"].broadcast_to([P, E1])),
                 (spreader[:, :, :], a["k_spread"]),
                 (before_mask[:, :, :], a["k_before"].broadcast_to([P, G1, G1]))]
        block = ctx.enter_context(nc.Block())

        def cols(buf, n):
            return buf[:, bass.ds(n * BLOCK, BLOCK)]

        def blocks(engine, body, last=None):
            with engine.Fori(0, 2) as r:
                engine.wait_ge(S["ends_ready"], r + 1)
                end = engine.value_load(ends[0:1, bass.ds(r, 1)], min_val=FIRST_BLOCKS // 2, max_val=BLOCKS // 2)
                with engine.Fori(r * (FIRST_BLOCKS // 2), end) as i:
                    for q in range(2):
                        body(i * 2 + q, q)
                if last is not None:
                    last(r)

        @block.sync
        def _(sp):
            for dst, src in loads:
                sp.dma_start(dst, src).then_inc(S["w_loaded"], 16)

            def send(n, q):
                sp.wait_ge(S["x_done"], n + 2)
                sp.dma_start(cols(out, n), cols(X, n)).then_inc(S["sent"], 16)
                wait_apart(sp, S["sent"], n * 16 + 16, env.passed["sp"])
            blocks(sp, send)

        @block.tensor
        def _(pe):
            def center(n):
                pe.matmul(cent, env.cen[:, :], cols(X, n % BLOCKS), start=True, stop=True).then_inc(S["cent_ready"], 1)

            def variance(n):
                pe.wait_ge(S["sq_ready"], n + 1)
                pe.wait_ge(S["wt_ready"], n + 1)
                pe.matmul(var, env.avg[:, :], sq[:, :], start=True, stop=True).then_inc(S["var_ready"], 1)

            def gate(n, q):
                pe.wait_ge(S["xn_ready"], n + 1)
                for s in range(BT):
                    mm = pe.matmul(logits[:, s * E1:(s + 1) * E1], xn[q][:, s * P:(s + 1) * P], gate_w[:, :],
                                   start=True, stop=True)
                mm.then_inc(S["logits_ready"], 1)

            def ranks(n):
                pe.wait_ge(S["sel_ready"], n + 1)
                for s in range(BT):
                    for before in range(s):
                        pe.matmul(rank[:, s, :], env.ones16[:, :], sel[:, before, :], start=(before == 0), stop=False)
                    pe.matmul(rank[:, s, :], env.ltri[:, :], sel[:, s, :], start=(s == 0), stop=True)
                for s in range(BT):
                    mm = pe.matmul(tot, env.ones16[:, :], sel[:, s, :], start=(s == 0), stop=(s == BT - 1))
                mm.then_inc(S["rank_ready"], 1)

            def turn_weights(n):
                pe.wait_ge(S["wg_ready"], n + 1)
                for s in range(BT):
                    mm = pe.transpose(var[0:E1, s * P:(s + 1) * P], wg[:, s, :, :].rearrange("p g e -> p (g e)"), env.idf[:, :])
                mm.then_inc(S["wg_turned"], 1)

            def up(n, q, k):
                pe.wait_ge(S["h_ready"], n * EP1 + k + 1)
                if k == 0:
                    pe.wait_ge(S["xn_ready"], n + 1)
                pe.matmul(A[k % 2], w1[:, k, :], xn[q][:, :], start=True, stop=True).then_inc(S["a_ready"], 1)
                pe.matmul(B[k % 2], w3[:, k, :], xn[q][:, :], start=True, stop=True).then_inc(S["b_ready"], 1)

            def spread(n, q, k):
                if k == 0:
                    pe.wait_ge(S["wt_ready"], n + 2)
                pe.wait_ge(S["h_ready"], n * EP1 + k + 2)
                pe.matmul(wb, spreader[:, k, :], wt[q][:, :], start=True, stop=True).then_inc(S["wb_ready"], 1)

            def down(n, k):
                pe.wait_ge(S["h_ready"], n * EP1 + k + 3)
                if k == 0:
                    pe.wait_ge(S["x_done"], n + 1)
                mm = pe.matmul(y, w2[:, k, :], h[k % 2][:, :], start=(k == 0), stop=(k == EP1 - 1))
                mm.then_inc(S["down_done"], 1)

            def body(n, q):
                for k in range(EP1):
                    up(*((n, q, k + 1) if k + 1 < EP1 else (n + 1, 1 - q, 0)))
                    if k == 0:
                        center(n + 1)
                    if k == 1:
                        variance(n + 1)
                    if k == 3:
                        gate(n + 1, 1 - q)
                    if k == 5:
                        ranks(n + 1)
                    if k == 7:
                        turn_weights(n + 1)
                    down(n, k)
                    spread(*((n, q, k + 1) if k + 1 < EP1 else (n + 1, 1 - q, 0)))

            pe.wait_ge(S["w_loaded"], 16 * len(loads))
            center(0)
            variance(0)
            gate(0, 0)
            ranks(0)
            turn_weights(0)
            up(0, 0, 0)
            spread(0, 0, 0)
            blocks(pe, body)

        @block.scalar
        def _(act):
            act.preload_act_table_set("natural_log_exp_and_others")

            def square(n):
                act.wait_ge(S["cent_ready"], n + 1)
                act.activation(sq[:, :], cent, ACT.Square).then_inc(S["sq_ready"], 1)

            def rstd(n):
                act.wait_ge(S["var_ready"], n + 1)
                act.activation(rs[:, :], var, ACT.Ln, bias=env.eps[:, 1:2], scale=1.0).then_inc(S["ln_ready"], 1)
                act.wait_ge(S["ln_ready"], n + 1)
                act.activation(rs[:, :], rs[:, :], ACT.Exp, scale=-0.5).then_inc(S["rs_ready"], 1)

            def gate(n):
                act.wait_ge(S["logits_ready"], n + 1)
                act.wait_ge(S["ranked"], n + 1)
                act.activation(scores[:, :, :, :].rearrange("p s g e -> p (s g e)"), logits, ACT.Exp, scale=-1.0)\
                    .then_inc(S["ex_ready"], 1)

            def take_weights(n, q):
                act.wait_ge(S["wg_turned"], n + 1)
                act.activation(wt[q][0:E1, :], var[0:E1, :], ACT.Copy).then_inc(S["wt_ready"], 1)

            def sigmoid(n, k):
                j, s = n * EP1 + k + 1, sig[k % 2]
                act.wait_ge(S["a_ready"], j)
                act.activation(s[:, :], A[k % 2], ACT.Exp, scale=-1.0).then_inc(S["exp_ready"], 1)
                act.wait_ge(S["exp_ready"], j)
                act.activation(s[:, :], s[:, :], ACT.Ln, bias=env.ones32[:, 0:1], scale=1.0).then_inc(S["softplus_ready"], 1)
                act.wait_ge(S["softplus_ready"], j)
                act.activation(s[:, :], s[:, :], ACT.Exp, scale=-1.0).then_inc(S["sig_ready"], 1)

            def body(n, q):
                for k in range(EP1):
                    sigmoid(n, k)
                    if k == 1:
                        square(n + 1)
                    if k == 2:
                        rstd(n + 1)
                    if k == 4:
                        gate(n + 1)
                take_weights(n + 1, 1 - q)

            act.sem_inc(S["wt_ready"], 1)
            square(0)
            rstd(0)
            gate(0)
            act.wait_ge(S["cleared"], 2)
            take_weights(0, 0)
            blocks(act, body)

        @block.vector
        def _(dve):
            dve.sem_inc(S["ranked"], 1)
            dve.sem_inc(S["h_ready"], 2)
            dve.sem_inc(S["x_done"], 1)
            dve.sem_inc(S["down_done"], 2)
            wide = lambda ap: ap.unsqueeze(3).broadcast_to([P, BT, G1, 2])

            def step(n, k, ins):
                ins.then_inc(S["steps"], 1)
                dve.wait_ge(S["steps"], n * STEPS1 + k + 1)

            def norm(n, q):
                dve.wait_ge(S["rs_ready"], n + 1)
                dve.tensor_tensor(xn[q][:, :], cent, rs[:, :], ALU.mult).then_inc(S["xn_ready"], 1)

            def select(n):
                dve.wait_ge(S["ex_ready"], n + 1)
                f = lambda t: t[:, :, :, :].rearrange("p s g e -> p (s g e)")
                step(n, 0, dve.tensor_scalar(f(scores), f(scores), 1.0, None, ALU.add))
                step(n, 1, dve.reciprocal(f(scores), f(scores)))
                step(n, 2, dve.tensor_tensor(biased[:, :, :, :].rearrange("p s g e -> p s (g e)"),
                                             scores[:, :, :, :].rearrange("p s g e -> p s (g e)"),
                                             gate_b[:, :].unsqueeze(1).broadcast_to([P, BT, E1]), ALU.add))
                step(n, 3, dve.tensor_tensor(group[:, :, :], biased[:, :, :, 0], biased[:, :, :, 1], ALU.add))
                own = group[:, :, :].unsqueeze(3).broadcast_to([P, BT, G1, G1])
                other = group[:, :, :].unsqueeze(2).broadcast_to([P, BT, G1, G1])
                step(n, 4, dve.tensor_tensor(above[:, :, :, :], other, own, ALU.is_gt))
                step(n, 5, dve.tensor_tensor(tie[:, :, :, :], other, own, ALU.is_equal))
                flat = lambda t: t[:, :, :, :].rearrange("p s g h -> p s (g h)")
                step(n, 6, dve.tensor_tensor(flat(tie), flat(tie), before_mask[:, :, :].rearrange("p g h -> p (g h)")
                                             .unsqueeze(1).broadcast_to([P, BT, G1 * G1]), ALU.mult))
                step(n, 7, dve.tensor_tensor(flat(above), flat(above), flat(tie), ALU.add))
                step(n, 8, dve.tensor_reduce(place[:, :, :], above[:, :, :, :], AX.X, ALU.add))
                step(n, 9, dve.tensor_scalar(selected[:, :, :], place[:, :, :], float(TOP_G), None, ALU.is_lt))
                dve.tensor_copy(sel[:, :, :], selected[:, :, :]).then_inc(S["sel_ready"], 1)

            def weigh(n):
                step(n, 10, dve.tensor_tensor(masked[:, :, :, :], scores[:, :, :, :], wide(selected[:, :, :]), ALU.mult))
                step(n, 11, dve.tensor_reduce(total[:, :], masked[:, :, :, :].rearrange("p s g e -> p s (g e)"), AX.X, ALU.add))
                step(n, 12, dve.reciprocal(total[:, :], total[:, :]))
                step(n, 13, dve.tensor_scalar(total[:, :], total[:, :], SCALE1, None, ALU.mult))
                dve.wait_ge(S["rank_ready"], n + 1)
                step(n, 14, dve.tensor_tensor(keep[:, :, :], rank, taken[:, :].unsqueeze(1).broadcast_to([P, BT, G1]), ALU.add))
                step(n, 15, dve.tensor_copy(taken_before[:, :], taken[:, :]))
                step(n, 16, dve.tensor_tensor(taken[:, :], taken[:, :], tot, ALU.add))
                step(n, 17, dve.tensor_scalar(keep[:, :, :], keep[:, :, :], float(CAP), None, ALU.is_lt))
                step(n, 18, dve.tensor_tensor(keep[:, :, :], keep[:, :, :], total[:, :].unsqueeze(2).broadcast_to([P, BT, G1]), ALU.mult))
                dve.tensor_tensor(wg[:, :, :, :], masked[:, :, :, :], wide(keep[:, :, :]), ALU.mult).then_inc(S["wg_ready"], 1)
                dve.sem_inc(S["ranked"], 1)

            def pair(n, k):
                j, q = n * EP1 + k + 1, k % 2
                dve.wait_ge(S["sig_ready"], j)
                dve.tensor_tensor(u[q][:, :], sig[q][:, :], A[q], ALU.mult).then_inc(S["u_ready"], 1)
                dve.wait_ge(S["u_ready"], j)
                dve.wait_ge(S["b_ready"], j)
                dve.tensor_tensor(u[q][:, :], u[q][:, :], B[q], ALU.mult).then_inc(S["g_ready"], 1)
                dve.wait_ge(S["g_ready"], j)
                dve.wait_ge(S["wb_ready"], j)
                dve.wait_ge(S["down_done"], j)
                dve.tensor_tensor(h[q][:, :], u[q][:, :], wb, ALU.mult).then_inc(S["h_ready"], 1)

            def body(n, q):
                for k in range(EP1):
                    pair(n, k)
                    if k == 2:
                        norm(n + 1, 1 - q)
                    if k == 4:
                        select(n + 1)
                    if k == 6:
                        weigh(n + 1)
                dve.wait_ge(S["down_done"], n * EP1 + EP1 + 2)
                dve.tensor_tensor(cols(X, n), cols(X, n), y, ALU.add).then_inc(S["x_done"], 1)

            def decide(r):
                room = lambda j, ins: (ins.then_inc(S["decided"], 1), dve.wait_ge(S["decided"], r * 2 + j))
                room(2, dve.tensor_reduce(least[0:1, 0:1], taken_before[0:1, :], AX.X, ALU.min))
                room(3, dve.tensor_scalar(least[0:1, 1:2], least[0:1, 0:1], float(CAP), float((BLOCKS - FIRST_BLOCKS) // 2),
                                          ALU.is_lt, ALU.mult))
                dve.tensor_scalar(ends[0:1, bass.ds(r + 1, 1)], least[0:1, 1:2], float(FIRST_BLOCKS // 2), None, ALU.add)\
                    .then_inc(S["ends_ready"], 1)

            for q in range(2):
                dve.memset(wt[q][:, :], 0.0).then_inc(S["cleared"], 1)
            dve.memset(taken[:, :], 0.0).then_inc(S["decided"], 1)
            dve.wait_ge(S["decided"], 1)
            dve.wait_ge(S["w_loaded"], 16 * len(loads))
            norm(0, 0)
            select(0)
            weigh(0)
            dve.memset(ends[0:1, 0:1], FIRST_BLOCKS // 2).then_inc(S["ends_ready"], 1)
            blocks(dve, body, last=decide)


class Env:
    pass


def build(nc, a, out):
    env = Env()
    with ExitStack() as ctx:
        sb = lambda n, s, d=F32: ctx.enter_context(nc.sbuf_tensor(n, s, d))
        env.X = sb("X", [P, TOKENS])
        env.cen, env.avg, env.idf, env.ltri32 = sb("cen", [P, P]), sb("avg", [P, P]), sb("idf", [P, P]), sb("ltri32", [P, P])
        env.ltri, env.ones16, env.idb = sb("ltri", [P, P], BF16), sb("ones16", [P, P], BF16), sb("idb", [P, P], BF16)
        env.ones32 = sb("ones32", [P, 1])
        env.small = sb("small", [P, SMALL])
        env.mask_group = env.small[:, 0:16]
        env.rev = env.small[:, 16:24]
        env.pair_no = env.small[:, 24:24 + PAIRS]
        env.lane = env.small[:, 52:53]
        env.par, env.eps = sb("par", [P, 9]), sb("eps", [P, 3])
        env.slot, env.starts = sb("slot", [P, TILES], I32), sb("starts", [1, PAIRS + 2], I32)
        env.finals = sb("finals", [1, PAIRS], I32)
        env.zero = sb("zero_row", [P, ROW])
        env.passed = {name: ctx.enter_context(nc.semaphore(f"passed_{name}")) for name in ("pool", "pe", "sp", "dve")}
        env.cleared = ctx.enter_context(nc.semaphore("rows_cleared"))
        env.bnst = sb("bnst", [P, IMAGES * 12])
        env.psum = [ctx.enter_context(nc.psum_tensor(f"ps{i}", [P, 2 * HALF], F32)) for i in range(4)]
        xg = nc.dram_tensor("dispatched", (CLEARED, ROW), F32, kind="Internal").ap()
        yg = nc.dram_tensor("expert_out", ((MAX_TILES + 1) * SLOT, C), F32, kind="Internal").ap()
        env.xg, env.yg = xg, yg
        setup_constants(nc, env, a)
        with ExitStack() as first:
            sb1 = lambda n, s, d=F32: first.enter_context(nc.sbuf_tensor(n, s, d))
            env.Y = sb1("Y", [P, TOKENS])
            env.rstd, env.shift, env.gates = sb1("rstd", [P, TILES]), sb1("shift", [P, TILES]), sb1("gates", [P, 2 * TILES])
            env.logit, env.rowst = sb1("logit", [P, TILES * E0]), sb1("rowst", [P, TILES * 6])
            phase_norm0(nc, env, a, xg)
            with nc.sbuf_tensor("CONV", [P, TOKENS], BF16) as CONV:
                env.CONV = CONV
                phase_conv(nc, env, a)
                phase_tokens0(nc, env, a)
            phase_route0(nc, env)
            phase_dispatch(nc, env)
        with ExitStack() as second:
            sb2 = lambda n, s, d=F32: second.enter_context(nc.sbuf_tensor(n, s, d))
            env.weights = sb2("weights", [P, E0 * WCOLS], F16)
            split_weights0(nc, env, a)
            phase_experts0(nc, env, a)
        phase_involution(nc, env, a, out)
        phase_experts1(nc, env, a, out)


SMALL = 53


def constants():
    small = np.zeros((P, SMALL), np.float32)
    small[np.arange(P), np.arange(P) // GROUP_IN] = 1.0
    small[:, 16:24] = E0 - np.arange(E0)
    small[:, 24:24 + PAIRS] = np.arange(PAIRS)
    small[:, 52] = np.arange(P)
    return {
        "k_center": np.eye(P, dtype=np.float32) - np.float32(1 / C),
        "k_average": np.full((P, P), 1 / C, np.float32),
        "k_identity": np.eye(P, dtype=np.float32),
        "k_lower": np.triu(np.ones((P, P), np.float32), 1),
        "k_small": small,
        "k_groups": np.where((np.arange(P)[:, None] < 64) & (np.arange(P)[:, None] // G8 == np.arange(P)[None, :] % 64 // G8),
                             np.float32(1 / G8), np.float32(0)),
        "k_before": np.tril(np.ones((G1, G1), np.float32), -1).reshape(1, G1, G1),
        "k_spread": (np.arange(P)[:, None, None] == 2 * np.arange(EP1)[None, :, None] + np.arange(P)[None, None, :] // M1)
                    .astype(np.float32),
        "k_pairs": np.array(PAIR_LIST + PAIR_LIST[-1:], np.int32).reshape(1, 2 * PAIRS + 2),
    }


def layout(i):
    i = {k: np.asarray(v) for k, v in i.items()}
    a = dict(constants())
    a["x"] = i["x"].transpose(1, 0, 2, 3).reshape(C, IMAGES, PIX)
    a["chan"] = np.stack([i["L0_conv_bn1_gamma"], i["L0_conv_bn1_beta"], i["L0_conv_bn2_gamma"],
                          i["L0_conv_bn2_beta"], i["L0_conv_prelu_a"]], axis=1)
    a["conv_w"] = i["L0_conv_conv_w"].reshape(C, GROUP_IN * TAPS)
    a["w_router"] = i["L0_ffn_W_router"]
    w1 = i["L0_ffn_W1"]
    w2 = i["L0_ffn_W2"].reshape(E0, KM, P, C).transpose(0, 2, 1, 3).reshape(E0, P, H0)
    a["w_moe0"] = np.concatenate([w1, w2], axis=2)
    a["b1"] = i["L0_ffn_b1"].reshape(E0, KM, P).transpose(2, 0, 1).reshape(P, E0 * KM)
    a["b2"] = i["L0_ffn_b2"].reshape(1, E0 * C)
    d4 = lambda w: w[:, :, np.array(PERMS)].transpose(1, 3, 0, 2).reshape(C, -1)
    a["w_v"] = d4(i["L1_conv_w_v"])
    a["w1_d4"] = np.concatenate([d4(i["L1_conv_w1"])] * 2, axis=1)
    a["gn"] = np.concatenate([np.stack([i["L1_conv_gn_gamma"], i["L1_conv_gn_beta"]], axis=1)] * 2)
    base = np.arange(TAPS).reshape(3, 3)
    source = np.stack([base, np.rot90(base, 1), np.rot90(base, 2), np.rot90(base, 3), np.rot90(base.T, 3),
                       np.rot90(base.T, 2), np.rot90(base.T, 1), base.T]).reshape(G8, TAPS)
    w2 = np.zeros((2, CMID, G8, TAPS, C // G8, G8), np.float32)
    for g in range(G8):
        w2[:, :, g, :, :, g] = i["L1_conv_w2"][source[g]].T[None, :, :, None]
    a["w2_taps"] = w2.reshape(P, TAPS, P)
    a["b2_taps"] = np.tile(i["L1_conv_b2"][source], (C // G8, 1))
    a["w1_moe1"] = i["L1_ffn_w1"].transpose(1, 0, 2).reshape(P, EP1, P)
    a["w3_moe1"] = i["L1_ffn_w3"].transpose(1, 0, 2).reshape(P, EP1, P)
    a["w2_moe1"] = i["L1_ffn_w2"].reshape(EP1, P, C).transpose(1, 0, 2)
    a["gate_w"] = i["L1_ffn_gate_w"].T
    a["gate_b"] = i["L1_ffn_gate_b"].reshape(1, E1)
    return {k: np.ascontiguousarray(v) for k, v in a.items()}


def kernel(**inputs):
    import concourse.bacc as bacc
    from concourse.bass_utils import run_bass_kernel_spmd
    arrays = layout(inputs)
    nc = bacc.Bacc("TRN2", target_bir_lowering=False, num_devices=1)
    a = {name: nc.dram_tensor(name, value.shape, mybir.dt.from_np(value.dtype), kind="ExternalInput").ap()
         for name, value in arrays.items()}
    out = nc.dram_tensor("out", (P, TOKENS), F32, kind="ExternalOutput").ap()
    build(nc, a, out)
    result = run_bass_kernel_spmd(nc, [arrays], core_ids=[0])
    return result.results[0]["out"].reshape(C, IMAGES, SIDE, SIDE).transpose(1, 0, 2, 3)
```

```python
from contextlib import ExitStack, contextmanager

import numpy as np

import concourse.bass as bass
from concourse import mybir
from concourse.alu_op_type import AluOpType as ALU

ACT = mybir.ActivationFunctionType
AX = mybir.AxisListType
F32, F16, BF16 = mybir.dt.float32, mybir.dt.float16, mybir.dt.bfloat16
I32, U32 = mybir.dt.int32, mybir.dt.uint32

IMAGES, C, SIDE = 16, 128, 32
PIX = SIDE * SIDE
TOKENS = IMAGES * PIX
HALF = 512
P = 128
TILES = TOKENS // P
FLIGHT = 4
TPI = PIX // P
PAD = SIDE + 2
GROUP_IN = 8
TAPS = 9
E0, H0 = 8, 512
KM = H0 // P
PAIRS = E0 * (E0 - 1) // 2
SLOT = 256
SUB = SLOT // P
MAX_TILES = TOKENS // SLOT + PAIRS
ROW = C + 2
CMID, G8 = 8, 8
E1, M1, CAP = 16, 64, 256
TOP_G = 4
SCALE1 = 2.5
G1 = 8
BLOCK = 512
BT, BLOCKS = BLOCK // P, TOKENS // BLOCK
FIRST_BLOCKS = 4
FIRST_IMAGES = FIRST_BLOCKS * BLOCK // PIX
STEPS1 = 25
CLEARED1 = 3
UNIT1 = BLOCK // 2
WSCALE = 32.0
POOL_TAPS = 4
OWN_ADDS = TAPS - POOL_TAPS - 1
STEPS_PER_IMAGE = 5
WCOLS = 4 * H0 + C + 2 * KM
EPS_C, EPS = 1e-6, 1e-5
CLEARED = (MAX_TILES + 2) * SLOT
CLEARS = 4
PERMS = ((0, 1, 2, 3, 4, 5, 6, 7), (3, 0, 1, 2, 5, 6, 7, 4), (2, 3, 0, 1, 6, 7, 4, 5), (1, 2, 3, 0, 7, 4, 5, 6),
         (4, 5, 6, 7, 0, 1, 2, 3), (5, 6, 7, 4, 3, 0, 1, 2), (6, 7, 4, 5, 2, 3, 0, 1), (7, 4, 5, 6, 1, 2, 3, 0))
PAIR_LIST = [(a, b) for a in range(E0) for b in range(a + 1, E0)]


@contextmanager
def by_two(engine, start, end):
    with engine.Fori(start // 2, end // 2) as i:
        yield i * 2


@contextmanager
def maybe_loop(engine, start, end):
    with engine.If(start < end):
        with engine.Fori(start, end) as i:
            yield i


def wait_apart(engine, sem, value, passed):
    engine.wait_ge(sem, value)
    engine.sem_inc(passed, 1)


def image(buf, n):
    return buf[:, bass.ds(n * PIX, PIX)]


def setup_constants(nc, env, a):
    with ExitStack() as ctx:
        got = ctx.enter_context(nc.semaphore("const_loaded"))
        cast = ctx.enter_context(nc.semaphore("const_cast"))
        block = ctx.enter_context(nc.Block())
        loads = [(env.cen[:, :], a["k_center"]), (env.avg[:, :], a["k_average"]), (env.idf[:, :], a["k_identity"]),
                 (env.small[:, :], a["k_small"]), (env.par[:, 0:5], a["chan"]),
                 (env.ltri32[:, :], a["k_lower"])]

        @block.sync
        def _(sp):
            for dst, src in loads:
                sp.dma_start(dst, src).then_inc(got, 16)

        @block.vector
        def _(dve):
            dve.wait_ge(got, 16 * len(loads))
            dve.tensor_copy(env.ltri[:, :], env.ltri32[:, :]).then_inc(cast, 1)
            dve.memset(env.ones16[:, :], 1.0).then_inc(cast, 1)
            dve.tensor_copy(env.idb[:, :], env.idf[:, :]).then_inc(cast, 1)
            dve.memset(env.eps[:, 0:1], EPS_C).then_inc(cast, 1)
            dve.memset(env.eps[:, 1:2], EPS).then_inc(cast, 1)
            dve.memset(env.eps[:, 2:3], 0.0).then_inc(cast, 1)
            dve.memset(env.ones32[:, :], 1.0).then_inc(cast, 1)
            dve.wait_ge(cast, 7)


def chain(engine, sem):
    count = [0]

    def link(instruction):
        count[0] += 1
        instruction.then_inc(sem, 1)
        engine.wait_ge(sem, count[0])
    return link


def phase_norm0(nc, env, a, zero_rows):
    X, Y = env.X, env.Y
    with ExitStack() as ctx:
        sem = lambda n: ctx.enter_context(nc.semaphore(n))
        loaded = [sem(f"n0_loaded{q}") for q in range(2)]
        cent_ready, sq_ready, var_ready = sem("n0_cent_ready"), sem("n0_sq_ready"), sem("n0_var_ready")
        ln_ready, rstd_ready, norm_free = sem("n0_ln_ready"), sem("n0_rstd_ready"), sem("n0_norm_free")
        sq_free = sem("n0_sq_free")
        zeroed, stats = sem("n0_zeroed"), sem("n0_stats")
        sq = [ctx.enter_context(nc.sbuf_tensor(f"n0_sq{q}", [P, PIX], F32)) for q in range(2)]
        rs = [ctx.enter_context(nc.sbuf_tensor(f"n0_rs{q}", [P, PIX], F32)) for q in range(2)]
        cent, var = env.psum[0:2], env.psum[2:4]
        block = ctx.enter_context(nc.Block())

        @block.sync
        def _(sp):
            for q in range(2):
                sp.dma_start(image(X, q), a["x"][:, q, :]).then_inc(loaded[q], 16)
            with by_two(sp, 2, IMAGES) as n:
                for q in range(2):
                    sp.wait_ge(loaded[q], n * 8)
                    sp.dma_start(image(X, n + q), a["x"][:, bass.ds(n + q, 1), :]).then_inc(loaded[q], 16)

        @block.gpsimd
        def _(pool):
            pool.memset(env.zero[:, :], 0.0).then_inc(zeroed, 1)
            pool.wait_ge(zeroed, 1)
            rows = CLEARED // P // CLEARS
            for q in range(2):
                pool.wait_ge(loaded[q], IMAGES * 8)
            for i in range(CLEARS):
                pool.dma_start(zero_rows[i * P * rows:(i + 1) * P * rows, :].rearrange("(p r) c -> p r c", p=P),
                               env.zero[:, :].unsqueeze(1).broadcast_to([P, rows, ROW])).then_inc(env.cleared, 16)

        @block.tensor
        def _(pe):
            def center(n, q):
                pe.wait_ge(loaded[q], (n - q) * 8 + 16)
                pe.wait_ge(norm_free, n + 1)
                for h in range(2):
                    mm = pe.matmul(cent[q][:, h * HALF:(h + 1) * HALF], env.cen[:, :],
                                   X[:, bass.ds(n * PIX + h * HALF, HALF)], start=True, stop=True)
                mm.then_inc(cent_ready, 1)

            def variance(n, q):
                pe.wait_ge(sq_ready, n + 1)
                for h in range(2):
                    mm = pe.matmul(var[q][:, h * HALF:(h + 1) * HALF], env.avg[:, :],
                                   sq[q][:, h * HALF:(h + 1) * HALF], start=True, stop=True)
                mm.then_inc(var_ready, 1)

            center(0, 0)
            center(1, 1)
            variance(0, 0)
            with by_two(pe, 0, IMAGES - 2) as n:
                for q in range(2):
                    variance(n + q + 1, 1 - q)
                    center(n + q + 2, q)
            variance(IMAGES - 1, 1)

        @block.scalar
        def _(act):
            def square(n, q):
                act.wait_ge(cent_ready, n + 1)
                act.activation(sq[q][:, :], cent[q][:, :], ACT.Square).then_inc(sq_ready, 1)

            def rstd(n, q):
                act.wait_ge(var_ready, n + 1)
                act.wait_ge(norm_free, n + 1)
                act.activation(rs[q][:, :], var[q][:, :], ACT.Ln, bias=env.eps[:, 0:1], scale=1.0).then_inc(ln_ready, 1)
                act.wait_ge(ln_ready, n + 1)
                act.activation(rs[q][:, :], rs[q][:, :], ACT.Exp, scale=-0.5).then_inc(rstd_ready, 1)

            act.preload_act_table_set("natural_log_exp_and_others")
            square(0, 0)
            square(1, 1)
            rstd(0, 0)
            with by_two(act, 0, IMAGES - 2) as n:
                for q in range(2):
                    rstd(n + q + 1, 1 - q)
                    square(n + q + 2, q)
            rstd(IMAGES - 1, 1)

        @block.vector
        def _(dve):
            dve.sem_inc(norm_free, 2)
            with by_two(dve, 0, IMAGES) as n:
                for q in range(2):
                    dve.wait_ge(rstd_ready, n + q + 1)
                    dve.tensor_tensor(image(Y, n + q), cent[q][:, :], rs[q][:, :], ALU.mult).then_inc(norm_free, 1)
                    dve.wait_ge(norm_free, n + q + 3)
                    for h in range(2):
                        dve.bn_stats(env.bnst[:, bass.ds((n + q) * 12 + h * 6, 6)],
                                     Y[:, bass.ds((n + q) * PIX + h * HALF, HALF)]).then_inc(stats, 1)
            dve.wait_ge(stats, 2 * IMAGES)


def phase_conv(nc, env, a):
    Y, CONV, par = env.Y, env.CONV, env.par
    with ExitStack() as ctx:
        sem = lambda n: ctx.enter_context(nc.semaphore(n))
        sb = lambda n, s, d=F32: ctx.enter_context(nc.sbuf_tensor(n, s, d))
        w_loaded, w_sign, w_spread, w_turned, w_ready = (sem(f"cv_w_{x}") for x in ("loaded", "sign", "spread", "turned", "ready"))
        var1, rs1, coef1, border = sem("cv_var1"), sem("cv_rs1"), sem("cv_coef1"), sem("cv_border")
        sign_ready, conv_ready, evac_free, stats, steps, asteps = (sem(f"cv_{x}") for x in
            ("sign_ready", "conv_ready", "evac_free", "stats", "steps", "asteps"))
        var2, rs2 = sem("cv_var2"), sem("cv_rs2")
        cw, sg, dev, mag = sb("cv_w", [P, GROUP_IN * TAPS]), sb("cv_sg", [P, GROUP_IN * TAPS]), sb("cv_dev", [P, GROUP_IN * TAPS]), sb("cv_mag", [P, GROUP_IN * TAPS])
        spread = sb("cv_spread", [P, TAPS, P], BF16)
        taps = sb("cv_taps", [P, TAPS, P], BF16)
        t = sb("cv_t", [P, 24])
        padded = [sb(f"cv_padded{q}", [P, PAD, PAD], BF16) for q in range(2)]
        col = lambda k: t[:, k:k + 1]
        mean1, vari1, lnv1, rstd1 = col(0), col(1), col(2), col(3)
        wsum, wmean, wss, wabs, wln, wrs, sw = (col(k) for k in range(4, 11))
        mean2, vari2, sv, lnv2, rstd2, tmp = (col(k) for k in range(12, 18))
        A1, B1 = par[:, 5:6], par[:, 6:7]
        A2, B2 = par[:, 7:8], par[:, 8:9]
        g1, b1, g2, b2 = (par[:, k:k + 1] for k in range(4))
        block = ctx.enter_context(nc.Block())

        @block.sync
        def _(sp):
            sp.dma_start(cw[:, :], a["conv_w"]).then_inc(w_loaded, 16)

        @block.vector
        def _(dve):
            link = chain(dve, steps)
            for q in range(2):
                dve.memset(padded[q][:, :, :], 0.0).then_inc(border, 1)
            dve.bn_aggr(t[:, 0:2], env.bnst[:, :].rearrange("p (n s) -> p n s", s=6)).then_inc(var1, 1)
            dve.wait_ge(w_loaded, 16)
            n = GROUP_IN * TAPS
            link(dve.reduce_sum(wsum, cw[:, :], AX.X))
            link(dve.tensor_scalar(wmean, wsum, 1.0 / n, None, ALU.mult))
            link(dve.tensor_scalar(dev[:, :], cw[:, :], wmean, None, ALU.subtract))
            link(dve.tensor_tensor(mag[:, :], dev[:, :], dev[:, :], ALU.mult))
            link(dve.reduce_sum(wss, mag[:, :], AX.X))
            link(dve.scalar_tensor_tensor(mag[:, :], dev[:, :], -1.0, dev[:, :], ALU.mult, ALU.max))
            link(dve.reduce_sum(wabs, mag[:, :], AX.X))
            dve.wait_ge(w_sign, 1)
            for k in range(TAPS):
                dve.tensor_tensor(
                    spread[:, k, :].rearrange("p (g i) -> p g i", i=GROUP_IN),
                    sg[:, :].rearrange("p (i k) -> p k i", k=TAPS)[:, k:k + 1, :].broadcast_to([P, C // GROUP_IN, GROUP_IN]),
                    env.mask_group[:, :].unsqueeze(2).broadcast_to([P, C // GROUP_IN, GROUP_IN]),
                    ALU.mult).then_inc(w_spread, 1)
            dve.wait_ge(rs1, 1)
            link(dve.tensor_tensor(A1, g1, rstd1, ALU.mult))
            link(dve.tensor_tensor(tmp, mean1, A1, ALU.mult))
            dve.tensor_tensor(B1, b1, tmp, ALU.subtract).then_inc(coef1, 1)
            dve.wait_ge(rs1, 2)
            link(dve.tensor_scalar(wrs, wrs, wabs, 1.0 / n, ALU.mult, ALU.mult))
            for half in range(2):
                dve.wait_ge(w_turned, half + 1)
                k0, k1 = (0, 8) if half == 0 else (8, TAPS)
                dve.tensor_copy(taps[:, k0:k1, :], env.psum[half][:, 0:(k1 - k0) * P]
                                .rearrange("p (k o) -> p k o", o=P)).then_inc(w_ready, 1)
            with dve.Fori(0, IMAGES) as n_:
                dve.wait_ge(evac_free, n_ + 3)
                for h in range(2):
                    dve.bn_stats(env.bnst[:, bass.ds(n_ * 12 + h * 6, 6)],
                                 CONV[:, bass.ds(n_ * PIX + h * HALF, HALF)]).then_inc(stats, 1)
            dve.wait_ge(stats, 2 * IMAGES)
            link(dve.bn_aggr(t[:, 12:14], env.bnst[:, :].rearrange("p (n s) -> p n s", s=6)))
            link(dve.tensor_tensor(sv, vari2, wrs, ALU.mult))
            dve.tensor_tensor(sv, sv, wrs, ALU.mult).then_inc(var2, 1)
            dve.wait_ge(rs2, 1)
            link(dve.tensor_tensor(tmp, g2, wrs, ALU.mult))
            link(dve.tensor_tensor(A2, tmp, rstd2, ALU.mult))
            link(dve.tensor_tensor(tmp, mean2, A2, ALU.mult))
            link(dve.tensor_tensor(B2, b2, tmp, ALU.subtract))

        @block.scalar
        def _(act):
            link = chain(act, asteps)
            act.preload_act_table_set("natural_log_exp_and_others")
            act.sem_inc(evac_free, 2)
            act.wait_ge(w_loaded, 16)
            act.activation(sg[:, :], cw[:, :], ACT.Sign).then_inc(w_sign, 1)
            act.wait_ge(var1, 1)
            link(act.activation(lnv1, vari1, ACT.Ln, bias=env.eps[:, 1:2], scale=1.0))
            act.activation(rstd1, lnv1, ACT.Exp, scale=-0.5).then_inc(rs1, 1)
            act.wait_ge(steps, 7)
            link(act.activation(wln, wss, ACT.Ln, scale=1.0 / (GROUP_IN * TAPS - 1)))
            act.activation(wrs, wln, ACT.Exp, scale=-0.5).then_inc(rs1, 1)
            act.wait_ge(coef1, 1)
            act.wait_ge(border, 2)

            def sign(n, q):
                act.wait_ge(evac_free, n + 1)
                act.activation(padded[q][:, 1:1 + SIDE, 1:1 + SIDE],
                               image(Y, n).rearrange("p (h w) -> p h w", w=SIDE), ACT.Sign, bias=B1, scale=A1)\
                   .then_inc(sign_ready, 1)

            def evacuate(n, q):
                act.wait_ge(conv_ready, n + 1)
                act.activation(image(CONV, n), env.psum[2 + q][:, :], ACT.Copy).then_inc(evac_free, 1)

            sign(0, 0)
            with by_two(act, 0, IMAGES - 2) as n:
                for q in range(2):
                    sign(n + q + 1, 1 - q)
                    evacuate(n + q, q)
            sign(IMAGES - 1, 1)
            evacuate(IMAGES - 2, 0)
            evacuate(IMAGES - 1, 1)
            act.wait_ge(var2, 1)
            link(act.activation(lnv2, sv, ACT.Ln, bias=env.eps[:, 1:2], scale=1.0))
            act.activation(rstd2, lnv2, ACT.Exp, scale=-0.5).then_inc(rs2, 1)

        @block.tensor
        def _(pe):
            pe.wait_ge(w_spread, TAPS)
            for k in range(TAPS):
                mm = pe.matmul(env.psum[k // 8][:, (k % 8) * P:(k % 8 + 1) * P], spread[:, k, :], env.idb[:, :],
                               start=True, stop=True)
                if k in (7, TAPS - 1):
                    mm.then_inc(w_turned, 1)
            pe.wait_ge(w_ready, 2)
            with by_two(pe, 0, IMAGES) as n:
                for q in range(2):
                    pe.wait_ge(sign_ready, n + q + 1)
                    pe.wait_ge(evac_free, n + q + 1)
                    for h in range(2):
                        for k in range(TAPS):
                            dy, dx = divmod(k, 3)
                            mm = pe.matmul(env.psum[2 + q][:, h * HALF:(h + 1) * HALF], taps[:, k, :],
                                           padded[q][:, h * 16 + dy:h * 16 + dy + 16, dx:dx + SIDE],
                                           start=(k == 0), stop=(k == TAPS - 1))
                    mm.then_inc(conv_ready, 1)


def phase_tokens0(nc, env, a):
    X, Y, CONV, par = env.X, env.Y, env.CONV, env.par
    with ExitStack() as ctx:
        sem = lambda n: ctx.enter_context(nc.semaphore(n))
        sb = lambda n, s, d=F32: ctx.enter_context(nc.sbuf_tensor(n, s, d))
        wr_loaded, wr_turned, wr_ready, coef = sem("t0_wr_loaded"), sem("t0_wr_turned"), sem("t0_wr_ready"), sem("t0_coef")
        sum_ready, act_ready, half_ready, x_ready = sem("t0_sum_ready"), sem("t0_act_ready"), sem("t0_half_ready"), sem("t0_x_ready")
        rows_free, kept_free, copied_free, stats_free = (sem(f"t0_{x}_free") for x in ("rows", "kept", "copied", "stats"))
        negs = sb("t0_negs", [P, 2])
        negB2, negalpha = negs[:, 0:1], negs[:, 1:2]
        wr, wc = sb("t0_wr", [P, E0]), sb("t0_wc", [P, E0])
        u = [sb(f"t0_u{k}", [P, HALF]) for k in range(FLIGHT)]
        neg = [sb(f"t0_neg{k}", [P, HALF]) for k in range(FLIGHT)]
        bank = lambda i: env.psum[i // 2][:, i % 2 * HALF:(i % 2 + 1) * HALF]
        rows, logits = [bank(k) for k in range(FLIGHT)], [bank(FLIGHT + k) for k in range(FLIGHT)]
        A2, B2, alpha = par[:, 7:8], par[:, 8:9], par[:, 4:5]
        units, per = TOKENS // HALF, HALF // P
        half = lambda buf, n: buf[:, bass.ds(n * HALF, HALF)]
        block = ctx.enter_context(nc.Block())

        def each(engine, body):
            for k in range(FLIGHT):
                body(k, k, 3)
            with engine.Fori(1, units // FLIGHT - 1) as i:
                for k in range(FLIGHT):
                    body(i * FLIGHT + k, k, 3)
            for k in range(FLIGHT):
                body(units - FLIGHT + k, k, FLIGHT - 1 - k)

        @block.sync
        def _(sp):
            sp.dma_start(wr[:, :], a["w_router"]).then_inc(wr_loaded, 16)

        @block.tensor
        def _(pe):
            pe.wait_ge(wr_loaded, 16)
            pe.matmul(logits[0][:, 0:E0], env.cen[:, :], wr[:, :], start=True, stop=True).then_inc(wr_turned, 1)
            pe.wait_ge(wr_ready, 1)
            pe.sem_inc(rows_free, FLIGHT)

            def turn(n, k, ahead):
                pe.wait_ge(x_ready, n + 1)
                pe.wait_ge(copied_free, n + 1)
                pe.wait_ge(stats_free, n + 1)
                for j in range(per):
                    pe.transpose(rows[k][:, j * P:(j + 1) * P], u[k][:, j * P:(j + 1) * P], env.idf[:, :])
                for j in range(per):
                    mm = pe.matmul(logits[k][:, j * E0:(j + 1) * E0], u[k][:, j * P:(j + 1) * P], wc[:, :], start=True, stop=True)
                mm.then_inc(rows_free, 1)
            each(pe, turn)

        @block.vector
        def _(dve):
            dve.wait_ge(wr_turned, 1)
            dve.tensor_copy(wc[:, :], logits[0][:, 0:E0]).then_inc(wr_ready, 1)
            dve.sem_inc(stats_free, FLIGHT)
            dve.tensor_scalar(negB2, B2, -1.0, None, ALU.mult).then_inc(coef, 1)
            dve.tensor_scalar(negalpha, alpha, -1.0, None, ALU.mult).then_inc(coef, 1)

            def residual(n, k):
                dve.wait_ge(rows_free, n + 1)
                dve.wait_ge(kept_free, n + 1)
                dve.scalar_tensor_tensor(u[k][:, :], half(CONV, n), A2, half(Y, n), ALU.mult, ALU.add).then_inc(sum_ready, 1)

            def add(n, k):
                dve.wait_ge(half_ready, n + 1)
                dve.scalar_tensor_tensor(u[k][:, :], neg[k][:, :], negalpha, u[k][:, :], ALU.mult, ALU.add).then_inc(x_ready, 1)

            def statistics(n, k):
                dve.wait_ge(rows_free, n + FLIGHT + 1)
                dve.tensor_copy(env.logit[:, bass.ds(n * (per * E0), per * E0)], logits[k][:, 0:per * E0])
                dve.wait_ge(copied_free, n + FLIGHT + 1)
                for j in range(per):
                    st = dve.bn_stats(env.rowst[:, bass.ds((n * per + j) * 6, 6)], Y[:, bass.ds(n * HALF + j * P, P)])
                st.then_inc(stats_free, 1)

            def unit(n, k, ahead):
                if ahead >= 3:
                    residual(n + 3, (k + 3) % FLIGHT)
                if ahead >= 1:
                    add(n + 1, (k + 1) % FLIGHT)
                if not isinstance(n, int) or n > 0:
                    statistics(n - 1, (k - 1) % FLIGHT)

            for k in range(3):
                residual(k, k)
            add(0, 0)
            each(dve, unit)
            statistics(units - 1, FLIGHT - 1)
            dve.wait_ge(stats_free, units + FLIGHT)

        @block.gpsimd
        def _(pool):
            def add_x(n, k, ahead):
                pool.wait_ge(act_ready, n * 2 + 2)
                pool.tensor_tensor(u[k][:, :], half(X, n), u[k][:, :], ALU.add).then_inc(half_ready, 1)
            each(pool, add_x)

        @block.scalar
        def _(act):
            act.preload_act_table_set("natural_log_exp_and_others")
            act.sem_inc(copied_free, FLIGHT)
            act.sem_inc(kept_free, FLIGHT)
            act.wait_ge(coef, 2)

            def prelu(n, k):
                act.wait_ge(sum_ready, n + 1)
                act.activation(neg[k][:, :], u[k][:, :], ACT.Relu, bias=negB2, scale=-1.0).then_inc(act_ready, 1)
                act.activation(u[k][:, :], u[k][:, :], ACT.Relu, bias=B2, scale=1.0).then_inc(act_ready, 1)

            def keep(n, k):
                act.wait_ge(x_ready, n + 1)
                act.activation(half(X, n), u[k][:, :], ACT.Copy).then_inc(kept_free, 1)

            def copy(n, k):
                act.wait_ge(rows_free, n + FLIGHT + 1)
                act.activation(half(Y, n), rows[k][:, :], ACT.Copy).then_inc(copied_free, 1)

            def unit(n, k, ahead):
                if not isinstance(n, int) or n > 0:
                    copy(n - 1, (k - 1) % FLIGHT)
                if ahead >= 3:
                    prelu(n + 3, (k + 3) % FLIGHT)
                if ahead >= 1:
                    keep(n + 1, (k + 1) % FLIGHT)

            for k in range(3):
                prelu(k, k)
            keep(0, 0)
            each(act, unit)
            copy(units - 1, FLIGHT - 1)


def phase_route0(nc, env):
    with ExitStack() as ctx:
        sem = lambda n: ctx.enter_context(nc.semaphore(n))
        sb = lambda n, s, d=F32: ctx.enter_context(nc.sbuf_tensor(n, s, d))
        steps, var_ready, rstd_ready, logs = sem("r0_steps"), sem("r0_var_ready"), sem("r0_rstd_ready"), sem("r0_logs")
        gap_ready, exp_ready, hot_ready = sem("r0_gap_ready"), sem("r0_exp_ready"), sem("r0_hot_ready")
        total_ready, total_copied, prefix_ready = sem("r0_total_ready"), sem("r0_total_copied"), sem("r0_prefix_ready")
        small = {k: sb(f"r0_{k}", [P, TILES]) for k in
                 ("mean2", "dm", "m2", "var", "ln", "top1", "top2", "rev1", "rev2", "gap", "ex", "g1", "g2", "swap", "hi", "lo", "pid", "slot")}
        v = {k: x[:, :] for k, x in small.items()}
        wide = [sb(f"r0_wide{k}", [P, TILES, E0]) for k in range(3)]
        hot = sb("r0_hot", [P, PAIRS, TILES], BF16)
        total, where = (env.weights[:, k * 2 * PAIRS * TILES:(k + 1) * 2 * PAIRS * TILES].bitcast(F32) for k in range(2))
        pc = {k: sb(f"r0_p{k}", [P, PAIRS]) for k in ("cum", "count", "tiles", "cumt", "adj")}
        pi = sb("r0_pi", [P, PAIRS], I32)
        st = env.rowst[:, :].rearrange("p (t s) -> p t s", s=6)
        over_e = lambda x: x.unsqueeze(2).broadcast_to([P, TILES, E0])
        rev = env.rev.unsqueeze(1).broadcast_to([P, TILES, E0])
        chunks = PAIRS * TILES // HALF
        bank = lambda c: env.psum[c // 2][:, (c % 2) * HALF:(c % 2 + 1) * HALF]
        block = ctx.enter_context(nc.Block())

        @block.scalar
        def _(act):
            act.preload_act_table_set("natural_log_exp_and_others")
            act.wait_ge(var_ready, 1)
            act.activation(v["ln"], v["var"], ACT.Ln, bias=env.eps[:, 1:2], scale=1.0 / C).then_inc(logs, 1)
            act.wait_ge(logs, 1)
            act.activation(env.rstd[:, :], v["ln"], ACT.Exp, scale=-0.5).then_inc(rstd_ready, 1)
            act.wait_ge(gap_ready, 1)
            act.activation(v["ex"], v["gap"], ACT.Exp).then_inc(exp_ready, 1)
            for c in range(chunks):
                act.wait_ge(total_ready, c + 1)
                act.activation(total[:, c * HALF:(c + 1) * HALF], bank(c), ACT.Copy).then_inc(total_copied, 1)

        @block.tensor
        def _(pe):
            pe.wait_ge(hot_ready, 1)
            cols = hot[:, :, :].rearrange("p a t -> p (a t)")
            for c in range(chunks):
                pe.matmul(bank(c), env.ones16[:, :], cols[:, c * HALF:(c + 1) * HALF], start=True, stop=True)\
                  .then_inc(total_ready, 1)
            for c in range(chunks):
                pe.wait_ge(total_copied, c + 1)
                pe.matmul(bank(c), env.ltri[:, :], cols[:, c * HALF:(c + 1) * HALF], start=True, stop=True)\
                  .then_inc(prefix_ready, 1)

        @block.vector
        def _(dve):
            link = chain(dve, steps)
            link(dve.tensor_tensor(v["dm"], st[:, :, 1], st[:, :, 4], ALU.subtract))
            link(dve.tensor_tensor(v["m2"], st[:, :, 2], st[:, :, 5], ALU.add))
            link(dve.tensor_tensor(v["dm"], v["dm"], v["dm"], ALU.mult))
            dve.scalar_tensor_tensor(v["var"], v["dm"], C / 4.0, v["m2"], ALU.mult, ALU.add).then_inc(var_ready, 1)
            link(dve.tensor_tensor(v["mean2"], st[:, :, 1], st[:, :, 4], ALU.add))
            dve.wait_ge(rstd_ready, 1)
            link(dve.scalar_tensor_tensor(env.shift[:, :], v["mean2"], -0.5, env.rstd[:, :], ALU.mult, ALU.mult))
            l, hit, l2 = (w[:, :, :] for w in wide)
            link(dve.tensor_tensor(l, env.logit[:, :].rearrange("p (t e) -> p t e", e=E0), over_e(env.rstd[:, :]), ALU.mult))
            link(dve.tensor_reduce(v["top1"], l, AX.X, ALU.max))
            link(dve.tensor_tensor(hit, l, over_e(v["top1"]), ALU.is_equal))
            link(dve.tensor_tensor(hit, hit, rev, ALU.mult))
            link(dve.tensor_reduce(v["rev1"], hit, AX.X, ALU.max))
            link(dve.tensor_tensor(hit, hit, over_e(v["rev1"]), ALU.is_equal))
            link(dve.scalar_tensor_tensor(l2.rearrange("p t e -> p (t e)"), hit.rearrange("p t e -> p (t e)"), -1e30,
                                          l.rearrange("p t e -> p (t e)"), ALU.mult, ALU.add))
            link(dve.tensor_reduce(v["top2"], l2, AX.X, ALU.max))
            link(dve.tensor_tensor(hit, l2, over_e(v["top2"]), ALU.is_equal))
            link(dve.tensor_tensor(hit, hit, rev, ALU.mult))
            link(dve.tensor_reduce(v["rev2"], hit, AX.X, ALU.max))
            dve.tensor_tensor(v["gap"], v["top2"], v["top1"], ALU.subtract).then_inc(gap_ready, 1)
            link(dve.tensor_tensor(v["lo"], v["rev1"], v["rev2"], ALU.max))
            link(dve.tensor_tensor(v["hi"], v["rev1"], v["rev2"], ALU.min))
            link(dve.tensor_scalar(v["pid"], v["lo"], -1.0, float(E0), ALU.mult, ALU.add))
            link(dve.scalar_tensor_tensor(v["pid"], v["lo"], float(E0 - 1), v["pid"], ALU.add, ALU.mult))
            link(dve.tensor_tensor(v["hi"], v["lo"], v["hi"], ALU.subtract))
            link(dve.scalar_tensor_tensor(v["pid"], v["pid"], 0.5, v["hi"], ALU.mult, ALU.add))
            link(dve.tensor_scalar(v["pid"], v["pid"], -1.0, None, ALU.add))
            dve.tensor_tensor(hot[:, :, :], v["pid"].unsqueeze(1).broadcast_to([P, PAIRS, TILES]),
                              env.pair_no.unsqueeze(2).broadcast_to([P, PAIRS, TILES]), ALU.is_equal).then_inc(hot_ready, 1)
            dve.wait_ge(exp_ready, 1)
            link(dve.tensor_scalar(v["g1"], v["ex"], 1.0, None, ALU.add))
            link(dve.reciprocal(v["g1"], v["g1"]))
            link(dve.tensor_tensor(v["g2"], v["ex"], v["g1"], ALU.mult))
            link(dve.tensor_tensor(v["swap"], v["rev1"], v["rev2"], ALU.is_gt))
            link(dve.tensor_tensor(v["lo"], v["g1"], v["g2"], ALU.subtract))
            link(dve.tensor_tensor(v["swap"], v["swap"], v["lo"], ALU.mult))
            link(dve.tensor_tensor(v["lo"], v["g2"], v["swap"], ALU.add))
            link(dve.tensor_tensor(v["hi"], v["g1"], v["swap"], ALU.subtract))
            gates = env.gates[:, :].rearrange("p (t g) -> p t g", g=2)
            link(dve.tensor_scalar(gates[:, :, 0], v["lo"], 1.0 / WSCALE ** 2, None, ALU.mult))
            link(dve.tensor_scalar(gates[:, :, 1], v["hi"], 1.0 / WSCALE ** 2, None, ALU.mult))
            dve.wait_ge(total_copied, chunks)
            link(dve.tensor_tensor_scan(where[:, :], total[:, :], env.eps[:, 2:3].broadcast_to([P, PAIRS * TILES]), 0.0, ALU.add, ALU.add))
            cum, count, tiles, cumt, adj = (pc[k][:, :] for k in ("cum", "count", "tiles", "cumt", "adj"))
            link(dve.tensor_copy(cum, where[:, :].rearrange("p (a t) -> p a t", t=TILES)[:, :, TILES - 1]))
            link(dve.tensor_tensor(where[:, :], where[:, :], total[:, :], ALU.subtract))
            link(dve.tensor_copy(count[:, 0:1], cum[:, 0:1]))
            link(dve.tensor_tensor(count[:, 1:PAIRS], cum[:, 1:PAIRS], cum[:, 0:PAIRS - 1], ALU.subtract))
            link(dve.tensor_scalar(tiles, count, float(SLOT - 1), float(SLOT), ALU.add, ALU.max))
            link(dve.tensor_copy(pi[:, :], tiles))
            link(dve.tensor_scalar(pi[:, :], pi[:, :], SLOT.bit_length() - 1, None, ALU.arith_shift_right))
            link(dve.tensor_copy(tiles, pi[:, :]))
            link(dve.tensor_tensor_scan(cumt, tiles, env.eps[:, 2:3].broadcast_to([P, PAIRS]), 0.0, ALU.add, ALU.add))
            link(dve.memset(env.starts[:, 0:1], 0))
            link(dve.tensor_copy(env.starts[:, 1:PAIRS + 1], cumt[0:1, :]))
            link(dve.tensor_scalar(env.finals[:, :], cumt[0:1, :], -1.0, None, ALU.add))
            link(dve.tensor_scalar(env.starts[:, PAIRS + 1:PAIRS + 2], cumt[0:1, PAIRS - 1:PAIRS], -1.0, float(MAX_TILES + 1),
                                   ALU.mult, ALU.add))
            link(dve.tensor_tensor(adj, cumt, tiles, ALU.subtract))
            link(dve.scalar_tensor_tensor(adj, adj, float(SLOT), cum, ALU.mult, ALU.subtract))
            link(dve.tensor_tensor(adj, adj, count, ALU.add))
            grid = lambda x: x.rearrange("p (a t) -> p a t", t=TILES)
            link(dve.tensor_tensor(grid(where[:, :]), grid(where[:, :]), adj.unsqueeze(2).broadcast_to([P, PAIRS, TILES]), ALU.add))
            for c in range(chunks):
                dve.wait_ge(prefix_ready, c + 1)
                part = slice(c * HALF, (c + 1) * HALF)
                link(dve.tensor_tensor(where[:, part], bank(c), where[:, part], ALU.add))
            link(dve.tensor_tensor(where[:, :], where[:, :], hot[:, :, :].rearrange("p a t -> p (a t)"), ALU.mult))
            link(dve.tensor_reduce(v["slot"], where[:, :].rearrange("p (a t) -> p t a", t=TILES), AX.X, ALU.add))
            link(dve.tensor_copy(env.slot[:, :], v["slot"]))


def phase_dispatch(nc, env, a):
    Y, W = env.Y, env.weights
    half2 = lambda e, part: W[:, e * WCOLS:e * WCOLS + 4 * H0].rearrange("p (w s n) -> p w s n", w=2, s=2)[:, :, part, :]
    with ExitStack() as ctx:
        sem = lambda n: ctx.enter_context(nc.semaphore(n))
        sb = lambda n, s, d=F32: ctx.enter_context(nc.sbuf_tensor(n, s, d))
        depth = 4
        rows = [sb(f"d0_rows{k}", [P, ROW]) for k in range(depth)]
        index = [sb(f"d0_index{k}", [P, 1], U32) for k in range(depth)]
        ready = sem("d0_ready")
        sent = [sem(f"d0_sent{k}") for k in range(depth)]
        loaded, biases = [sem(f"w0_loaded{q}") for q in range(2)], sem("w0_biases")
        high, low, steps = sem("w0_high"), sem("w0_low"), sem("w0_steps")
        raw = [sb(f"w0_raw{q}", [P, 2 * H0]) for q in range(2)]
        b1, b2, rest = sb("w0_b1", [P, E0 * KM]), sb("w0_b2", [P, E0 * C]), sb("w0_rest", [P, E0 * C])
        parts = [sb(f"w0_part{k}", [P, E0 * C], BF16) for k in range(3)]
        block = ctx.enter_context(nc.Block())

        @block.sync
        def _(sp):
            sp.dma_start(b1[:, :], a["b1"]).then_inc(biases, 16)
            sp.dma_start(b2[:, :], a["b2"].broadcast_to([P, E0 * C])).then_inc(biases, 16)
            for e in range(E0):
                if e >= 2:
                    sp.wait_ge(low, e - 1)
                sp.dma_start(raw[e % 2][:, :], a["w_moe0"][e, :, :]).then_inc(loaded[e % 2], 16)

        @block.scalar
        def _(act):
            act.preload_act_table_set("natural_log_exp_and_others")
            for e in range(E0):
                act.wait_ge(loaded[e % 2], 16 * (e // 2 + 1))
                act.activation(half2(e, 0), raw[e % 2][:, :].rearrange("p (w n) -> p w n", w=2), ACT.Copy, scale=WSCALE)\
                   .then_inc(high, 1)

        @block.vector
        def _(dve):
            link = chain(dve, steps)

            def fill(i, k):
                dve.tensor_scalar(rows[k][:, 0:C], Y[:, bass.ds(i * P, P)], env.rstd[:, bass.ds(i, 1)],
                                  env.shift[:, bass.ds(i, 1)], ALU.mult, ALU.add).then_inc(ready, 1)
                dve.tensor_copy(rows[k][:, C:ROW], env.gates[:, bass.ds(i * 2, 2)]).then_inc(ready, 1)
                dve.tensor_copy(index[k][:, :], env.slot[:, bass.ds(i, 1)]).then_inc(ready, 1)

            def fills(first, last):
                with dve.Fori(first, last) as j:
                    for k in range(depth):
                        dve.wait_ge(sent[k], j * 16)
                        fill(j * depth + k, k)

            for k in range(depth):
                fill(k, k)
            dve.wait_ge(biases, 32)
            link(dve.tensor_scalar(b2[:, :], b2[:, :], WSCALE ** 2, None, ALU.mult))
            link(dve.tensor_copy(parts[0][:, :], b2[:, :]))
            fills(1, 2)
            link(dve.tensor_tensor(rest[:, :], b2[:, :], parts[0][:, :], ALU.subtract))
            link(dve.tensor_copy(parts[1][:, :], rest[:, :]))
            fills(2, 3)
            link(dve.tensor_tensor(rest[:, :], rest[:, :], parts[1][:, :], ALU.subtract))
            link(dve.tensor_copy(parts[2][:, :], rest[:, :]))
            fills(3, 4)
            biasrow = W[:, :].rearrange("p (e n) -> p e n", n=WCOLS)[:, :, 4 * H0:4 * H0 + C].bitcast(BF16)
            link(dve.memset(biasrow, 0.0))
            for k in range(3):
                link(dve.tensor_copy(biasrow[32 * k:32 * k + 1, :, :],
                                     parts[k][32 * k:32 * k + 1, :].rearrange("p (e n) -> p e n", e=E0)))
            fills(4, 5)
            for e in range(E0):
                at = e * WCOLS + 4 * H0 + C
                link(dve.tensor_scalar(W[:, at:at + 2 * KM].bitcast(F32), b1[:, e * KM:(e + 1) * KM], WSCALE, None, ALU.mult))
            for e in range(E0):
                fills(5 + e * 3, 8 + e * 3)
                dve.wait_ge(high, e + 1)
                for w in range(2):
                    at = e * WCOLS + w * 2 * H0
                    ins = dve.scalar_tensor_tensor(W[:, at + H0:at + 2 * H0], raw[e % 2][:, w * H0:(w + 1) * H0], WSCALE,
                                                   W[:, at:at + H0], ALU.mult, ALU.subtract)
                ins.then_inc(low, 1)
            fills(5 + E0 * 3, TILES // depth)
            dve.wait_ge(low, E0)

        @block.gpsimd
        def _(pool):
            pool.wait_ge(env.cleared, CLEARS * 16)
            with pool.Fori(0, TILES // depth) as j:
                for k in range(depth):
                    i = j * depth + k
                    wait_apart(pool, ready, i * 3 + 3, env.passed["pool"])
                    pool.indirect_dma_start(env.xg, bass.IndirectOffsetOnAxis(ap=index[k][:, :], axis=0), rows[k][:, :], None)\
                        .then_inc(sent[k], 16)
            for k in range(depth):
                pool.wait_ge(sent[k], TILES // depth * 16)


def phase_experts0(nc, env, a):
    with ExitStack() as ctx:
        sem = lambda n: ctx.enter_context(nc.semaphore(n))
        sb = lambda n, s, d=F32: ctx.enter_context(nc.sbuf_tensor(n, s, d))
        staged = [sem(f"m0_staged{q}") for q in range(2)]
        rows_loaded, turned, x_split = sem("m0_rows_loaded"), sem("m0_turned"), sem("m0_x_split")
        x_high, h_ready, relu_ready, h_split = sem("m0_x_high"), sem("m0_h_ready"), sem("m0_relu_ready"), sem("m0_h_split")
        filled = sem("m0_filled")
        hh_ready, result_free = sem("m0_hh_ready"), sem("m0_result_free")
        lo_ready, hi_ready, part_ready, out_ready = (sem(f"m0_{x}") for x in ("lo_ready", "hi_ready", "part_ready", "out_ready"))
        x_taken = sem("m0_x_taken")
        gates_ready, stored, table_loaded, next_gates = sem("m0_gates_ready"), sem("m0_stored"), sem("m0_table_loaded"), sem("m0_next_gates")
        stage = [[sb(f"m0_stage{q}{e}", [P, WCOLS], F16) for e in range(2)] for q in range(2)]
        table = sb("m0_table", [1, 2 * PAIRS + 2], I32)
        rows = sb("m0_rows", [P, SUB, ROW])
        x = sb("m0_x", [P, 2, SLOT], F16)
        coming_x = sb("m0_coming_x", [P, 2, SLOT], F16)
        xh, xl = x[:, 0, :], x[:, 1, :]
        hf = [sb(f"m0_hf{e}", [P, KM, SLOT]) for e in range(2)]
        hh = [sb(f"m0_hh{e}", [P, KM, SLOT], F16) for e in range(2)]
        hl = [sb(f"m0_hl{e}", [P, KM, SLOT], F16) for e in range(2)]
        gates, coming = sb("m0_gates", [P, SUB, 2]), sb("m0_coming", [P, SUB, 2])
        part, result = sb("m0_part", [P, SUB, C]), sb("m0_result", [P, SUB, C])
        hidden, turn = env.psum[0:2], env.psum[2][:, 0:SLOT]
        y = [env.psum[3][:, e * HALF:e * HALF + SUB * C].rearrange("p (s c) -> p s c", s=SUB) for e in range(2)]
        block = ctx.enter_context(nc.Block())

        def pairs(engine):
            with engine.Fori(0, PAIRS // 2) as half:
                for q in range(2):
                    p = half * 2 + q
                    first = engine.value_load(env.starts[0:1, bass.ds(p, 1)], min_val=0, max_val=MAX_TILES - 1)
                    last = engine.value_load(env.finals[0:1, bass.ds(p, 1)], min_val=0, max_val=MAX_TILES - 1)
                    yield half, q, p, first, last

        @block.sync
        def _(sp):
            sp.dma_start(table[:, :], a["k_pairs"]).then_inc(table_loaded, 16)
            sp.wait_ge(table_loaded, 16)

            def load(i):
                sp.dma_start(rows[:, :, :], env.xg[bass.ds(i * SLOT, SLOT), :].rearrange("(s p) c -> p s c", p=P))\
                  .then_inc(rows_loaded, 16)

            def stage_pair(p, q):
                for e in range(2):
                    expert = sp.value_load(table[0:1, bass.ds(p * 2 + e, 1)], min_val=0, max_val=E0 - 1)
                    sp.dma_start(stage[q][e][:, :].bitcast(U32),
                                 env.weights[:, :].bitcast(U32)[:, bass.ds(expert * (WCOLS // 2), WCOLS // 2)]).then_inc(staged[q], 16)

            load(0)
            stage_pair(0, 0)
            sp.wait_ge(x_split, 2)
            load(1)
            for half, q, p, first, last in pairs(sp):
                sp.wait_ge(x_split, first + 3)
                load(first + 2)
                sp.wait_ge(hi_ready, first + 1)
                stage_pair(p + 1, 1 - q)
                with maybe_loop(sp, first + 1, last + 1) as i:
                    sp.wait_ge(x_split, i + 3)
                    load(i + 2)
            total = sp.value_load(env.starts[0:1, PAIRS:PAIRS + 1], min_val=PAIRS, max_val=MAX_TILES)
            wait_apart(sp, rows_loaded, total * 16 + 32, env.passed["sp"])
            sp.wait_ge(staged[0], 16 * (PAIRS + 2))

        @block.gpsimd
        def _(pool):
            pool.sem_inc(result_free, 1)
            total = pool.value_load(env.starts[0:1, PAIRS:PAIRS + 1], min_val=PAIRS, max_val=MAX_TILES)
            with pool.Fori(total, MAX_TILES + 1) as i:
                pool.dma_start(env.yg[bass.ds(i * SLOT, SLOT), :].rearrange("(s p) c -> p s c", p=P),
                               env.zero[:, 0:C].unsqueeze(1).broadcast_to([P, SUB, C])).then_inc(filled, 16)
            spare = pool.value_load(env.starts[0:1, PAIRS + 1:PAIRS + 2], min_val=1, max_val=MAX_TILES + 1 - PAIRS)
            wait_apart(pool, filled, spare * 16, env.passed["pool"])
            with pool.Fori(0, total) as i:
                pool.wait_ge(out_ready, i + 2)
                pool.dma_start(env.yg[bass.ds(i * SLOT, SLOT), :].rearrange("(s p) c -> p s c", p=P), result[:, :, :])\
                    .then_inc(stored, 16)
                pool.wait_ge(stored, i * 16 + 16)
                pool.sem_inc(result_free, 1)

        @block.tensor
        def _(pe):
            def transpose(i):
                pe.wait_ge(rows_loaded, i * 16 + 16)
                pe.wait_ge(x_split, i + 1)
                for s in range(SUB):
                    mm = pe.transpose(turn[:, s * P:(s + 1) * P], rows[:, s, 0:C], env.idf[:, :])
                mm.then_inc(turned, 1)

            def up(w, e):
                for m in range(KM):
                    out = hidden[e][:, m * SLOT:(m + 1) * SLOT]
                    high, low = w[:, m * P:(m + 1) * P], w[:, H0 + m * P:H0 + (m + 1) * P]
                    pe.matmul(out, high, xh, start=True, stop=False)
                    pe.matmul(out, high, xl, start=False, stop=False)
                    mm = pe.matmul(out, low, xh, start=False, stop=True)
                    if m % 2:
                        mm.then_inc(h_ready, 1)

            def down(w, e):
                for s in range(SUB):
                    cols = slice(s * P, (s + 1) * P)
                    for k in range(KM):
                        high, low = w[:, 2 * H0 + k * P:2 * H0 + (k + 1) * P], w[:, 3 * H0 + k * P:3 * H0 + (k + 1) * P]
                        pe.matmul(y[e][:, s, :], hh[e][:, k, cols], high, start=(k == 0), stop=False)
                        pe.matmul(y[e][:, s, :], hh[e][:, k, cols], low, start=False, stop=False)
                        pe.matmul(y[e][:, s, :], hl[e][:, k, cols], high, start=False, stop=False)
                    mm = pe.matmul(y[e][:, s, :], env.ones16[:, :], w[:, 4 * H0:4 * H0 + C].bitcast(BF16), start=False, stop=True)
                mm.then_inc((lo_ready, hi_ready)[e], 1)

            def tile(i, w, following, weights_here=None):
                up(w[1], 1)
                pe.wait_ge(h_split, i * 4 + 6)
                pe.wait_ge(part_ready, i + 1)
                down(w[0], 0)
                if weights_here is not None:
                    pe.wait_ge(*weights_here)
                pe.wait_ge(x_taken, i + 2)
                up(following[0], 0)
                pe.wait_ge(h_split, i * 4 + 8)
                pe.wait_ge(out_ready, i + 1)
                down(w[1], 1)
                transpose(i + 2)

            pe.sem_inc(hi_ready, 1)
            transpose(0)
            pe.wait_ge(x_taken, 1)
            transpose(1)
            pe.wait_ge(staged[0], 32)
            up(stage[0][0], 0)
            for half, q, p, first, last in pairs(pe):
                with maybe_loop(pe, first, last) as i:
                    tile(i, stage[q], stage[q])
                tile(last, stage[q], stage[1 - q], (staged[1 - q], half * 32 + 32 + 32 * q))

        @block.scalar
        def _(act):
            act.preload_act_table_set("natural_log_exp_and_others")

            def high_x(i):
                act.wait_ge(turned, i + 1)
                if not isinstance(i, int) or i > 0:
                    act.wait_ge(x_taken, i)
                act.activation(coming_x[:, 0, :], turn, ACT.Copy).then_inc(x_high, 1)

            def relu(i, w, e, b):
                bias = w[e][:, 4 * H0 + C:4 * H0 + C + 2 * KM].bitcast(F32)
                act.wait_ge(h_ready, i * 4 + (2 * e + b + 1))
                act.wait_ge(h_split, i * 4 + (2 * e + b + 1))
                for m in (2 * b, 2 * b + 1):
                    ins = act.activation(hf[e][:, m, :], hidden[e][:, m * SLOT:(m + 1) * SLOT], ACT.Relu,
                                         bias=bias[:, m:m + 1], scale=1.0)
                ins.then_inc(relu_ready, 1)

            def tile(i, w, following, weights_here=None):
                relu(i, w, 1, 0)
                relu(i, w, 1, 1)
                act.wait_ge(lo_ready, i + 1)
                act.wait_ge(gates_ready, i + 1)
                act.wait_ge(out_ready, i + 1)
                for s in range(SUB):
                    ins = act.activation(part[:, s, :], y[0][:, s, :], ACT.Copy, scale=gates[:, s, 0:1])
                ins.then_inc(part_ready, 1)
                if weights_here is not None:
                    act.wait_ge(*weights_here)
                relu(i + 1, following, 0, 0)
                relu(i + 1, following, 0, 1)
                high_x(i + 2)

            act.sem_inc(part_ready, 1)
            high_x(0)
            act.wait_ge(staged[0], 32)
            high_x(1)
            relu(0, stage[0], 0, 0)
            relu(0, stage[0], 0, 1)
            for half, q, p, first, last in pairs(act):
                with maybe_loop(act, first, last) as i:
                    tile(i, stage[q], stage[q])
                tile(last, stage[q], stage[1 - q], (staged[1 - q], half * 32 + 32 + 32 * q))

        @block.vector
        def _(dve):
            dve.sem_inc(x_split, 1)
            dve.sem_inc(h_split, 4)
            dve.sem_inc(out_ready, 1)

            def low_x(i):
                dve.wait_ge(x_high, i + 1)
                dve.tensor_copy(coming[:, :, :], rows[:, :, C:ROW]).then_inc(next_gates, 1)
                dve.tensor_tensor(coming_x[:, 1, :], turn, coming_x[:, 0, :], ALU.subtract).then_inc(x_split, 1)

            def take_x(i):
                dve.wait_ge(x_split, i + 2)
                dve.tensor_copy(x[:, :, :], coming_x[:, :, :]).then_inc(x_taken, 1)

            def take_gates(i):
                dve.wait_ge(next_gates, i + 1)
                dve.tensor_copy(gates[:, :, :], coming[:, :, :]).then_inc(gates_ready, 1)

            def split(i, e, b):
                m = slice(2 * b, 2 * b + 2)
                dve.wait_ge(relu_ready, i * 4 + (2 * e + b + 1))
                dve.tensor_copy(hh[e][:, m, :], hf[e][:, m, :]).then_inc(hh_ready, 1)
                dve.wait_ge(hh_ready, i * 4 + (2 * e + b + 1))
                dve.tensor_tensor(hl[e][:, m, :], hf[e][:, m, :], hh[e][:, m, :], ALU.subtract).then_inc(h_split, 1)

            dve.wait_ge(turned, 1)
            low_x(0)
            take_x(0)
            take_gates(0)
            dve.wait_ge(gates_ready, 1)
            low_x(1)
            split(0, 0, 0)
            split(0, 0, 1)
            total = dve.value_load(env.starts[0:1, PAIRS:PAIRS + 1], min_val=PAIRS, max_val=MAX_TILES)
            with dve.Fori(0, total) as i:
                dve.wait_ge(h_ready, i * 4 + 4)
                take_x(i + 1)
                split(i, 1, 0)
                split(i, 1, 1)
                split(i + 1, 0, 0)
                split(i + 1, 0, 1)
                dve.wait_ge(hi_ready, i + 2)
                dve.wait_ge(part_ready, i + 2)
                dve.wait_ge(result_free, i + 1)
                for s in range(SUB):
                    ins = dve.scalar_tensor_tensor(result[:, s, :], y[1][:, s, :], gates[:, s, 1:2], part[:, s, :], ALU.mult, ALU.add)
                ins.then_inc(out_ready, 1)
                dve.wait_ge(out_ready, i + 2)
                take_gates(i + 1)
                dve.wait_ge(gates_ready, i + 2)
                low_x(i + 2)


def phase_involution(nc, env, a, out):
    X, par = env.X, env.par
    with ExitStack() as ctx:
        names = ("gathered turned x_added cent_ready sq_ready var_ready ln_ready rstd_ready y_ready t_ready v_ready "
                 "padded_ready e2_ready group_ready gvar_ready gln_ready grstd_ready coef_ready relu_ready split_ready "
                 "tap_ready product_ready summed pool_summed done steps w_loaded w_ready border sent index_ready").split()
        S = {n: ctx.enter_context(nc.semaphore(f"iv_{n}")) for n in names}
        sb = lambda n, s, d=F32: ctx.enter_context(nc.sbuf_tensor(f"iv_{n}", s, d))
        wv, w1, gavg = sb("wv", [P, C]), sb("w1", [P, P]), sb("gavg", [P, P])
        w2, w2b, gn = sb("w2", [P, TAPS, P]), sb("w2b", [P, TAPS]), sb("gn", [P, 2])
        wa, wb = sb("wa", [P, TAPS, P], F16), sb("wb", [P, TAPS, P], F16)
        got = [sb(f"got{k}", [P, C]) for k in range(TPI)]
        index = [sb(f"index{k}", [P, 1], U32) for k in range(TPI)]
        sq, rs, y, tf = (sb(n, [P, PIX]) for n in ("sq", "rs", "y", "tf"))
        ct = [sb(f"ct{q}", [P, PIX], F16) for q in range(2)]
        xv = [sb(f"xv{q}", [P, PAD, PAD]) for q in range(2)]
        pool_part = [sb(f"pool_part{k}", [P, SIDE, SIDE]) for k in range(POOL_TAPS)]
        own_part = [sb(f"own_part{k}", [P, SIDE, SIDE]) for k in range(2)]
        own_sum, pool_sum = sb("own_sum", [P, SIDE, SIDE]), sb("pool_sum", [P, SIDE, SIDE])
        t = sb("t", [P, 32])
        D = env.psum
        cent = [D[1][:, HALF:PIX], D[1][:, 0:HALF]]
        halves = [slice(0, HALF), slice(HALF, PIX)]
        grid = lambda ap: ap.rearrange("p (h w) -> p h w", w=SIDE)
        loads = [(wv[:, :], a["w_v"]), (w1[:, :], a["w1_d4"]), (gavg[:, :], a["k_groups"]), (w2[:, :, :], a["w2_taps"]),
                 (w2b[:, :], a["b2_taps"]), (gn[:, :], a["gn"])]
        block = ctx.enter_context(nc.Block())

        def images(engine, body):
            with by_two(engine, 0, IMAGES - 4) as n:
                for q in range(2):
                    body(n + q, q, 3)
            for n in range(IMAGES - 4, IMAGES):
                body(n, n % 2, min(3, IMAGES - 1 - n))

        def half(buf, n, h):
            return buf[:, bass.ds(n * PIX + h * HALF, HALF)]

        @block.sync
        def _(sp):
            for dst, src in loads:
                sp.dma_start(dst, src).then_inc(S["w_loaded"], 16)

            with sp.Fori(FIRST_IMAGES, IMAGES) as n:
                sp.wait_ge(S["done"], n + 3)
                sp.dma_start(out[:, bass.ds(n * PIX, PIX)], image(X, n)).then_inc(S["sent"], 16)
            sp.wait_ge(S["sent"], 16 * (IMAGES - FIRST_IMAGES))

        @block.gpsimd
        def _(pool):
            pool.sem_inc(S["pool_summed"], POOL_TAPS)

            def gather(n, first=False):
                if not first:
                    pool.wait_ge(S["turned"], n * 2)
                for k in range(TPI):
                    pool.tensor_copy(index[k][:, :], env.slot[:, bass.ds(n * TPI + k, 1)]).then_inc(S["index_ready"], 1)
                for k in range(TPI):
                    wait_apart(pool, S["index_ready"], n * TPI + k + 1, env.passed["pool"])
                    pool.indirect_dma_start(got[k][:, :], None, env.yg, bass.IndirectOffsetOnAxis(ap=index[k][:, :], axis=0))\
                        .then_inc(S["gathered"], 16)

            def body(n, q, ahead):
                for k in range(POOL_TAPS):
                    pool.wait_ge(S["product_ready"], n * TAPS + k + 3)
                    if k == 0:
                        pool.wait_ge(S["done"], n + 2)
                    else:
                        pool.wait_ge(S["pool_summed"], n * POOL_TAPS + k + POOL_TAPS)
                    pool.tensor_tensor(pool_sum[:, :, :], grid(image(X, n)) if k == 0 else pool_sum[:, :, :],
                                       pool_part[k][:, :, :], ALU.add).then_inc(S["pool_summed"], 1)
                if ahead >= 3:
                    gather(n + 3)

            gather(0, first=True)
            gather(1)
            gather(2)
            images(pool, body)

        @block.tensor
        def _(pe):
            def turn(n, h):
                if h == 0:
                    pe.wait_ge(S["gathered"], n * 16 * TPI + 16 * TPI)
                    if not isinstance(n, int) or n > 0:
                        pe.wait_ge(S["gvar_ready"], n)
                else:
                    pe.wait_ge(S["x_added"], n * 2 + 1)
                for k in range(TPI // 2):
                    mm = pe.transpose(D[1][:, k * P:(k + 1) * P], got[h * TPI // 2 + k][:, :], env.idf[:, :])
                mm.then_inc(S["turned"], 1)

            def center(n, h):
                pe.wait_ge(S["x_added"], n * 2 + h + 1)
                if h == 0 and (not isinstance(n, int) or n > 0):
                    pe.wait_ge(S["padded_ready"], n * 2)
                pe.matmul(cent[h], env.cen[:, :], half(X, n, h), start=True, stop=True).then_inc(S["cent_ready"], 1)

            def variance(n, h):
                pe.wait_ge(S["sq_ready"], n * 2 + h + 1)
                pe.wait_ge(S["relu_ready"], n + 1)
                pe.matmul(D[0][:, halves[h]], env.avg[:, :], sq[:, halves[h]], start=True, stop=True).then_inc(S["var_ready"], 1)

            def kernels(n):
                pe.wait_ge(S["y_ready"], n * 2 + 4)
                for h in halves:
                    mm = pe.matmul(D[0][:, h], w1[:, :], y[:, h], start=True, stop=True)
                mm.then_inc(S["t_ready"], 1)

            def values(n):
                for h in halves:
                    pe.matmul(D[1][:, h], wv[:, :], y[:, h], start=True, stop=True).then_inc(S["v_ready"], 1)

            def group(n):
                pe.wait_ge(S["e2_ready"], n + 1)
                pe.wait_ge(S["padded_ready"], n * 2 + 1)
                pe.matmul(D[1][:, 0:2], gavg[:, :], t[:, 0:2], start=True, stop=True).then_inc(S["group_ready"], 1)

            def tap(n, q, k):
                if k == 0:
                    pe.wait_ge(S["split_ready"], n + 2)
                pe.wait_ge(S["product_ready"], n * TAPS + k + 1)
                dst = D[2 + (q * TAPS + k) % 2]
                for h in halves:
                    pe.matmul(dst[:, h], wa[:, k, :], ct[q][:, h], start=True, stop=False)
                    mm = pe.matmul(dst[:, h], wb[:, k, :], ct[q][:, h], start=False, stop=True)
                mm.then_inc(S["tap_ready"], 1)

            def body(n, q, ahead):
                tap(n, q, 0)
                if ahead >= 1:
                    kernels(n + 1)
                tap(n, q, 1)
                if ahead >= 1:
                    values(n + 1)
                tap(n, q, 2)
                tap(n, q, 3)
                if ahead >= 1:
                    group(n + 1)
                tap(n, q, 4)
                if ahead >= 2:
                    turn(n + 2, 0)
                tap(n, q, 5)
                if ahead >= 2:
                    center(n + 2, 0)
                    turn(n + 2, 1)
                tap(n, q, 6)
                if ahead >= 2:
                    variance(n + 2, 0)
                    center(n + 2, 1)
                tap(n, q, 7)
                if ahead >= 2:
                    variance(n + 2, 1)
                tap(n, q, 8)

            def norm(n):
                turn(n, 0)
                center(n, 0)
                turn(n, 1)
                variance(n, 0)
                center(n, 1)
                variance(n, 1)

            pe.wait_ge(S["w_loaded"], 16 * len(loads))
            pe.wait_ge(S["w_ready"], 3)
            norm(0)
            kernels(0)
            values(0)
            group(0)
            norm(1)
            images(pe, body)

        @block.scalar
        def _(act):
            act.preload_act_table_set("natural_log_exp_and_others")
            act.sem_inc(S["relu_ready"], 1)

            def square(n, h):
                act.wait_ge(S["cent_ready"], n * 2 + h + 1)
                act.activation(sq[:, halves[h]], cent[h], ACT.Square).then_inc(S["sq_ready"], 1)

            def rstd(n, h):
                j, part = n * 2 + h + 1, rs[:, halves[h]]
                act.wait_ge(S["var_ready"], j)
                act.wait_ge(S["y_ready"], j)
                act.activation(part, D[0][:, halves[h]], ACT.Ln, bias=env.eps[:, 0:1], scale=1.0).then_inc(S["ln_ready"], 1)
                act.wait_ge(S["ln_ready"], j)
                act.activation(part, part, ACT.Exp, scale=-0.5).then_inc(S["rstd_ready"], 1)

            def values(n, q):
                act.wait_ge(S["done"], n + 1)
                for h in range(2):
                    act.wait_ge(S["v_ready"], n * 2 + h + 1)
                    act.activation(xv[q][:, 1 + 16 * h:17 + 16 * h, 1:1 + SIDE], D[1][:, halves[h]].rearrange("p (h w) -> p h w", w=SIDE),
                                   ACT.Copy).then_inc(S["padded_ready"], 1)

            def relu(n, q):
                act.wait_ge(S["gvar_ready"], n + 1)
                act.activation(t[:, 8:9], t[:, 7:8], ACT.Ln, bias=env.eps[:, 1:2], scale=-1.0).then_inc(S["gln_ready"], 1)
                act.wait_ge(S["gln_ready"], n + 1)
                act.activation(t[:, 9:10], t[:, 8:9], ACT.Exp, scale=-0.5).then_inc(S["grstd_ready"], 1)
                act.wait_ge(S["coef_ready"], n + 2)
                act.wait_ge(S["split_ready"], n + 1)
                act.activation(tf[:, :], D[0][:, :], ACT.Relu, bias=t[:, 11:12], scale=t[:, 10:11])
                act.activation(ct[q][:, :], D[0][:, :], ACT.Relu, bias=t[:, 11:12], scale=t[:, 10:11]).then_inc(S["relu_ready"], 1)

            def norm(n):
                for h in range(2):
                    square(n, h)
                    rstd(n, h)

            def body(n, q, ahead):
                if ahead >= 1:
                    values(n + 1, 1 - q)
                    relu(n + 1, 1 - q)
                if ahead >= 2:
                    norm(n + 2)

            act.wait_ge(S["border"], 2)
            norm(0)
            values(0, 0)
            relu(0, 0)
            norm(1)
            images(act, body)

        @block.vector
        def _(dve):
            dve.sem_inc(S["coef_ready"], 1)
            dve.sem_inc(S["y_ready"], 2)
            dve.sem_inc(S["split_ready"], 1)
            dve.sem_inc(S["done"], 2)
            dve.sem_inc(S["product_ready"], 2)
            for q in range(2):
                dve.memset(xv[q][:, :, :], 0.0).then_inc(S["border"], 1)
            dve.wait_ge(S["w_loaded"], 16 * len(loads))
            dve.tensor_copy(wa[:, :, :], w2[:, :, :]).then_inc(S["w_ready"], 1)
            dve.memset(wb[64:128, :, :], 0.0).then_inc(S["w_ready"], 1)
            dve.wait_ge(S["w_ready"], 1)
            dve.tensor_tensor(wb[0:64, :, :], w2[0:64, :, :], wa[0:64, :, :], ALU.subtract).then_inc(S["w_ready"], 1)

            def step(n, k, ins, apart=False):
                ins.then_inc(S["steps"], 1)
                if apart:
                    wait_apart(dve, S["steps"], n * STEPS_PER_IMAGE + k + 1, env.passed["dve"])
                else:
                    dve.wait_ge(S["steps"], n * STEPS_PER_IMAGE + k + 1)

            def add_x(n, h):
                dve.wait_ge(S["turned"], n * 2 + h + 1)
                dve.tensor_tensor(half(X, n, h), D[1][:, 0:HALF], half(X, n, h), ALU.add).then_inc(S["x_added"], 1)

            def norm(n, h):
                dve.wait_ge(S["rstd_ready"], n * 2 + h + 1)
                if not isinstance(n, int) or n > 0:
                    dve.wait_ge(S["v_ready"], n * 2)
                dve.tensor_tensor(y[:, halves[h]], cent[h], rs[:, halves[h]], ALU.mult).then_inc(S["y_ready"], 1)

            def statistics(n):
                dve.wait_ge(S["t_ready"], n + 1)
                step(n, 0, dve.bn_stats(t[:, 12:18], D[0][:, halves[0]]))
                step(n, 1, dve.bn_stats(t[:, 18:24], D[0][:, halves[1]]), apart=True)
                step(n, 2, dve.bn_aggr(t[:, 0:2], t[:, 12:24].rearrange("p (n s) -> p n s", s=6)))
                dve.scalar_tensor_tensor(t[:, 1:2], t[:, 0:1], t[:, 0:1], t[:, 1:2], ALU.mult, ALU.add).then_inc(S["e2_ready"], 1)

            def group_variance(n):
                dve.wait_ge(S["group_ready"], n + 1)
                step(n, 3, dve.tensor_scalar(t[:, 4:6], D[1][:, 0:2], -1.0, None, ALU.mult))
                dve.scalar_tensor_tensor(t[:, 7:8], t[:, 4:5], t[:, 4:5], t[:, 5:6], ALU.mult, ALU.add).then_inc(S["gvar_ready"], 1)

            def coefficients(n):
                dve.wait_ge(S["grstd_ready"], n + 1)
                step(n, 4, dve.tensor_tensor(t[:, 10:11], gn[:, 0:1], t[:, 9:10], ALU.mult))
                dve.scalar_tensor_tensor(t[:, 11:12], t[:, 4:5], t[:, 10:11], gn[:, 1:2], ALU.mult, ALU.add).then_inc(S["coef_ready"], 1)

            def split(n, q):
                dve.wait_ge(S["relu_ready"], n + 2)
                dve.tensor_tensor(ct[q][64:128, :], tf[64:128, :], ct[q][64:128, :], ALU.subtract).then_inc(S["split_ready"], 1)

            def product(n, q, k):
                dve.wait_ge(S["tap_ready"], n * TAPS + k + 1)
                if k == 0:
                    dve.wait_ge(S["padded_ready"], n * 2 + 2)
                dy, dx = divmod(k, 3)
                if k < POOL_TAPS:
                    dve.wait_ge(S["pool_summed"], n * POOL_TAPS + k + 1)
                    dst = pool_part[k]
                else:
                    dst = own_sum if k == POOL_TAPS else own_part[k % 2]
                    if k == POOL_TAPS:
                        dve.wait_ge(S["done"], n + 2)
                    if k > POOL_TAPS + 2:
                        dve.wait_ge(S["summed"], n * OWN_ADDS + k - POOL_TAPS - 2)
                dve.scalar_tensor_tensor(dst[:, :, :], grid(D[2 + (q * TAPS + k) % 2][:, :]), w2b[:, k:k + 1],
                                         xv[q][:, dy:dy + SIDE, dx:dx + SIDE], ALU.add, ALU.mult).then_inc(S["product_ready"], 1)

            def add(n, k):
                dve.wait_ge(S["product_ready"], n * TAPS + k + 3)
                if k > POOL_TAPS + 1:
                    dve.wait_ge(S["summed"], n * OWN_ADDS + k - POOL_TAPS - 1)
                dve.tensor_tensor(own_sum[:, :, :], own_sum[:, :, :], own_part[k % 2][:, :, :], ALU.add).then_inc(S["summed"], 1)

            def finish(n):
                dve.wait_ge(S["summed"], n * OWN_ADDS + OWN_ADDS)
                dve.wait_ge(S["pool_summed"], n * POOL_TAPS + 2 * POOL_TAPS)
                dve.tensor_tensor(grid(image(X, n)), own_sum[:, :, :], pool_sum[:, :, :], ALU.add).then_inc(S["done"], 1)

            def body(n, q, ahead):
                for k in range(TAPS):
                    product(n, q, k)
                    if k == 1 and ahead >= 1:
                        statistics(n + 1)
                    if k == 2 and ahead >= 1:
                        group_variance(n + 1)
                    if k == 3 and ahead >= 1:
                        coefficients(n + 1)
                    if k in (4, 5) and ahead >= 2:
                        add_x(n + 2, k - 4)
                    if k == 6 and ahead >= 1:
                        split(n + 1, 1 - q)
                    if k in (6, 7) and ahead >= 2:
                        norm(n + 2, k - 6)
                    if k > POOL_TAPS + 1:
                        add(n, k - 1)
                add(n, TAPS - 1)
                finish(n)

            for h in range(2):
                add_x(0, h)
            for h in range(2):
                norm(0, h)
            statistics(0)
            group_variance(0)
            coefficients(0)
            split(0, 0)
            for h in range(2):
                add_x(1, h)
            for h in range(2):
                norm(1, h)
            images(dve, body)


def phase_gate1(nc, env, a):
    X, XN, WT = env.X, env.XN, env.WT
    with ExitStack() as ctx:
        names = ("gate_loaded w_loaded cleared cent_ready sq_ready var_ready ln_ready rs_ready xn_ready kept logits_ready ex_ready "
                 "sel_ready rank_ready ranked wp_ready w_turned wt_ready steps ends_ready decided").split()
        S = {n: ctx.enter_context(nc.semaphore(f"g1_{n}")) for n in names}
        sb = lambda n, s, d=F32: ctx.enter_context(nc.sbuf_tensor(f"g1_{n}", s, d))
        gate_w, gate_b, before_mask = sb("gate_w", [P, E1]), sb("gate_b", [P, E1]), sb("before_mask", [P, G1, G1])
        sq, rs, xs = ([sb(f"{n}{q}", [P, BLOCK]) for q in range(2)] for n in ("sq", "rs", "xs"))
        scores = [sb(f"scores{q}", [P, BT, G1, 2]) for q in range(2)]
        biased, masked = (sb(n, [P, BT, G1, 2]) for n in ("biased", "masked"))
        group = sb("group", [P, BT, G1])
        above, tie = sb("above", [P, BT, G1, G1]), sb("tie", [P, BT, G1, G1])
        place, selected, keep = sb("place", [P, BT, G1]), sb("selected", [P, BT, G1]), sb("keep", [P, BT, G1])
        sel = sb("sel", [P, BT, G1], BF16)
        total, taken, room, need = sb("total", [P, BT]), sb("taken", [P, G1]), sb("room", [P, G1]), sb("need", [P, G1])
        wg, rest = sb("wg", [P, BT, E1]), sb("rest", [P, BT, E1])
        parts = sb("parts", [P, BT, P], BF16)
        least, ends = sb("least", [1, 2]), sb("ends", [1, 3], I32)
        cent, var, logits = ([env.psum[i][:, q * HALF:(q + 1) * HALF] for q in range(2)] for i in range(3))
        rank = env.psum[3][:, 0:BT * G1].rearrange("p (s g) -> p s g", g=G1)
        tot, turned = env.psum[3][:, BT * G1:BT * G1 + G1], env.psum[3][:, HALF:PIX]
        loads = [(gate_w[:, :], a["gate_w"]), (gate_b[:, :], a["gate_b"].broadcast_to([P, E1])),
                 (before_mask[:, :, :], a["k_before"].broadcast_to([P, G1, G1]))]
        weight_loads = [(env.spread32[:, :, :], a["k_spread"]), (env.w1[:, :, :], a["w1_moe1"]), (env.w3[:, :, :], a["w3_moe1"]),
                 (env.w2[:, :, :], a["w2_moe1"])]
        block = ctx.enter_context(nc.Block())

        def cols(buf, n):
            return buf[:, bass.ds(n * BLOCK, BLOCK)]

        def blocks(engine, body, last=None):
            with engine.Fori(0, 2) as r:
                engine.wait_ge(S["ends_ready"], r + 1)
                end = engine.value_load(ends[0:1, bass.ds(r, 1)], min_val=FIRST_BLOCKS // 2, max_val=BLOCKS // 2)
                with maybe_loop(engine, r * (FIRST_BLOCKS // 2), end) as i:
                    for q in range(2):
                        body(i * 2 + q, q)
                if last is not None:
                    last(r)

        @block.sync
        def _(sp):
            for dst, src in loads:
                sp.dma_start(dst, src).then_inc(S["gate_loaded"], 16)
            for dst, src in weight_loads:
                sp.dma_start(dst, src).then_inc(S["w_loaded"], 16)
            sp.wait_ge(S["w_loaded"], 16 * len(weight_loads))

        @block.tensor
        def _(pe):
            def center(n, q):
                pe.wait_ge(S["xn_ready"], n + 1)
                pe.matmul(cent[q], env.cen[:, :], cols(X, n % BLOCKS), start=True, stop=True).then_inc(S["cent_ready"], 1)

            def variance(n, q):
                pe.wait_ge(S["sq_ready"], n + 1)
                pe.matmul(var[q], env.avg[:, :], sq[q][:, :], start=True, stop=True).then_inc(S["var_ready"], 1)

            def gate(n, q):
                pe.wait_ge(S["xn_ready"], n + 3)
                pe.wait_ge(S["ex_ready"], n + 1)
                for s in range(BT):
                    mm = pe.matmul(logits[q][:, s * E1:(s + 1) * E1], xs[q][:, s * P:(s + 1) * P], gate_w[:, :],
                                   start=True, stop=True)
                mm.then_inc(S["logits_ready"], 1)

            def ranks(n):
                pe.wait_ge(S["sel_ready"], n + 1)
                pe.wait_ge(S["ranked"], n + 2)
                for s in range(BT):
                    for before in range(s):
                        pe.matmul(rank[:, s, :], env.ones16[:, :], sel[:, before, :], start=(before == 0), stop=False)
                    pe.matmul(rank[:, s, :], env.ltri[:, :], sel[:, s, :], start=(s == 0), stop=True)
                for s in range(BT):
                    mm = pe.matmul(tot, env.ones16[:, :], sel[:, s, :], start=(s == 0), stop=(s == BT - 1))
                mm.then_inc(S["rank_ready"], 1)

            def turn_weights(n):
                pe.wait_ge(S["wp_ready"], n + 1)
                pe.wait_ge(S["wt_ready"], n + 1)
                for s in range(BT):
                    mm = pe.matmul(turned[:, s * P:(s + 1) * P], parts[:, s, :], env.idb[:, :], start=True, stop=True)
                mm.then_inc(S["w_turned"], 1)

            def body(n, q):
                center(n + 1, 1 - q)
                variance(n + 1, 1 - q)
                ranks(n)
                gate(n + 1, 1 - q)
                turn_weights(n)

            center(0, 0)
            variance(0, 0)
            pe.wait_ge(S["gate_loaded"], 16 * len(loads))
            gate(0, 0)
            blocks(pe, body)

        @block.scalar
        def _(act):
            act.preload_act_table_set("natural_log_exp_and_others")
            act.sem_inc(S["wt_ready"], 1)
            act.sem_inc(S["kept"], 2)
            act.sem_inc(S["ex_ready"], 2)

            def norm(n, q):
                act.wait_ge(S["cent_ready"], n + 1)
                act.activation(sq[q][:, :], cent[q], ACT.Square).then_inc(S["sq_ready"], 1)
                act.wait_ge(S["var_ready"], n + 1)
                act.activation(rs[q][:, :], var[q], ACT.Ln, bias=env.eps[:, 1:2], scale=1.0).then_inc(S["ln_ready"], 1)
                act.wait_ge(S["ln_ready"], n + 1)
                act.activation(rs[q][:, :], rs[q][:, :], ACT.Exp, scale=-0.5).then_inc(S["rs_ready"], 1)
                act.wait_ge(S["xn_ready"], n + 3)
                act.activation(cols(XN, n % BLOCKS), xs[q][:, :], ACT.Copy).then_inc(S["kept"], 1)
                act.wait_ge(S["logits_ready"], n + 1)
                act.wait_ge(S["ranked"], n + 1)
                act.activation(scores[q][:, :, :, :].rearrange("p s g e -> p (s g e)"), logits[q][:, 0:BT * E1], ACT.Exp, scale=-1.0)\
                    .then_inc(S["ex_ready"], 1)

            def take_weights(n):
                act.wait_ge(S["w_turned"], n + 1)
                act.activation(cols(WT, n), turned, ACT.Copy).then_inc(S["wt_ready"], 1)

            def body(n, q):
                norm(n + 1, 1 - q)
                take_weights(n)

            norm(0, 0)
            blocks(act, body)

        @block.vector
        def _(dve):
            dve.sem_inc(S["ranked"], 2)
            dve.sem_inc(S["xn_ready"], 2)
            wide = lambda ap: ap.unsqueeze(3).broadcast_to([P, BT, G1, 2])

            def step(n, k, ins):
                ins.then_inc(S["steps"], 1)
                dve.wait_ge(S["steps"], n * STEPS1 + k + 1)

            def norm(n, q):
                dve.wait_ge(S["rs_ready"], n + 1)
                dve.wait_ge(S["kept"], n + 1)
                dve.tensor_tensor(xs[q][:, :], cent[q], rs[q][:, :], ALU.mult).then_inc(S["xn_ready"], 1)

            def select(n, q):
                dve.wait_ge(S["ex_ready"], n + 3)
                f = lambda t: t[:, :, :, :].rearrange("p s g e -> p (s g e)")
                step(n, 0, dve.tensor_scalar(f(scores[q]), f(scores[q]), 1.0, None, ALU.add))
                step(n, 1, dve.reciprocal(f(scores[q]), f(scores[q])))
                step(n, 2, dve.tensor_tensor(biased[:, :, :, :].rearrange("p s g e -> p s (g e)"),
                                             scores[q][:, :, :, :].rearrange("p s g e -> p s (g e)"),
                                             gate_b[:, :].unsqueeze(1).broadcast_to([P, BT, E1]), ALU.add))
                step(n, 3, dve.tensor_tensor(group[:, :, :], biased[:, :, :, 0], biased[:, :, :, 1], ALU.add))
                own = group[:, :, :].unsqueeze(3).broadcast_to([P, BT, G1, G1])
                other = group[:, :, :].unsqueeze(2).broadcast_to([P, BT, G1, G1])
                step(n, 4, dve.tensor_tensor(above[:, :, :, :], other, own, ALU.is_gt))
                step(n, 5, dve.tensor_tensor(tie[:, :, :, :], other, own, ALU.is_equal))
                flat = lambda t: t[:, :, :, :].rearrange("p s g h -> p s (g h)")
                step(n, 6, dve.tensor_tensor(flat(tie), flat(tie), before_mask[:, :, :].rearrange("p g h -> p (g h)")
                                             .unsqueeze(1).broadcast_to([P, BT, G1 * G1]), ALU.mult))
                step(n, 7, dve.tensor_tensor(flat(above), flat(above), flat(tie), ALU.add))
                step(n, 8, dve.tensor_reduce(place[:, :, :], above[:, :, :, :], AX.X, ALU.add))
                step(n, 9, dve.tensor_scalar(selected[:, :, :], place[:, :, :], float(TOP_G), None, ALU.is_lt))
                dve.tensor_copy(sel[:, :, :], selected[:, :, :]).then_inc(S["sel_ready"], 1)

            def weigh(n, q):
                step(n, 10, dve.tensor_tensor(masked[:, :, :, :], scores[q][:, :, :, :], wide(selected[:, :, :]), ALU.mult))
                step(n, 11, dve.tensor_reduce(total[:, :], masked[:, :, :, :].rearrange("p s g e -> p s (g e)"), AX.X, ALU.add))
                step(n, 12, dve.reciprocal(total[:, :], total[:, :]))
                step(n, 13, dve.tensor_scalar(total[:, :], total[:, :], SCALE1, None, ALU.mult))
                dve.wait_ge(S["rank_ready"], n + 1)
                step(n, 14, dve.tensor_tensor(keep[:, :, :], rank, taken[:, :].unsqueeze(1).broadcast_to([P, BT, G1]), ALU.add))
                step(n, 15, dve.tensor_tensor(taken[:, :], taken[:, :], tot, ALU.add))
                step(n, 16, dve.tensor_scalar(room[:, :], taken[:, :], float(CAP), None, ALU.is_lt))
                step(n, 17, dve.tensor_tensor(need[:, :], need[:, :], room[:, :], ALU.add))
                step(n, 18, dve.tensor_scalar(keep[:, :, :], keep[:, :, :], float(CAP), None, ALU.is_lt))
                step(n, 19, dve.tensor_tensor(keep[:, :, :], keep[:, :, :], total[:, :].unsqueeze(2).broadcast_to([P, BT, G1]), ALU.mult))
                pair = lambda t: t[:, :, :].rearrange("p s (g e) -> p s g e", e=2)
                step(n, 20, dve.tensor_tensor(pair(wg), masked[:, :, :, :], wide(keep[:, :, :]), ALU.mult))
                if not isinstance(n, int):
                    dve.wait_ge(S["w_turned"], n)
                step(n, 21, dve.tensor_copy(parts[:, :, 0:E1], wg[:, :, :]))
                step(n, 22, dve.tensor_tensor(rest[:, :, :], wg[:, :, :], parts[:, :, 0:E1], ALU.subtract))
                step(n, 23, dve.tensor_copy(parts[:, :, 32:32 + E1], rest[:, :, :]))
                step(n, 24, dve.tensor_tensor(rest[:, :, :], rest[:, :, :], parts[:, :, 32:32 + E1], ALU.subtract))
                dve.tensor_copy(parts[:, :, 64:64 + E1], rest[:, :, :]).then_inc(S["wp_ready"], 1)
                dve.sem_inc(S["ranked"], 1)

            def body(n, q):
                select(n, q)
                norm(n + 1, 1 - q)
                weigh(n, q)

            def decide(r):
                link = lambda j, ins: (ins.then_inc(S["decided"], 1), dve.wait_ge(S["decided"], r * 2 + j))
                link(CLEARED1 + 1, dve.tensor_reduce(least[0:1, 0:1], taken[0:1, :], AX.X, ALU.min))
                link(CLEARED1 + 2, dve.tensor_scalar(least[0:1, 1:2], least[0:1, 0:1], float(CAP), float((BLOCKS - FIRST_BLOCKS) // 2),
                                                     ALU.is_lt, ALU.mult))
                dve.tensor_scalar(ends[0:1, bass.ds(r + 1, 1)], least[0:1, 1:2], float(FIRST_BLOCKS // 2), None, ALU.add)\
                    .then_inc(S["ends_ready"], 1)

            dve.memset(taken[:, :], 0.0).then_inc(S["decided"], 1)
            dve.memset(need[:, :], 1.0).then_inc(S["decided"], 1)
            dve.memset(parts[:, :, :], 0.0).then_inc(S["decided"], 1)
            dve.wait_ge(S["decided"], CLEARED1)
            norm(0, 0)
            dve.wait_ge(S["gate_loaded"], 16 * len(loads))
            dve.memset(ends[0:1, 0:1], FIRST_BLOCKS // 2).then_inc(S["ends_ready"], 1)
            blocks(dve, body, last=decide)
            dve.wait_ge(S["w_loaded"], 16 * len(weight_loads))
            dve.tensor_copy(env.spread[:, :, :], env.spread32[:, :, :])
            link = chain(dve, S["cleared"])
            link(dve.tensor_scalar(need[:, :], need[:, :], float(BLOCKS), None, ALU.min))
            link(dve.tensor_tensor_scan(room[:, :], need[:, :], env.eps[:, 2:3].broadcast_to([P, G1]), 0.0, ALU.add, ALU.add))
            link(dve.memset(env.served[:, 0:1], 0))
            link(dve.tensor_copy(env.served[:, 1:G1 + 1], room[0:1, :]))
            link(dve.tensor_scalar(env.finals1[:, :], room[0:1, :], -1.0, None, ALU.add))
            link(dve.tensor_copy(env.sends[:, 0:1], ends[0:1, 1:2]))


def phase_experts1(nc, env, a, out):
    X, XN, WT, served = env.X, env.XN, env.WT, env.served
    with ExitStack() as ctx:
        names = "a_ready b_ready wb_ready exp_ready softplus_ready sig_ready u_ready g_ready h_free down_free x_done sent".split()
        S = {n: ctx.enter_context(nc.semaphore(f"e1_{n}")) for n in names}
        sb = lambda n, s, d=F32: ctx.enter_context(nc.sbuf_tensor(f"e1_{n}", s, d))
        sig, u, h = ([sb(f"{n}{q}", [P, UNIT1]) for q in range(2)] for n in ("sig", "u", "h"))
        A, B, spread_w, y = ([env.psum[i][:, q * HALF:q * HALF + UNIT1] for q in range(2)] for i in range(4))
        block = ctx.enter_context(nc.Block())

        def cols(buf, n, q):
            return buf[:, bass.ds(n * BLOCK + q * UNIT1, UNIT1)]

        def load_range(engine, g):
            return (engine.value_load(served[0:1, g:g + 1], min_val=0, max_val=G1 * BLOCKS - 1),
                    engine.value_load(served[0:1, g + 1:g + 2], min_val=1, max_val=G1 * BLOCKS))

        @block.sync
        def _(sp):
            last = sp.value_load(served[0:1, G1:G1 + 1], min_val=G1, max_val=G1 * BLOCKS)
            wait_apart(sp, S["x_done"], last * 2 + 2, env.passed["sp"])
            count = sp.value_load(env.sends[0:1, 0:1], min_val=FIRST_IMAGES, max_val=IMAGES)
            with sp.Fori(0, count) as n:
                sp.dma_start(out[:, bass.ds(n * PIX, PIX)], image(X, n)).then_inc(S["sent"], 16)
            wait_apart(sp, S["sent"], count * 16, env.passed["sp"])

        @block.tensor
        def _(pe):
            def up(j, q, g, n):
                pe.wait_ge(S["h_free"], j + 1)
                pe.matmul(A[q], env.w1[:, g, :], cols(XN, n, q), start=True, stop=True).then_inc(S["a_ready"], 1)
                pe.matmul(B[q], env.w3[:, g, :], cols(XN, n, q), start=True, stop=True).then_inc(S["b_ready"], 1)
                pe.matmul(spread_w[q], env.spread[:, g, :], cols(WT, n, q), start=True, stop=True).then_inc(S["wb_ready"], 1)

            def down(j, q, g):
                pe.wait_ge(S["h_free"], j + 3)
                pe.wait_ge(S["x_done"], j + 1)
                pe.matmul(y[q], env.w2[:, g, :], h[q][:, :], start=True, stop=True).then_inc(S["down_free"], 1)

            def step(i, g, n, following, n_following):
                up(i * 2 + 1, 1, g, n)
                down(i * 2, 0, g)
                up(i * 2 + 2, 0, following, n_following)
                down(i * 2 + 1, 1, g)

            up(0, 0, 0, 0)
            for g in range(G1):
                first, last = load_range(pe, g)
                final = pe.value_load(env.finals1[0:1, g:g + 1], min_val=0, max_val=G1 * BLOCKS - 1)
                with maybe_loop(pe, first, final) as i:
                    step(i, g, (i - first) % BLOCKS, g, (i - first + 1) % BLOCKS)
                step(final, g, (final - first) % BLOCKS, min(g + 1, G1 - 1), 0)

        @block.scalar
        def _(act):
            act.preload_act_table_set("natural_log_exp_and_others")
            last = act.value_load(served[0:1, G1:G1 + 1], min_val=G1, max_val=G1 * BLOCKS)
            with act.Fori(0, last) as i:
                for q in range(2):
                    j, s = i * 2 + q + 1, sig[q]
                    act.wait_ge(S["a_ready"], j)
                    act.activation(s[:, :], A[q], ACT.Exp, scale=-1.0).then_inc(S["exp_ready"], 1)
                    act.wait_ge(S["exp_ready"], j)
                    act.activation(s[:, :], s[:, :], ACT.Ln, bias=env.ones32[:, 0:1], scale=1.0).then_inc(S["softplus_ready"], 1)
                    act.wait_ge(S["softplus_ready"], j)
                    act.activation(s[:, :], s[:, :], ACT.Exp, scale=-1.0).then_inc(S["sig_ready"], 1)

        @block.vector
        def _(dve):
            dve.sem_inc(S["h_free"], 2)
            dve.sem_inc(S["x_done"], 2)
            dve.sem_inc(S["down_free"], 2)

            def hidden(i, q):
                j = i * 2 + q + 1
                dve.wait_ge(S["sig_ready"], j)
                dve.tensor_tensor(u[q][:, :], sig[q][:, :], A[q], ALU.mult).then_inc(S["u_ready"], 1)
                dve.wait_ge(S["u_ready"], j)
                dve.wait_ge(S["b_ready"], j)
                dve.tensor_tensor(u[q][:, :], u[q][:, :], B[q], ALU.mult).then_inc(S["g_ready"], 1)
                dve.wait_ge(S["g_ready"], j)
                dve.wait_ge(S["wb_ready"], j)
                dve.wait_ge(S["down_free"], j)
                dve.tensor_tensor(h[q][:, :], u[q][:, :], spread_w[q], ALU.mult).then_inc(S["h_free"], 1)

            def add(i, q, n):
                dve.wait_ge(S["down_free"], i * 2 + q + 3)
                dve.tensor_tensor(cols(X, n, q), cols(X, n, q), y[q], ALU.add).then_inc(S["x_done"], 1)

            for g in range(G1):
                first, last = load_range(dve, g)
                with dve.Fori(first, last) as i:
                    hidden(i, 0)
                    hidden(i, 1)
                    add(i, 0, (i - first) % BLOCKS)
                    add(i, 1, (i - first) % BLOCKS)
            wait_apart(dve, S["x_done"], last * 2 + 2, env.passed["dve"])


class Env:
    pass


def build(nc, a, out):
    env = Env()
    with ExitStack() as ctx:
        sb = lambda n, s, d=F32: ctx.enter_context(nc.sbuf_tensor(n, s, d))
        env.X = sb("X", [P, TOKENS])
        env.cen, env.avg, env.idf, env.ltri32 = sb("cen", [P, P]), sb("avg", [P, P]), sb("idf", [P, P]), sb("ltri32", [P, P])
        env.ltri, env.ones16, env.idb = sb("ltri", [P, P], BF16), sb("ones16", [P, P], BF16), sb("idb", [P, P], BF16)
        env.ones32 = sb("ones32", [P, 1])
        env.small = sb("small", [P, SMALL])
        env.mask_group = env.small[:, 0:16]
        env.rev = env.small[:, 16:24]
        env.pair_no = env.small[:, 24:24 + PAIRS]
        env.lane = env.small[:, 52:53]
        env.par, env.eps = sb("par", [P, 9]), sb("eps", [P, 3])
        env.slot, env.starts = sb("slot", [P, TILES], I32), sb("starts", [1, PAIRS + 2], I32)
        env.finals = sb("finals", [1, PAIRS], I32)
        env.zero = sb("zero_row", [P, ROW])
        env.passed = {name: ctx.enter_context(nc.semaphore(f"passed_{name}")) for name in ("pool", "pe", "sp", "dve")}
        env.cleared = ctx.enter_context(nc.semaphore("rows_cleared"))
        env.bnst = sb("bnst", [P, IMAGES * 12])
        env.psum = [ctx.enter_context(nc.psum_tensor(f"ps{i}", [P, 2 * HALF], F32)) for i in range(4)]
        xg = nc.dram_tensor("dispatched", (CLEARED, ROW), F32, kind="Internal").ap()
        yg = nc.dram_tensor("expert_out", ((MAX_TILES + 1) * SLOT, C), F32, kind="Internal").ap()
        env.xg, env.yg = xg, yg
        setup_constants(nc, env, a)
        with ExitStack() as layer0:
            sb0 = lambda n, s, d=F32: layer0.enter_context(nc.sbuf_tensor(n, s, d))
            env.weights = sb0("weights", [P, E0 * WCOLS], F16)
            with ExitStack() as first:
                sb1 = lambda n, s, d=F32: first.enter_context(nc.sbuf_tensor(n, s, d))
                env.Y = sb1("Y", [P, TOKENS])
                env.rstd, env.shift, env.gates = sb1("rstd", [P, TILES]), sb1("shift", [P, TILES]), sb1("gates", [P, 2 * TILES])
                env.logit, env.rowst = sb1("logit", [P, TILES * E0]), sb1("rowst", [P, TILES * 6])
                env.CONV = env.weights[:, 0:TOKENS].bitcast(BF16)
                phase_norm0(nc, env, a, xg)
                phase_conv(nc, env, a)
                phase_tokens0(nc, env, a)
                phase_route0(nc, env)
                phase_dispatch(nc, env, a)
            phase_experts0(nc, env, a)
        phase_involution(nc, env, a, out)
        with ExitStack() as third:
            sb3 = lambda n, s, d=F32: third.enter_context(nc.sbuf_tensor(n, s, d))
            env.XN, env.WT = sb3("XN", [P, TOKENS]), sb3("WT", [P, TOKENS], BF16)
            env.w1, env.w3, env.w2, env.spread32 = (sb3(n, [P, G1, P]) for n in ("e1_w1", "e1_w3", "e1_w2", "spread32"))
            env.spread = sb3("spread", [P, G1, P], BF16)
            env.served, env.sends = sb3("served", [1, G1 + 1], I32), sb3("sends", [1, 1], I32)
            env.finals1 = sb3("finals1", [1, G1], I32)
            phase_gate1(nc, env, a)
            phase_experts1(nc, env, a, out)


SMALL = 53


def constants():
    small = np.zeros((P, SMALL), np.float32)
    small[np.arange(P), np.arange(P) // GROUP_IN] = 1.0
    small[:, 16:24] = E0 - np.arange(E0)
    small[:, 24:24 + PAIRS] = np.arange(PAIRS)
    small[:, 52] = np.arange(P)
    return {
        "k_center": np.eye(P, dtype=np.float32) - np.float32(1 / C),
        "k_average": np.full((P, P), 1 / C, np.float32),
        "k_identity": np.eye(P, dtype=np.float32),
        "k_lower": np.triu(np.ones((P, P), np.float32), 1),
        "k_small": small,
        "k_groups": np.where((np.arange(P)[:, None] < 64) & (np.arange(P)[:, None] // G8 == np.arange(P)[None, :] % 64 // G8),
                             np.float32(1 / G8), np.float32(0)),
        "k_before": np.tril(np.ones((G1, G1), np.float32), -1).reshape(1, G1, G1),
        "k_spread": ((np.arange(P) % 32 < E1) & (np.arange(P) < 96))[:, None, None]
                    * (np.arange(P)[:, None, None] % 32 == 2 * np.arange(G1)[None, :, None] + np.arange(P)[None, None, :] // M1)
                    .astype(np.float32),
        "k_pairs": np.array(PAIR_LIST + PAIR_LIST[-1:], np.int32).reshape(1, 2 * PAIRS + 2),
    }


def layout(i):
    i = {k: np.asarray(v) for k, v in i.items()}
    a = dict(constants())
    a["x"] = i["x"].transpose(1, 0, 2, 3).reshape(C, IMAGES, PIX)
    a["chan"] = np.stack([i["L0_conv_bn1_gamma"], i["L0_conv_bn1_beta"], i["L0_conv_bn2_gamma"],
                          i["L0_conv_bn2_beta"], i["L0_conv_prelu_a"]], axis=1)
    a["conv_w"] = i["L0_conv_conv_w"].reshape(C, GROUP_IN * TAPS)
    a["w_router"] = i["L0_ffn_W_router"]
    w1 = i["L0_ffn_W1"]
    w2 = i["L0_ffn_W2"].reshape(E0, KM, P, C).transpose(0, 2, 1, 3).reshape(E0, P, H0)
    a["w_moe0"] = np.concatenate([w1, w2], axis=2)
    a["b1"] = i["L0_ffn_b1"].reshape(E0, KM, P).transpose(2, 0, 1).reshape(P, E0 * KM)
    a["b2"] = i["L0_ffn_b2"].reshape(1, E0 * C)
    d4 = lambda w: w[:, :, np.array(PERMS)].transpose(1, 3, 0, 2).reshape(C, -1)
    a["w_v"] = d4(i["L1_conv_w_v"])
    a["w1_d4"] = np.concatenate([d4(i["L1_conv_w1"])] * 2, axis=1)
    a["gn"] = np.concatenate([np.stack([i["L1_conv_gn_gamma"], i["L1_conv_gn_beta"]], axis=1)] * 2)
    base = np.arange(TAPS).reshape(3, 3)
    source = np.stack([base, np.rot90(base, 1), np.rot90(base, 2), np.rot90(base, 3), np.rot90(base.T, 3),
                       np.rot90(base.T, 2), np.rot90(base.T, 1), base.T]).reshape(G8, TAPS)
    w2 = np.zeros((2, CMID, G8, TAPS, C // G8, G8), np.float32)
    for g in range(G8):
        w2[:, :, g, :, :, g] = i["L1_conv_w2"][source[g]].T[None, :, :, None]
    a["w2_taps"] = w2.reshape(P, TAPS, P)
    a["b2_taps"] = np.tile(i["L1_conv_b2"][source], (C // G8, 1))
    a["w1_moe1"] = i["L1_ffn_w1"].transpose(1, 0, 2).reshape(P, G1, P)
    a["w3_moe1"] = i["L1_ffn_w3"].transpose(1, 0, 2).reshape(P, G1, P)
    a["w2_moe1"] = i["L1_ffn_w2"].reshape(G1, P, C).transpose(1, 0, 2)
    a["gate_w"] = i["L1_ffn_gate_w"].T
    a["gate_b"] = i["L1_ffn_gate_b"].reshape(1, E1)
    return {k: np.ascontiguousarray(v) for k, v in a.items()}


def kernel(**inputs):
    import concourse.bacc as bacc
    from concourse.bass_utils import run_bass_kernel_spmd
    arrays = layout(inputs)
    nc = bacc.Bacc("TRN2", target_bir_lowering=False, num_devices=1)
    a = {name: nc.dram_tensor(name, value.shape, mybir.dt.from_np(value.dtype), kind="ExternalInput").ap()
         for name, value in arrays.items()}
    out = nc.dram_tensor("out", (P, TOKENS), F32, kind="ExternalOutput").ap()
    build(nc, a, out)
    result = run_bass_kernel_spmd(nc, [arrays], core_ids=[0])
    return result.results[0]["out"].reshape(C, IMAGES, SIDE, SIDE).transpose(1, 0, 2, 3)
```
